# Optimizing a Trainium2 kernel written in Bass

```python
import numpy as np
import jax
import jax.numpy as jnp

def _softmax(x, axis=-1):
    return jax.nn.softmax(x, axis=axis)

def _gelu(x):
    return jax.nn.gelu(x, approximate=True)

def _silu(x):
    return jax.nn.silu(x)

def _sigmoid(x):
    return jax.nn.sigmoid(x)

def _layernorm(x, axis=-1, eps=1e-05):
    m = jnp.mean(x, axis=axis, keepdims=True)
    v = jnp.var(x, axis=axis, keepdims=True)
    return (x - m) / jnp.sqrt(v + eps)

def _scatter_add(tgt, idx, src, axis=0):
    return tgt.at[idx].add(src)

def _segment_sum(src, seg, n):
    return jax.ops.segment_sum(src, seg, n)
kernel_name = 'mk_flamingo_gated_d2_seqx_r8_0ed603'

def setup_inputs(seed: int=0):
    np.random.seed(seed)
    _w = jnp.asarray

    def _rec_inputs():
        import jax
        import jax.numpy as jnp
        _rk = jax.random.key(seed)
        x = -0.000125 + 0.9999 * jax.random.normal(jax.random.fold_in(_rk, 1), (32, 64, 128), jnp.float32)
        _lenS = 64 - jax.random.randint(jax.random.fold_in(_rk, 7), (32,), 0, max(1, 64 // 4) + 1, jnp.int32)
        _lenS2 = 64 - jax.random.randint(jax.random.fold_in(_rk, 8), (32,), 0, max(1, 64 // 4) + 1, jnp.int32)
        _ctx_1024P = jax.random.normal(jax.random.fold_in(_rk, 11), (32, 16, 128), jnp.float32)
        _ctx_1024c = jax.random.dirichlet(jax.random.fold_in(_rk, 511), 0.3 * jnp.ones((16,), jnp.float32), (32, 64))
        _ctx_1024t = jnp.einsum('bsk,bkd->bsd', _ctx_1024c, _ctx_1024P)
        _ctx_1024t = _ctx_1024t * jax.lax.rsqrt(jnp.mean(jnp.square(_ctx_1024t)) + 1e-12) * 0.953939
        ctx_1024 = -1.52775e-05 + 0.999936 * (_ctx_1024t + 0.3 * jax.random.normal(jax.random.fold_in(_rk, 611), (32, 64, 128), jnp.float32))
        _validS = jnp.arange(64)[None, :] < _lenS[:, None]
        _validS2 = jnp.arange(64)[None, :] < _lenS2[:, None]
        _causal = jnp.tril(jnp.ones((64, 64), dtype=bool))
        mask_Bx1xS2_ik1 = jnp.where(jnp.broadcast_to(_validS2[:, None, :], (32, 1, 64)), 1, 0).astype(jnp.int32)
        _g = jax.random.normal(jax.random.fold_in(_rk, 9001), (2, 2), jnp.float32)
        _g = jnp.sign(_g) * jnp.maximum(jnp.abs(_g), 1.0) + (_g == 0) * 1.0
        g_xattn = _g[0]
        g_ffn = _g[1]
        return (x, ctx_1024, mask_Bx1xS2_ik1, g_xattn, g_ffn)
    x, ctx_1024, mask_Bx1xS2_ik1, g_xattn, g_ffn = _rec_inputs()

    def _L0_xattn_setup():
        import jax, jax.numpy as jnp
        import numpy as np
        BATCH, NUM, DIMS = (16, 256, 128)
        DROPOUT = 0.1
        DROPOUT_P = DROPOUT / (DIMS * NUM)
        SCALE = 1.0 / float(np.sqrt(BATCH))
        NEG = jnp.float32(-10000000000.0)
        key = jax.random.key(seed)
        kq, kk, kv, km = jax.random.split(key, 4)
        q = jax.random.normal(kq, (BATCH, NUM, DIMS), dtype=jnp.float32)
        k = jax.random.normal(kk, (BATCH, NUM, DIMS), dtype=jnp.float32)
        v = jax.random.normal(kv, (BATCH, NUM, DIMS), dtype=jnp.float32)
        mask = jax.random.randint(km, (BATCH, 1, NUM), 0, 2, dtype=jnp.int32)
        return {'q': q, 'k': k, 'v': v, 'mask': mask}
    _L0_xattn_all = _L0_xattn_setup()
    _L0_xattn_in = {k: v for k, v in _L0_xattn_all.items() if k in ()}
    del _L0_xattn_all

    def _L0_ffn_setup():
        import jax, jax.numpy as jnp
        import numpy as np
        D_MODEL, D_FF, RANK = (128, 512, 32)
        B, S = (4, 512)
        key = jax.random.key(seed)
        ks = jax.random.split(key, 7)
        return {'x': jax.random.normal(ks[0], (B, S, D_MODEL), dtype=jnp.float32), 'U1': jax.random.normal(ks[1], (D_MODEL, RANK), dtype=jnp.float32) * 0.02, 'V1': jax.random.normal(ks[2], (RANK, D_FF), dtype=jnp.float32) * 0.02, 'b1': jnp.zeros((D_FF,), dtype=jnp.float32), 'U2': jax.random.normal(ks[3], (D_FF, RANK), dtype=jnp.float32) * 0.02, 'V2': jax.random.normal(ks[4], (RANK, D_MODEL), dtype=jnp.float32) * 0.02, 'b2': jnp.zeros((D_MODEL,), dtype=jnp.float32)}
    _L0_ffn_all = _L0_ffn_setup()
    _L0_ffn_in = {k: v for k, v in _L0_ffn_all.items() if k in ('U1', 'V1', 'b1', 'U2', 'V2', 'b2')}
    del _L0_ffn_all

    def _L1_xattn_setup():
        import jax, jax.numpy as jnp
        import numpy as np
        E = 128
        H = 16
        D = E // H
        key = jax.random.key(seed)
        ks = jax.random.split(key, 12)
        B, Tq, Tk = (2, 128, 1024)
        s = 0.02
        return {'hidden_states': jax.random.normal(ks[0], (B, Tq, E), jnp.float32), 'key_value_states': jax.random.normal(ks[1], (B, Tk, E), jnp.float32), 'Wq': jax.random.normal(ks[2], (E, E), jnp.float32) * s, 'bq': jnp.zeros((E,), jnp.float32), 'Wk': jax.random.normal(ks[3], (E, E), jnp.float32) * s, 'bk': jnp.zeros((E,), jnp.float32), 'Wv': jax.random.normal(ks[4], (E, E), jnp.float32) * s, 'bv': jnp.zeros((E,), jnp.float32), 'Wo': jax.random.normal(ks[5], (E, E), jnp.float32) * s, 'bo': jnp.zeros((E,), jnp.float32), 'stride': 16}
    _L1_xattn_all = _L1_xattn_setup()
    _L1_xattn_in = {k: v for k, v in _L1_xattn_all.items() if k in ('Wq', 'bq', 'Wk', 'bk', 'Wv', 'bv', 'Wo', 'bo')}
    del _L1_xattn_all

    def _L1_ffn_setup():
        import jax, jax.numpy as jnp
        import numpy as np
        D = 128
        H = 4
        HD = D // H
        E = 8
        FF = 512
        CAP_FACTOR = 1.0

        def _ln(x, g, b, eps=1e-05):
            mu = jnp.mean(x, -1, keepdims=True)
            v = jnp.mean((x - mu) ** 2, -1, keepdims=True)
            return (x - mu) * jax.lax.rsqrt(v + eps) * g + b

        def _mha(x, w, b, ow, ob):
            L, N, _ = x.shape
            qkv = x @ w.T + b
            q, k, v = jnp.split(qkv, 3, axis=-1)
            rh = lambda t: t.reshape(L, N, H, HD).transpose(1, 2, 0, 3)
            q, k, v = (rh(q), rh(k), rh(v))
            scores = jnp.einsum('nhld,nhmd->nhlm', q, k) / np.float32(np.sqrt(HD))
            attn = jax.nn.softmax(scores, axis=-1)
            o = jnp.einsum('nhlm,nhmd->nhld', attn, v).transpose(2, 0, 1, 3).reshape(L, N, D)
            return o @ ow.T + ob

        def _moe(x, wg, w1, b1, w2, b2):
            L, N, _ = x.shape
            S = L * N
            cap = int(CAP_FACTOR * S) // E
            xf = x.reshape(S, D)
            gates = jax.nn.softmax(xf @ wg, axis=-1)
            idx = jnp.argmax(gates, axis=-1)
            mask1 = jax.nn.one_hot(idx, E, dtype=x.dtype)
            loc = jnp.sum((jnp.cumsum(mask1, 0) - 1.0) * mask1, -1).astype(jnp.int32)
            keep = loc < cap
            gate_val = jnp.take_along_axis(gates, idx[:, None], -1)[:, 0]
            slot = jnp.where(keep, idx.astype(jnp.int32) * cap + loc, E * cap)
            disp = jnp.zeros((E * cap, D), x.dtype).at[slot].set(xf, mode='drop')
            disp = disp.reshape(E, cap, D)
            h = jnp.einsum('ecd,edf->ecf', disp, w1) + b1[:, None, :]
            y = (jnp.einsum('ecf,efd->ecd', h, w2) + b2[:, None, :]).reshape(E * cap, D)
            out = jnp.where(keep[:, None], gate_val[:, None] * y[jnp.minimum(slot, E * cap - 1)], 0.0)
            return out.reshape(L, N, D)
        key = jax.random.key(seed)
        ks = jax.random.split(key, 8)
        L, N = (128, 16)
        s = 0.02
        return {'x': jax.random.normal(ks[0], (L, N, D), jnp.float32), 'in_proj_w': jax.random.normal(ks[1], (3 * D, D), jnp.float32) * s, 'in_proj_b': jnp.zeros((3 * D,), jnp.float32), 'out_proj_w': jax.random.normal(ks[2], (D, D), jnp.float32) * s, 'out_proj_b': jnp.zeros((D,), jnp.float32), 'ln1_g': jnp.ones((D,), jnp.float32), 'ln1_b': jnp.zeros((D,), jnp.float32), 'ln2_g': jnp.ones((D,), jnp.float32), 'ln2_b': jnp.zeros((D,), jnp.float32), 'wg': jax.random.normal(ks[3], (D, E), jnp.float32) * s, 'w1': jax.random.normal(ks[4], (E, D, FF), jnp.float32) * s, 'b1': jnp.zeros((E, FF), jnp.float32), 'w2': jax.random.normal(ks[5], (E, FF, D), jnp.float32) * s, 'b2': jnp.zeros((E, D), jnp.float32)}
    _L1_ffn_all = _L1_ffn_setup()
    _L1_ffn_in = {k: v for k, v in _L1_ffn_all.items() if k in ('in_proj_w', 'in_proj_b', 'out_proj_w', 'out_proj_b', 'ln1_g', 'ln1_b', 'ln2_g', 'ln2_b', 'wg', 'w1', 'b1', 'w2', 'b2')}
    del _L1_ffn_all
    return {'x': x, 'ctx_1024': ctx_1024, 'mask_Bx1xS2_ik1': mask_Bx1xS2_ik1, 'g_xattn': g_xattn, 'g_ffn': g_ffn, 'L0_ffn_U1': _L0_ffn_in['U1'], 'L0_ffn_V1': _L0_ffn_in['V1'], 'L0_ffn_b1': _L0_ffn_in['b1'], 'L0_ffn_U2': _L0_ffn_in['U2'], 'L0_ffn_V2': _L0_ffn_in['V2'], 'L0_ffn_b2': _L0_ffn_in['b2'], 'L1_xattn_Wq': _L1_xattn_in['Wq'], 'L1_xattn_bq': _L1_xattn_in['bq'], 'L1_xattn_Wk': _L1_xattn_in['Wk'], 'L1_xattn_bk': _L1_xattn_in['bk'], 'L1_xattn_Wv': _L1_xattn_in['Wv'], 'L1_xattn_bv': _L1_xattn_in['bv'], 'L1_xattn_Wo': _L1_xattn_in['Wo'], 'L1_xattn_bo': _L1_xattn_in['bo'], 'L1_ffn_in_proj_w': _L1_ffn_in['in_proj_w'], 'L1_ffn_in_proj_b': _L1_ffn_in['in_proj_b'], 'L1_ffn_out_proj_w': _L1_ffn_in['out_proj_w'], 'L1_ffn_out_proj_b': _L1_ffn_in['out_proj_b'], 'L1_ffn_ln1_g': _L1_ffn_in['ln1_g'], 'L1_ffn_ln1_b': _L1_ffn_in['ln1_b'], 'L1_ffn_ln2_g': _L1_ffn_in['ln2_g'], 'L1_ffn_ln2_b': _L1_ffn_in['ln2_b'], 'L1_ffn_wg': _L1_ffn_in['wg'], 'L1_ffn_w1': _L1_ffn_in['w1'], 'L1_ffn_b1': _L1_ffn_in['b1'], 'L1_ffn_w2': _L1_ffn_in['w2'], 'L1_ffn_b2': _L1_ffn_in['b2']}

def reference(x, ctx_1024, mask_Bx1xS2_ik1, g_xattn, g_ffn, L0_ffn_U1, L0_ffn_V1, L0_ffn_b1, L0_ffn_U2, L0_ffn_V2, L0_ffn_b2, L1_xattn_Wq, L1_xattn_bq, L1_xattn_Wk, L1_xattn_bk, L1_xattn_Wv, L1_xattn_bv, L1_xattn_Wo, L1_xattn_bo, L1_ffn_in_proj_w, L1_ffn_in_proj_b, L1_ffn_out_proj_w, L1_ffn_out_proj_b, L1_ffn_ln1_g, L1_ffn_ln1_b, L1_ffn_ln2_g, L1_ffn_ln2_b, L1_ffn_wg, L1_ffn_w1, L1_ffn_b1, L1_ffn_w2, L1_ffn_b2):
    import jax
    import jax.numpy as jnp

    def _L0_xattn_ref(q, k, v, mask):
        import jax, jax.numpy as jnp
        import numpy as np
        BATCH, NUM, DIMS = (16, 256, 128)
        DROPOUT = 0.1
        DROPOUT_P = DROPOUT / (DIMS * NUM)
        SCALE = 1.0 / float(np.sqrt(BATCH))
        NEG = jnp.float32(-10000000000.0)
        scores = jnp.einsum('bqd,bkd->bqk', q, k) * SCALE
        scores = jnp.where(mask == 0, NEG, scores)
        probs = jax.nn.softmax(scores, axis=-1)
        probs = probs * (1.0 / (1.0 - DROPOUT_P))
        return jnp.einsum('bqk,bkd->bqd', probs, v)

    def _L0_ffn_ref(x, U1, V1, b1, U2, V2, b2):
        import jax, jax.numpy as jnp
        import numpy as np
        D_MODEL, D_FF, RANK = (128, 512, 32)
        B, S = (4, 512)
        P = jnp.einsum('bsd,dr->bsr', x, U1)
        H = jax.nn.gelu(jnp.einsum('bsr,rf->bsf', P, V1) + b1)
        Q = jnp.einsum('bsf,fr->bsr', H, U2)
        return jnp.einsum('bsr,rd->bsd', Q, V2) + b2

    def _L1_xattn_ref(hidden_states, key_value_states, Wq, bq, Wk, bk, Wv, bv, Wo, bo, stride):
        import jax, jax.numpy as jnp
        import numpy as np
        E = 128
        H = 16
        D = E // H
        B, Tq, _ = hidden_states.shape
        Tk = key_value_states.shape[1]
        scaling = D ** (-0.5)
        Q = (hidden_states @ Wq.T + bq).reshape(B, Tq, H, D).transpose(0, 2, 1, 3)
        K = (key_value_states @ Wk.T + bk).reshape(B, Tk, H, D).transpose(0, 2, 1, 3)
        V = (key_value_states @ Wv.T + bv).reshape(B, Tk, H, D).transpose(0, 2, 1, 3)
        m = Tk // stride
        idx = jnp.arange(H)[:, None] + stride * jnp.arange(m)[None, :]
        gather = idx[None, :, :, None]
        Kg = jnp.take_along_axis(K, gather, axis=2)
        Vg = jnp.take_along_axis(V, gather, axis=2)
        scores = jnp.einsum('bhqd,bhkd->bhqk', Q, Kg) * scaling
        attn = jax.nn.softmax(scores, axis=-1)
        out = jnp.einsum('bhqk,bhkd->bhqd', attn, Vg)
        out = out.transpose(0, 2, 1, 3).reshape(B, Tq, E)
        return out @ Wo.T + bo

    def _L1_ffn_ref(x, in_proj_w, in_proj_b, out_proj_w, out_proj_b, ln1_g, ln1_b, ln2_g, ln2_b, wg, w1, b1, w2, b2):
        import jax, jax.numpy as jnp
        import numpy as np
        D = 128
        H = 4
        HD = D // H
        E = 8
        FF = 512
        CAP_FACTOR = 1.0

        def _ln(x, g, b, eps=1e-05):
            mu = jnp.mean(x, -1, keepdims=True)
            v = jnp.mean((x - mu) ** 2, -1, keepdims=True)
            return (x - mu) * jax.lax.rsqrt(v + eps) * g + b

        def _mha(x, w, b, ow, ob):
            L, N, _ = x.shape
            qkv = x @ w.T + b
            q, k, v = jnp.split(qkv, 3, axis=-1)
            rh = lambda t: t.reshape(L, N, H, HD).transpose(1, 2, 0, 3)
            q, k, v = (rh(q), rh(k), rh(v))
            scores = jnp.einsum('nhld,nhmd->nhlm', q, k) / np.float32(np.sqrt(HD))
            attn = jax.nn.softmax(scores, axis=-1)
            o = jnp.einsum('nhlm,nhmd->nhld', attn, v).transpose(2, 0, 1, 3).reshape(L, N, D)
            return o @ ow.T + ob

        def _moe(x, wg, w1, b1, w2, b2):
            L, N, _ = x.shape
            S = L * N
            cap = int(CAP_FACTOR * S) // E
            xf = x.reshape(S, D)
            gates = jax.nn.softmax(xf @ wg, axis=-1)
            idx = jnp.argmax(gates, axis=-1)
            mask1 = jax.nn.one_hot(idx, E, dtype=x.dtype)
            loc = jnp.sum((jnp.cumsum(mask1, 0) - 1.0) * mask1, -1).astype(jnp.int32)
            keep = loc < cap
            gate_val = jnp.take_along_axis(gates, idx[:, None], -1)[:, 0]
            slot = jnp.where(keep, idx.astype(jnp.int32) * cap + loc, E * cap)
            disp = jnp.zeros((E * cap, D), x.dtype).at[slot].set(xf, mode='drop')
            disp = disp.reshape(E, cap, D)
            h = jnp.einsum('ecd,edf->ecf', disp, w1) + b1[:, None, :]
            y = (jnp.einsum('ecf,efd->ecd', h, w2) + b2[:, None, :]).reshape(E * cap, D)
            out = jnp.where(keep[:, None], gate_val[:, None] * y[jnp.minimum(slot, E * cap - 1)], 0.0)
            return out.reshape(L, N, D)
        y1 = _ln(x + _mha(x, in_proj_w, in_proj_b, out_proj_w, out_proj_b), ln1_g, ln1_b)
        y2 = _ln(y1 + _moe(y1, wg, w1, b1, w2, b2), ln2_g, ln2_b)
        return y2
    x = x + jnp.tanh(g_xattn[0]) * _L0_xattn_ref(_layernorm(x, axis=-1), ctx_1024, ctx_1024, mask_Bx1xS2_ik1)
    x = x + jnp.tanh(g_ffn[0]) * _L0_ffn_ref(_layernorm(x, axis=-1), L0_ffn_U1, L0_ffn_V1, L0_ffn_b1, L0_ffn_U2, L0_ffn_V2, L0_ffn_b2)
    x = x + jnp.tanh(g_xattn[1]) * _L1_xattn_ref(_layernorm(x, axis=-1), ctx_1024, L1_xattn_Wq, L1_xattn_bq, L1_xattn_Wk, L1_xattn_bk, L1_xattn_Wv, L1_xattn_bv, L1_xattn_Wo, L1_xattn_bo, 16)
    x = x + jnp.tanh(g_ffn[1]) * _L1_ffn_ref(_layernorm(x, axis=-1), L1_ffn_in_proj_w, L1_ffn_in_proj_b, L1_ffn_out_proj_w, L1_ffn_out_proj_b, L1_ffn_ln1_g, L1_ffn_ln1_b, L1_ffn_ln2_g, L1_ffn_ln2_b, L1_ffn_wg, L1_ffn_w1, L1_ffn_b1, L1_ffn_w2, L1_ffn_b2)
    return x

_drawn_inputs = setup_inputs


def setup_inputs(seed=0):
    import zlib

    import numpy as np

    out = dict(_drawn_inputs(seed))
    spreads = {'g_ffn': (-1.0, 0.2),
     'L0_ffn_b1': (0.0, 0.8),
     'L0_ffn_b2': (0.0, 0.348),
     'L1_xattn_bq': (0.0, 2.0),
     'L1_xattn_bk': (0.0, 2.0),
     'L1_xattn_bv': (0.0, 1.264),
     'L1_xattn_bo': (0.0, 0.293),
     'L1_ffn_in_proj_b': (0.0, 0.775),
     'L1_ffn_out_proj_b': (0.0, 0.1),
     'L1_ffn_ln1_g': (1.0, 0.2),
     'L1_ffn_ln1_b': (0.0, 0.1),
     'L1_ffn_ln2_g': (1.0, 0.2),
     'L1_ffn_ln2_b': (0.0, 0.1),
     'L1_ffn_b1': (0.0, 2.0),
     'L1_ffn_b2': (0.0, 1.755)}
    factors = {'L0_ffn_U1': 8.0,
     'L0_ffn_V1': 8.0,
     'L0_ffn_U2': 8.0,
     'L0_ffn_V2': 8.0,
     'L1_xattn_Wq': 56.427,
     'L1_xattn_Wk': 49.784,
     'L1_ffn_in_proj_w': 3.528,
     'L1_xattn_Wv': 4.267,
     'L1_ffn_wg': 2.767,
     'L1_ffn_w1': 8.0,
     'L1_ffn_w2': 3.873}
    for name, (base, spread) in spreads.items():
        noise = np.random.default_rng([zlib.crc32(name.encode()), seed]).standard_normal(out[name].shape)
        drawn = base * np.exp(spread * noise) if base else spread * noise
        out[name] = jnp.asarray(drawn.astype(out[name].dtype))
    for name, factor in factors.items():
        out[name] = (out[name] * factor).astype(out[name].dtype)
    return out
```

```python
from contextlib import ExitStack

import concourse.bass as bass
from concourse import mybir

F32 = mybir.dt.float32
BF16 = mybir.dt.bfloat16
I32 = mybir.dt.int32
ALU = mybir.AluOpType
ACT = mybir.ActivationFunctionType
AX_X = mybir.AxisListType.X

P = 128
D = 128
NB, NS = 32, 64
T = NB * NS // P
G = 4
TG = T // G
GT = TG * P
KEYS = 64
R = 32
FC = 4
H0 = 16
HD0 = D // H0
H1, HD1 = 4, 32
L, N = 32, 64
E = 8
CAP = NB * NS // E
EPS = 1e-5
SCALE_A = 1.0 / 16.0 ** 0.5
KEEP_A = 1.0 / (1.0 - 0.1 / (128 * 256))
SCALE_C = float(HD0) ** -0.5
SCALE_D = float(HD1) ** -0.5
MASKED = -1e30

A, B, C, SA, LN1, LN2 = range(6)

BQ, BK, BV, IPB, L1G, L1B, FB1, MB1 = 0, 1, 2, 3, 6, 7, 8, 12
NROWS = MB1 + E * FC

J_CTX, J_W, J_COL, J_KT, J_VT, J_VO, J_W1, J_WC, J_CT, J_IP, J_C8 = 0, 4, 5, 6, 10, 14, 18, 26, 28, 29, 30
JOBS = 31


def program(nc, x, ctxt, mask, g_xattn, g_ffn, U1, V1, b1, U2, V2, b2,
            Wq, bq, Wk, bk, Wv, bv, Wo, bo,
            ipw, ipb, opw, opb, ln1g, ln1b, ln2g, ln2b, wg, w1, mb1, w2, mb2, out):
    with ExitStack() as ctx:
        def sb(name, shape, dt=F32):
            return ctx.enter_context(nc.sbuf_tensor(name, shape, dt))

        def sem(name):
            return ctx.enter_context(nc.semaphore(name))

        def row(v):
            return v.rearrange("(o n) -> o n", o=1)

        def spread(ap, k):
            return ap.unsqueeze(1).to_broadcast([P, k, ap.shape[1]])

        def along(ap, k):
            return ap.unsqueeze(len(ap.shape)).to_broadcast([*ap.shape, k])

        ps = ctx.enter_context(nc.psum_tensor("ps", [P, 8, 512], F32))

        x0, x1, x2, x3 = (sb(f"x{i}", [P, T, D]) for i in range(4))
        xb2 = x0
        xn = sb("xn", [P, T, D])
        xr = x2
        y1 = x0
        xf = x1
        res = xn
        xT = sb("xT", [P, T * P])
        xnl = xT[:, :].rearrange("p (n l) -> p n l", l=L)
        stats = sb("stats", [P, T, 6])
        mv = sb("mv", [P, T, 2])
        veps = sb("veps", [P, T])
        rstd = sb("rstd", [P, T])
        minus_half = sb("minus_half", [P, TG])

        ctxv = sb("ctxv", [P, T, D])
        hat = ctxv
        ctxT = sb("ctxT", [P, T * P])
        kmT = sb("kmT", [P, T * P])
        vmT = sb("vmT", [P, T * P])
        vo = sb("vo", [P, T, D])
        head_mask = sb("head_mask", [P, H0])
        bo16 = sb("bo16", [P, D])

        w_rows = sb("w_rows", [P, 4, D])
        wT = sb("wT", [P, 4, D])
        rows = sb("rows", [NROWS, D])
        col = sb("col", [P, NROWS])
        gates_in = sb("gates_in", [P, 4])
        gates = sb("gates", [P, 4])
        u1 = sb("u1", [P, R])
        v1 = sb("v1", [R, FC * P])
        u2 = sb("u2", [P, FC, R])
        v2 = sb("v2", [P, TG, D])
        b2b = sb("b2b", [P, D])
        b2g = sb("b2g", [P, D])
        ip_rows = w_rows
        ipT = sb("ipT", [P, 4, D])
        vbb = sb("vbb", [P, D])
        obb = sb("obb", [P, D])
        l1gb, l1bb, l2gb, l2bb = (sb(n, [P, D]) for n in ("l1gb", "l1bb", "l2gb", "l2bb"))
        wgs = sb("wgs", [P, E])
        w1s = sb("w1s", [P, E, FC * P])
        w2s = sb("w2s", [P, E, FC, D])
        w1T = sb("w1T", [P, E, FC, P])
        wc = sb("wc", [P, E, D])
        cT = sb("cT", [P, E])
        mb2s = sb("mb2s", [E, D])
        c8 = sb("c8", [E, D])

        mx = sb("mx", [P, T, H0])
        negmax = sb("negmax", [P, T])
        ssum = sb("ssum", [P, T, H0])
        rsum = sb("rsum", [P, T, H0])
        fac = sb("fac", [P, T])
        prob = sb("prob", [P, T, KEYS])
        probT = sb("probT", [P, G, 2, P])
        hT = sb("hT", [P, FC, T * P])
        qs = prob[:, 0:T // 2, :].rearrange("p (g a) k -> p g (a k)", g=G)
        qT = prob[:, T // 2:T, :].rearrange("p (g a) k -> p g (a k)", g=G)
        loT = ctxT[0:R, :]
        mrow = hT[0:1, 0, :].bitcast(I32)
        mbias = hT[0:1, 1, 0:NB * KEYS // 2].bitcast(BF16)
        qcT = hT[:, 0, :]
        qdT = hT[:, 0, :].rearrange("p (n l) -> p n l", l=L)
        kdT = hT[:, 1, :].rearrange("p (n l) -> p n l", l=L)
        vd = hT[:, 2, :].rearrange("p (t n) -> p t n", n=D)
        oT = hT[:, 3, :].rearrange("p (l n) -> p l n", n=N)
        pd = ctxT[:, 0:1024].rearrange("p (s h n) -> p s h n", s=2, h=H1)
        pdT = ctxT[:, 1024:2048].rearrange("p (s h n) -> p s h n", s=2, h=H1)
        mxd = sb("mxd", [P, H1 * TG])
        sumd = sb("sumd", [P, G, H1 * TG])
        rsd = sb("rsd", [P, G, H1 * TG])
        y1T = ctxT
        lsh, lexp, oh, ranked = (prob[:, 2 * i:2 * i + 2, :].rearrange("p a (b e) -> p (a b) e", e=E)
                                 for i in range(4))
        lmax = sb("lmax", [P, T])
        lsum = sb("lsum", [P, T])
        gate = sb("gate", [P, T])
        rank8 = sb("rank8", [P, E])
        best = sb("best", [P, T])
        chosen = sb("chosen", [P, T, E], BF16)
        kept = sb("kept", [P, T, E], BF16)
        keptT = kmT[0:E, :]
        keptTb = hT[0:E, 0, 0:T * P // 2].bitcast(BF16)
        xm = vmT[:, :].rearrange("p (i n) -> p i n", i=4)
        ident = sb("ident", [P, P])
        identb = sb("identb", [P, P], BF16)
        tri = sb("tri", [P, P], BF16)
        ones = sb("ones", [P, P], BF16)
        zeros = sb("zeros", [1, GT], BF16)
        pick = sb("pick", [E, E, P], BF16)

        ld_x = [sem(f"ld_x{g}") for g in range(G)]
        ld_ctx = [sem(f"ld_ctx{g}") for g in range(G)]
        ld_mask, ld_w, ld_rows, ld_gate, ld_bo = (sem(n) for n in ("ld_mask", "ld_w", "ld_rows", "ld_gate", "ld_bo"))
        ld_ffn, ld_v2, ld_b2, ld_ip, ld_bc = (sem(n) for n in ("ld_ffn", "ld_v2", "ld_b2", "ld_ip", "ld_bc"))
        ld_w1, ld_w2 = sem("ld_w1"), sem("ld_w2")
        stored = sem("stored")
        pool_own = sem("pool_own")
        ident_ready, headmask_ready, v2_zeroed, moe_const = (
            sem(n) for n in ("ident_ready", "headmask_ready", "v2_zeroed", "moe_const"))
        prep_filled, prep_taken, kv_masked, vo_ready, c8_ready = (
            sem(n) for n in ("prep_filled", "prep_taken", "kv_masked", "vo_ready", "c8_ready"))
        gates_ready, fac_ready = sem("gates_ready"), sem("fac_ready")
        mbias_ready = sem("mbias_ready")
        dve_own = sem("dve_own")
        stats_ready, rstd_ready, norm_ready = sem("stats_ready"), sem("rstd_ready"), sem("norm_ready")
        xT_filled, xT_ready = sem("xT_filled"), sem("xT_ready")
        score_filled, negmax_ready, prob_a, prob_c, shifted, exped = (
            sem(n) for n in ("score_filled", "negmax_ready", "prob_a", "prob_c", "shifted", "exped"))
        probT_filled, probT_ready, pv_filled, x_ready = (
            sem(n) for n in ("probT_filled", "probT_ready", "pv_filled", "x_ready"))
        lo_filled, lo_ready, h_filled, h_ready, q_filled, q_ready, qT_filled, qT_ready, ffn_filled, xb2_ready = (
            sem(n) for n in ("lo_filled", "lo_ready", "h_filled", "h_ready", "q_filled", "q_ready",
                             "qT_filled", "qT_ready", "ffn_filled", "xb2_ready"))
        qc_filled, qc_ready = sem("qc_filled"), sem("qc_ready")
        qd_filled, qd_ready, kd_filled, kd_ready, vd_filled, vd_ready = (
            sem(n) for n in ("qd_filled", "qd_ready", "kd_filled", "kd_ready", "vd_filled", "vd_ready"))
        sd_filled, sd_shifted, sd_exped, pdT_ready, od_filled, od_ready, op_filled, xr_ready = (
            sem(n) for n in ("sd_filled", "sd_shifted", "sd_exped", "pdT_ready", "od_filled", "od_ready",
                             "op_filled", "xr_ready"))
        hatT_filled, y1T_ready, y1_ready, lg_filled, lsh_ready, lexp_ready, chosen_ready, count_filled = (
            sem(n) for n in ("hatT_filled", "y1T_ready", "y1_ready", "lg_filled", "lsh_ready", "lexp_ready",
                             "chosen_ready", "count_filled"))
        kept_ready, keptT_filled, keptTb_ready, keptT_ready = (
            sem(n) for n in ("kept_ready", "keptT_filled", "keptTb_ready", "keptT_ready"))
        wide_filled, xm_ready, xm_used, moe_filled, xf_ready, res_ready = (
            sem(n) for n in ("wide_filled", "xm_ready", "xm_used", "moe_filled", "xf_ready", "res_ready"))

        def tiles(g):
            return range(g * TG, (g + 1) * TG)

        def grp(g):
            return slice(g * TG, (g + 1) * TG)

        def key_cols(batch):
            u, half, b = batch // 4, batch % 4 // 2, batch % 2
            return slice(((u * 2 + b) * 2 + half) * KEYS, ((u * 2 + b) * 2 + half + 1) * KEYS)

        block = ctx.enter_context(nc.Block())

        @block.sync
        def _(sp):
            xv = x.rearrange("(t b) s d -> (b s) t d", b=2)
            ov = out.rearrange("(t b) s d -> (b s) t d", b=2)
            cv = ctxt.rearrange("(u h b) s d -> h s u b d", h=2, b=2)

            def load_ctx(g):
                for u in (2 * g, 2 * g + 1):
                    for h in range(2):
                        sp.dma_start(ctxv[h * 64:h * 64 + 64, 2 * u:2 * u + 2, :],
                                     cv[h, :, u, :, :]).then_inc(ld_ctx[g], 16)

            sp.dma_start(x0[:, grp(0), :], xv[:, grp(0), :]).then_inc(ld_x[0], 16)
            load_ctx(0)
            sp.dma_start(mrow[:, :], mask.rearrange("b o s -> o (b s)")).then_inc(ld_mask, 16)
            for g in range(1, G):
                sp.dma_start(x0[:, grp(g), :], xv[:, grp(g), :]).then_inc(ld_x[g], 16)
                load_ctx(g)
            sp.dma_start(w1s[:, :, :], w1.rearrange("e d f -> d e f")).then_inc(ld_w1, 16)
            sp.dma_start(w2s[:, :, :, :], w2.rearrange("e (c f) d -> f e c d", f=P)).then_inc(ld_w2, 16)
            sp.wait_ge(prep_filled, J_W + 1)
            for i in range(4):
                src = opw if i == 3 else ipw[i * D:(i + 1) * D, :]
                sp.dma_start(ip_rows[:, i, :], src).then_inc(ld_ip, 16)
            for g in range(G):
                sp.wait_ge(res_ready, g + 1)
                sp.dma_start(ov[:, grp(g), :], res[:, grp(g), :]).then_inc(stored, 16)
            sp.wait_ge(stored, 16 * G)

        @block.gpsimd
        def _(pool):
            own = [0]

            def after(ins):
                own[0] += 1
                ins.then_inc(pool_own, 1)
                pool.wait_ge(pool_own, own[0])

            nc.gpsimd.memset(minus_half[:, :], -0.5)
            after(nc.gpsimd.memset(ident[:, :], 0.0))
            nc.gpsimd.affine_select(out=ident[:, :], in_=ident[:, :], compare_op=ALU.not_equal, fill=1.0,
                                    base=0, pattern=[[-1, P]], channel_multiplier=1).then_inc(ident_ready, 1)
            nc.gpsimd.memset(ones[:, :], 1.0).then_inc(ident_ready, 1)

            def rsqrt(s, g):
                pool.wait_ge(stats_ready, s * G + g + 1)
                after(nc.gpsimd.tensor_scalar(veps[:, grp(g)], mv[:, grp(g), 1], EPS, None, ALU.add))
                nc.gpsimd.tensor_tensor(rstd[:, grp(g)], veps[:, grp(g)], minus_half[:, :],
                                        ALU.pow).then_inc(rstd_ready, 1)

            for g in range(G):
                rsqrt(A, g)
            after(nc.gpsimd.memset(head_mask[:, :], 1.0))
            after(nc.gpsimd.affine_select(out=head_mask[:, :], in_=head_mask[:, :], compare_op=ALU.is_ge, fill=0.0,
                                          base=0, pattern=[[-HD0, H0]], channel_multiplier=1))
            after(nc.gpsimd.affine_select(out=head_mask[:, :], in_=head_mask[:, :], compare_op=ALU.is_ge, fill=0.0,
                                          base=HD0 - 1, pattern=[[HD0, H0]], channel_multiplier=-1))
            nc.gpsimd.memset(v2[:, :, :], 0.0).then_inc(v2_zeroed, 1)
            pool.wait_ge(ld_bo, 16)
            after(nc.gpsimd.tensor_scalar(bo16[:, :], bo16[:, :], 1.0 / H0, None, ALU.mult))
            for first, buf in ((J_KT, kmT), (J_VT, vmT)):
                for g in range(G):
                    pool.wait_ge(prep_taken, first + g + 1)
                    v = buf[:, g * GT:(g + 1) * GT].rearrange("p (r h) -> p r h", h=H0)
                    nc.gpsimd.tensor_tensor(v, v, spread(head_mask[:, :], GT // H0), ALU.mult).then_inc(kv_masked, 1)
                if first == J_KT:
                    pool.wait_ge(ld_gate, 32)
                    pool.wait_ge(gates_ready, 1)
                    pool.wait_ge(ld_b2, 16)
                    after(nc.gpsimd.tensor_scalar(b2g[:, :], b2b[:, :], gates[:, 2:3], None, ALU.mult))
            for g in range(G):
                rsqrt(B, g)
                pool.wait_ge(x_ready, A * G + g + 1)
                nc.gpsimd.tensor_tensor(xb2[:, grp(g), :], x1[:, grp(g), :], spread(b2g[:, :], TG),
                                        ALU.add).then_inc(xb2_ready, 1)
            for g in range(G):
                pool.wait_ge(prep_taken, J_VO + g + 1)
                nc.gpsimd.tensor_tensor(vo[:, grp(g), :], vo[:, grp(g), :], spread(bo16[:, :], TG),
                                        ALU.add).then_inc(vo_ready, 1)
            nc.gpsimd.memset(zeros[:, :], 0.0).then_inc(moe_const, 1)
            nc.gpsimd.tensor_copy(identb[:, :], ident[:, :]).then_inc(moe_const, 1)
            nc.gpsimd.affine_select(out=tri[:, :], in_=ones[:, :], compare_op=ALU.is_ge, fill=0.0,
                                    base=0, pattern=[[1, P]], channel_multiplier=-1).then_inc(moe_const, 1)
            after(nc.gpsimd.memset(pick[:, :, :], 0.0))
            nc.gpsimd.affine_select(out=pick[:, :, :], in_=pick[:, :, :], compare_op=ALU.not_equal, fill=1.0,
                                    base=0, pattern=[[-1, E], [0, P]], channel_multiplier=1).then_inc(moe_const, 1)
            nc.gpsimd.iota(rank8[:, :], pattern=[[-1, E]], base=E, channel_multiplier=0,
                           allow_small_or_imprecise_dtypes=True).then_inc(moe_const, 1)
            pool.wait_ge(ld_bc, 16 * 6)
            nc.gpsimd.tensor_scalar(l2gb[:, :], l2gb[:, :], gates[:, 3:4], None, ALU.mult).then_inc(moe_const, 1)
            after(nc.gpsimd.tensor_scalar(l2bb[:, :], l2bb[:, :], gates[:, 3:4], None, ALU.mult))
            for g in range(G):
                rsqrt(C, g)
            for g in range(G):
                rsqrt(SA, g)
                pool.wait_ge(x_ready, C * G + g + 1)
                nc.gpsimd.tensor_tensor(xf[:, grp(g), :], x3[:, grp(g), :], spread(l2bb[:, :], TG),
                                        ALU.add).then_inc(xf_ready, 1)
            for g in range(G):
                pool.wait_ge(norm_ready, SA * G + g + 1)
                nc.gpsimd.tensor_tensor(xr[:, grp(g), :], xn[:, grp(g), :], spread(obb[:, :], TG),
                                        ALU.add).then_inc(xr_ready, 1)
            for g in range(G):
                rsqrt(LN1, g)
            for g in range(G):
                pool.wait_ge(norm_ready, LN1 * G + g + 1)
                after(nc.gpsimd.tensor_tensor(y1[:, grp(g), :], hat[:, grp(g), :], spread(l1gb[:, :], TG), ALU.mult))
                nc.gpsimd.tensor_tensor(y1[:, grp(g), :], y1[:, grp(g), :], spread(l1bb[:, :], TG),
                                        ALU.add).then_inc(y1_ready, 1)
            for g in range(G):
                rsqrt(LN2, g)

        @block.scalar
        def _(act):
            for i, w in enumerate((Wk, Wv, Wq, Wo)):
                act.dma_start(w_rows[:, i, :], w).then_inc(ld_w, 16)
            for i, v in ((BQ, bq), (BK, bk), (BV, bv), (L1G, ln1g), (L1B, ln1b)):
                act.dma_start(rows[i:i + 1, :], row(v)).then_inc(ld_rows, 16)
            act.dma_start(rows[IPB:IPB + 3, :], ipb.rearrange("(i n) -> i n", n=D)).then_inc(ld_rows, 16)
            act.dma_start(rows[FB1:FB1 + FC, :], b1.rearrange("(i n) -> i n", n=P)).then_inc(ld_rows, 16)
            act.dma_start(rows[MB1:MB1 + E * FC, :], mb1.rearrange("e (c n) -> (e c) n", n=P)).then_inc(ld_rows, 16)
            act.dma_start(gates_in[:, 0:2], row(g_xattn).to_broadcast([P, 2])).then_inc(ld_gate, 16)
            act.dma_start(gates_in[:, 2:4], row(g_ffn).to_broadcast([P, 2])).then_inc(ld_gate, 16)
            act.dma_start(bo16[:, :], row(bo).to_broadcast([P, D])).then_inc(ld_bo, 16)
            act.dma_start(b2b[:, :], row(b2).to_broadcast([P, D])).then_inc(ld_b2, 16)
            act.dma_start(u1[:, :], U1).then_inc(ld_ffn, 16)
            act.dma_start(v1[:, :], V1).then_inc(ld_ffn, 16)
            act.dma_start(u2[:, :, :], U2.rearrange("(c f) r -> f c r", f=P)).then_inc(ld_ffn, 16)
            for dst, v in ((vbb, ipb[2 * D:3 * D]), (obb, opb), (l1gb, ln1g), (l1bb, ln1b), (l2gb, ln2g), (l2bb, ln2b)):
                act.dma_start(dst[:, :], row(v).to_broadcast([P, D])).then_inc(ld_bc, 16)
            act.dma_start(wgs[:, :], wg).then_inc(ld_ffn, 16)
            act.dma_start(mb2s[:, :], mb2).then_inc(ld_ffn, 16)
            act.wait_ge(v2_zeroed, 1)
            for t in range(TG):
                act.dma_start(v2[R * t:R * t + R, t, :], V2).then_inc(ld_v2, 16)

            def take(j, dst, src, **kw):
                act.wait_ge(prep_filled, j + 1)
                fn = ACT.Identity if kw else ACT.Copy
                nc.scalar.activation(dst, src, fn, **kw).then_inc(prep_taken, 1)

            def job(j):
                return ps[:, 6 + j % 2, :]

            def take_xT(s, g):
                act.wait_ge(xT_filled, s * G + g + 1)
                nc.scalar.activation(xT[:, g * GT:(g + 1) * GT], ps[:, g, :], ACT.Copy).then_inc(xT_ready, 1)

            def take_probT(k, g):
                act.wait_ge(probT_filled, k * G + g + 1)
                nc.scalar.activation(probT[:, g, :, :], ps[:, g, 0:2 * P].rearrange("p (i q) -> p i q", i=2),
                                     ACT.Copy).then_inc(probT_ready, 1)

            def take_heads(g):
                act.wait_ge(od_filled, g + 1)
                for k in range(4):
                    ins = nc.scalar.activation(
                        oT[:, :, 16 * g:16 * g + 16].rearrange("p l (q k) -> p k q l", k=4)[:, k],
                        ps[:, 4 + k, 0:P].rearrange("p (q l) -> p q l", q=TG), ACT.Copy)
                ins.then_inc(od_ready, 1)

            for g in range(G):
                take(J_CTX + g, ctxT[:, g * GT:(g + 1) * GT], job(J_CTX + g))
            take(J_W, wT[:, :, :], job(J_W).rearrange("p (i n) -> p i n", i=4))
            take(J_COL, col[:, :], job(J_COL)[:, 0:NROWS])
            act.wait_ge(ld_gate, 32)
            nc.scalar.activation(gates[:, :], gates_in[:, :], ACT.Tanh).then_inc(gates_ready, 1)
            for g in range(G):
                take_xT(A, g)
            act.wait_ge(prep_taken, J_COL + 1)
            for g in range(G):
                take(J_KT + g, kmT[:, g * GT:(g + 1) * GT], job(J_KT + g), bias=col[:, BK:BK + 1], scale=1.0)
            for g in range(G):
                act.wait_ge(negmax_ready, g + 1)
                for t in tiles(g):
                    ins = nc.scalar.activation(prob[:, t, :], ps[:, g, t % TG * KEYS:(t % TG + 1) * KEYS], ACT.Exp,
                                               bias=negmax[:, t:t + 1], scale=SCALE_A, accum_out=ssum[:, t, 0:1])
                ins.then_inc(prob_a, 1)
            for g in range(G):
                take(J_VT + g, vmT[:, g * GT:(g + 1) * GT], job(J_VT + g), bias=col[:, BV:BV + 1], scale=1.0)
            for g in range(G):
                take_probT(0, g)
            for g in range(G):
                take(J_VO + g, vo[:, grp(g), :], job(J_VO + g).rearrange("p (i n) -> p i n", i=TG))
            for g in range(G):
                take_xT(B, g)
            for g in range(G):
                act.wait_ge(lo_filled, g + 1)
                nc.scalar.activation(loT[:, g * GT:(g + 1) * GT], ps[0:R, g, :], ACT.Copy).then_inc(lo_ready, 1)
            for c in range(FC):
                for g in range(G):
                    act.wait_ge(h_filled, c * G + g + 1)
                    nc.scalar.activation(hT[:, c, g * GT:(g + 1) * GT], ps[:, g, :], ACT.Gelu_apprx_tanh,
                                         bias=col[:, FB1 + c:FB1 + c + 1], scale=1.0).then_inc(h_ready, 1)
            for g in range(G):
                act.wait_ge(q_filled, g + 1)
                nc.scalar.activation(qs[:, g, :], ps[:, g, 0:P], ACT.Copy).then_inc(q_ready, 1)
            for j in range(J_W1, J_W1 + 4):
                take(j, w1T[:, j - J_W1, :, :], job(j).rearrange("p (c n) -> p c n", c=FC))
            for g in range(G):
                act.wait_ge(qT_filled, g + 1)
                nc.scalar.activation(qT[:, g, :], ps[:, g, 0:P], ACT.Copy).then_inc(qT_ready, 1)
            for j in range(J_W1 + 4, J_W1 + 8):
                take(j, w1T[:, j - J_W1, :, :], job(j).rearrange("p (c n) -> p c n", c=FC))
            for g in range(G):
                take_xT(C, g)
            for g in range(G):
                act.wait_ge(qc_filled, g + 1)
                nc.scalar.activation(qcT[:, g * GT:(g + 1) * GT], ps[:, g, :], ACT.Identity,
                                     bias=col[:, BQ:BQ + 1], scale=1.0).then_inc(qc_ready, 1)
            for j in (J_WC, J_WC + 1):
                k = (j - J_WC) * 4
                take(j, wc[:, k:k + 4, :], job(j).rearrange("p (e n) -> p e n", e=4))
            take(J_CT, cT[:, :], job(J_CT)[:, 0:E])
            for g in range(G):
                act.wait_ge(shifted, g + 1)
                v = prob[:, grp(g), :]
                nc.scalar.activation(v, v, ACT.Exp, scale=SCALE_C).then_inc(exped, 1)
            take(J_IP, ipT[:, :, :], job(J_IP).rearrange("p (i n) -> p i n", i=4))
            for g in range(G):
                take_probT(1, g)
            for g in range(G):
                act.wait_ge(xT_filled, SA * G + g + 1)
                nc.scalar.activation(xnl[:, :, 8 * g:8 * g + 8].rearrange("p n l -> p l n"),
                                     ps[:, g, :].rearrange("p (l n) -> p l n", n=N), ACT.Copy).then_inc(xT_ready, 1)
            for g in range(G):
                for filled, done, b, dst, which in ((qd_filled, qd_ready, g, qdT, 0), (kd_filled, kd_ready, 4 + g, kdT, 1)):
                    act.wait_ge(filled, g + 1)
                    nc.scalar.activation(dst[:, :, 8 * g:8 * g + 8],
                                         ps[:, b, :].rearrange("p (n l) -> p n l", n=N), ACT.Identity,
                                         bias=col[:, IPB + which:IPB + which + 1], scale=1.0).then_inc(done, 1)
            for g in range(G):
                act.wait_ge(sd_shifted, g + 1)
                v = pd[:, g % 2, :, :]
                nc.scalar.activation(v, v, ACT.Exp, scale=SCALE_D).then_inc(sd_exped, 1)
                if g > 0:
                    take_heads(g - 1)
            take_heads(G - 1)
            for g in range(G):
                act.wait_ge(hatT_filled, g + 1)
                nc.scalar.activation(y1T[:, g * GT:(g + 1) * GT], ps[:, g, :], ACT.Identity,
                                     bias=col[:, L1B:L1B + 1], scale=col[:, L1G:L1G + 1]).then_inc(y1T_ready, 1)
            act.wait_ge(lsh_ready, 1)
            nc.scalar.activation(lexp[:, :, :], lsh[:, :, :], ACT.Exp).then_inc(lexp_ready, 1)
            for g in range(G):
                act.wait_ge(keptT_filled, g + 1)
                nc.scalar.activation(keptTb[:, g * GT:(g + 1) * GT], ps[0:E, g, :], ACT.Copy).then_inc(keptTb_ready, 1)

        @block.tensor
        def _(pe):
            def mm(o, lhsT, rhs, start=True, stop=True):
                return nc.tensor.matmul(o, lhsT, rhs, start=start, stop=stop)

            def job(j):
                if j >= 2:
                    pe.wait_ge(prep_taken, j - 1)
                return ps[:, 6 + j % 2, :]

            def transpose4(dst, src):
                for i in range(4):
                    ins = nc.tensor.transpose(dst[:, i * P:(i + 1) * P], src(i), ident[:, :])
                return ins

            def x_transposes(s, g):
                pe.wait_ge(norm_ready, s * G + g + 1)
                transpose4(ps[:, g, :], lambda i: xn[:, g * TG + i, :]).then_inc(xT_filled, 1)

            def prob_transposes(k, g):
                pe.wait_ge(prob_a if k == 0 else prob_c, g + 1)
                for i in range(2):
                    pair = prob[:, g * TG + 2 * i:g * TG + 2 * i + 2, :].rearrange("p t k -> p (t k)")
                    ins = nc.tensor.transpose(ps[:, g, i * P:(i + 1) * P], pair, ident[:, :])
                ins.then_inc(probT_filled, 1)

            def prob_values(k, g, values):
                pe.wait_ge(probT_ready, k * G + g + 1)
                if g >= 2:
                    pe.wait_ge(x_ready, (A if k == 0 else C) * G + g - 1)
                for t in tiles(g):
                    i, half = t % TG // 2, t % 2
                    for b in range(2):
                        ins = mm(ps[64 * b:64 * b + 64, 4 + g % 2 if half else g, i * P:(i + 1) * P],
                                 probT[64 * half:64 * half + 64, g, i, 64 * b:64 * b + 64],
                                 values[64 * half:64 * half + 64, (t // 2) * 2 + b, :])
                ins.then_inc(pv_filled, 1)

            pe.wait_ge(ident_ready, 2)
            for g in range(G):
                pe.wait_ge(ld_ctx[g], 64)
                transpose4(job(J_CTX + g), lambda i: ctxv[:, g * TG + i, :]).then_inc(prep_filled, 1)
            pe.wait_ge(ld_w, 16 * 4)
            transpose4(job(J_W), lambda i: w_rows[:, i, :]).then_inc(prep_filled, 1)
            pe.wait_ge(ld_rows, 16 * 8)
            nc.tensor.transpose(job(J_COL)[:, 0:NROWS], rows[:, :], ident[0:NROWS, 0:NROWS]).then_inc(prep_filled, 1)
            for g in range(G):
                x_transposes(A, g)
            for g in range(G):
                o = job(J_KT + g)
                if g == 0:
                    pe.wait_ge(prep_taken, J_W + 1)
                mm(o, wT[:, 0, :], ctxT[:, g * GT:(g + 1) * GT]).then_inc(prep_filled, 1)
            pe.wait_ge(mbias_ready, 1)
            for g in range(G):
                pe.wait_ge(xT_ready, A * G + g + 1)
                for t in tiles(g):
                    for b in range(2):
                        kc = key_cols(2 * t + b)
                        o = ps[64 * b:64 * b + 64, g, t % TG * KEYS:(t % TG + 1) * KEYS]
                        mm(o, xT[:, t * P + 64 * b:t * P + 64 * b + 64], ctxT[:, kc], stop=False)
                        ins = mm(o, ones[0:1, 0:64], mbias[0:1, (2 * t + b) * KEYS:(2 * t + b + 1) * KEYS], start=False)
                ins.then_inc(score_filled, 1)
            for g in range(G):
                mm(job(J_VT + g), wT[:, 1, :], ctxT[:, g * GT:(g + 1) * GT]).then_inc(prep_filled, 1)
            for g in range(G):
                prob_transposes(0, g)
            for g in range(G):
                o = job(J_VO + g)
                pe.wait_ge(kv_masked, G + g + 1)
                for i in range(TG):
                    c = (g * TG + i) * P
                    ins = mm(o[:, i * P:(i + 1) * P], vmT[:, c:c + P], wT[:, 3, :])
                ins.then_inc(prep_filled, 1)
            for g in range(G):
                prob_values(0, g, ctxv)
            for g in range(G):
                x_transposes(B, g)
            pe.wait_ge(ld_ffn, 16 * 5)
            for g in range(G):
                pe.wait_ge(xT_ready, B * G + g + 1)
                mm(ps[0:R, g, :], u1[:, :], xT[:, g * GT:(g + 1) * GT]).then_inc(lo_filled, 1)
            for c in range(FC):
                for g in range(G):
                    if c == 0:
                        pe.wait_ge(lo_ready, g + 1)
                    else:
                        pe.wait_ge(h_ready, (c - 1) * G + g + 1)
                    mm(ps[:, g, :], v1[:, c * P:(c + 1) * P], loT[:, g * GT:(g + 1) * GT]).then_inc(h_filled, 1)
            for g in range(G):
                pe.wait_ge(h_ready, (FC - 1) * G + g + 1)
                for i in range(TG):
                    for c in range(FC):
                        t = g * TG + i
                        ins = mm(ps[:, g, i * R:(i + 1) * R], hT[:, c, t * P:(t + 1) * P], u2[:, c, :],
                                 start=(c == 0), stop=(c == FC - 1))
                ins.then_inc(q_filled, 1)
            pe.wait_ge(ld_w1, 16)
            for j in range(J_W1, J_W1 + 4):
                e = j - J_W1
                transpose4(job(j), lambda i: w1s[:, e, i * P:(i + 1) * P]).then_inc(prep_filled, 1)
            for g in range(G):
                pe.wait_ge(q_ready, g + 1)
                nc.tensor.transpose(ps[:, g, 0:P], qs[:, g, :], ident[:, :]).then_inc(qT_filled, 1)
            for j in range(J_W1 + 4, J_W1 + 8):
                e = j - J_W1
                transpose4(job(j), lambda i: w1s[:, e, i * P:(i + 1) * P]).then_inc(prep_filled, 1)
            pe.wait_ge(ld_v2, 16 * TG)
            for g in range(G):
                pe.wait_ge(qT_ready, g + 1)
                mm(ps[:, g, :], qT[:, g, :], v2[:, :, :].rearrange("p t n -> p (t n)")).then_inc(ffn_filled, 1)
            def wc_job(j):
                o = job(j)
                for i in range(4):
                    e = (j - J_WC) * 4 + i
                    for c in range(FC):
                        ins = mm(o[:, i * P:(i + 1) * P], w1T[:, e, c, :], w2s[:, e, c, :],
                                 start=(c == 0), stop=(c == FC - 1))
                ins.then_inc(prep_filled, 1)

            for g in range(G):
                x_transposes(C, g)
            for g in range(G):
                pe.wait_ge(xT_ready, C * G + g + 1)
                mm(ps[:, g, :], wT[:, 2, :], xT[:, g * GT:(g + 1) * GT]).then_inc(qc_filled, 1)
            pe.wait_ge(ld_w2, 16)
            pe.wait_ge(prep_taken, J_W1 + E)
            wc_job(J_WC)
            pe.wait_ge(kv_masked, G)
            for g in range(G):
                pe.wait_ge(qc_ready, g + 1)
                for t in tiles(g):
                    for b in range(2):
                        ins = mm(ps[64 * b:64 * b + 64, g, t % TG * KEYS:(t % TG + 1) * KEYS],
                                 qcT[:, t * P + 64 * b:t * P + 64 * b + 64], kmT[:, key_cols(2 * t + b)])
                ins.then_inc(score_filled, 1)
            wc_job(J_WC + 1)
            o = job(J_CT)
            for e in range(E):
                for c in range(FC):
                    ins = mm(o[:, e:e + 1], w2s[:, e, c, :], col[:, MB1 + e * FC + c:MB1 + e * FC + c + 1],
                             start=(c == 0), stop=(c == FC - 1))
            ins.then_inc(prep_filled, 1)
            pe.wait_ge(ld_ip, 16 * 4)
            transpose4(job(J_IP), lambda i: ip_rows[:, i, :]).then_inc(prep_filled, 1)
            for g in range(G):
                prob_transposes(1, g)
            pe.wait_ge(vo_ready, G)
            for g in range(G):
                prob_values(1, g, vo)
            for g in range(G):
                x_transposes(SA, g)
            pe.wait_ge(x_ready, C * G + G)
            pe.wait_ge(prep_taken, J_IP + 1)
            for g in range(G):
                pe.wait_ge(xT_ready, SA * G + g + 1)
                mm(ps[:, g, :], ipT[:, 0, :], xnl[:, :, 8 * g:8 * g + 8]).then_inc(qd_filled, 1)
                mm(ps[:, 4 + g, :], ipT[:, 1, :], xnl[:, :, 8 * g:8 * g + 8]).then_inc(kd_filled, 1)
            for g in range(G):
                pe.wait_ge(kd_ready, g + 1)
                for i in range(TG):
                    q = g * TG + i
                    ins = mm(ps[:, 4 + g, i * P:(i + 1) * P], xT[:, q * P:(q + 1) * P], ipT[:, 2, :])
                ins.then_inc(vd_filled, 1)
            pe.wait_ge(qd_ready, G)
            pe.wait_ge(kd_ready, G)

            def head_scores(g):
                if g >= 1:
                    pe.wait_ge(sd_shifted, g)
                for i in range(TG):
                    for k in range(4):
                        n = 4 * (g * TG + i) + k
                        for h in range(H1):
                            hs = slice(HD1 * h, HD1 * h + HD1)
                            ins = mm(ps[L * k:L * k + L, h, i * L:(i + 1) * L], qdT[hs, n, :], kdT[hs, n, :])
                ins.then_inc(sd_filled, 1)

            def head_values(g):
                pe.wait_ge(pdT_ready, g + 1)
                if g == 0:
                    pe.wait_ge(vd_ready, G)
                else:
                    pe.wait_ge(od_ready, g)
                for i in range(TG):
                    for h in range(H1):
                        for k in range(4):
                            ks = slice(L * k, L * k + L)
                            ins = mm(ps[HD1 * h:HD1 * h + HD1, 4 + k, i * L:(i + 1) * L],
                                     vd[ks, g * TG + i, HD1 * h:HD1 * h + HD1],
                                     pdT[ks, g % 2, h, i * L:(i + 1) * L])
                ins.then_inc(od_filled, 1)

            head_scores(0)
            for g in range(1, G):
                head_scores(g)
                head_values(g - 1)
            pe.wait_ge(sd_shifted, G)
            nc.tensor.transpose(ps[0:E, 0, 0:P], cT[:, :], ident[:, :]).then_inc(prep_filled, 1)
            head_values(G - 1)
            pe.wait_ge(od_ready, G)
            pe.wait_ge(c8_ready, 1)
            flat = oT[:, :, :].rearrange("p l n -> p (l n)")
            for g in range(G):
                for i in range(TG):
                    t = g * TG + i
                    ins = mm(ps[:, g, i * P:(i + 1) * P], flat[:, t * P:(t + 1) * P], ipT[:, 3, :])
                ins.then_inc(op_filled, 1)
            for g in range(G):
                pe.wait_ge(norm_ready, LN1 * G + g + 1)
                transpose4(ps[:, g, :], lambda i: hat[:, g * TG + i, :]).then_inc(hatT_filled, 1)
            for g in range(G):
                pe.wait_ge(y1T_ready, g + 1)
                for t in tiles(g):
                    ins = mm(ps[:, 4, t * E:(t + 1) * E], y1T[:, t * P:(t + 1) * P], wgs[:, :])
            ins.then_inc(lg_filled, 1)
            pe.wait_ge(moe_const, 6)
            pe.wait_ge(chosen_ready, 1)
            mm(ps[:, 5, 0:T * E], tri[:, :], chosen[:, :, :].rearrange("p t e -> p (t e)"), stop=False)
            for t in range(T - 1):
                ins = mm(ps[:, 5, (t + 1) * E:T * E], ones[:, :], spread(chosen[:, t, :], T - 1 - t),
                         start=False, stop=(t == T - 2))
            ins.then_inc(count_filled, 1)
            pe.wait_ge(kept_ready, 1)
            for g in range(G):
                for i in range(TG):
                    ins = mm(ps[0:E, g, i * P:(i + 1) * P], kept[:, g * TG + i, :], identb[:, :])
                ins.then_inc(keptT_filled, 1)

            def widen(i):
                g, e = divmod(i, E)
                if i >= 4:
                    pe.wait_ge(xm_ready, i - 3)
                mm(ps[:, 4 + i % 4, :], pick[:, e, :], keptTb[:, g * GT:(g + 1) * GT]).then_inc(wide_filled, 1)

            pe.wait_ge(keptTb_ready, G)
            for i in range(3):
                widen(i)
            pe.wait_ge(keptT_ready, G)
            for i in range(G * E):
                g, e = divmod(i, E)
                if i + 3 < G * E:
                    widen(i + 3)
                if e == 0:
                    mm(ps[:, g, :], zeros[0:1, 0:P], zeros[0:1, :], stop=False)
                    for t in range(TG):
                        mm(ps[:, g, t * P:(t + 1) * P], keptT[:, g * GT + t * P:g * GT + (t + 1) * P], c8[:, :],
                           start=False, stop=False)
                pe.wait_ge(xm_ready, i + 1)
                for t in range(TG):
                    ins = mm(ps[:, g, t * P:(t + 1) * P], xm[:, i % 4, t * P:(t + 1) * P], wc[:, e, :],
                             start=False, stop=(e == E - 1 and t == TG - 1))
                ins.then_inc(xm_used, 1)

        @block.vector
        def _(dve):
            own = [0]

            def mark(ins):
                own[0] += 1
                ins.then_inc(dve_own, 1)

            def settle():
                dve.wait_ge(dve_own, own[0])

            def statistics(s, g, src):
                for t in tiles(g):
                    ins = nc.vector.bn_stats(stats[:, t, :], src[:, t, :])
                mark(ins)
                settle()
                for t in tiles(g):
                    ins = nc.vector.bn_aggr(mv[:, t, :], stats[:, t, :])
                ins.then_inc(stats_ready, 1)

            def normalise(s, g, src, dst):
                dve.wait_ge(rstd_ready, s * G + g + 1)
                for t in tiles(g):
                    ins = nc.vector.tensor_scalar(dst[:, t, :], src[:, t, :], mv[:, t, 0:1], rstd[:, t:t + 1],
                                                  ALU.subtract, ALU.mult)
                ins.then_inc(norm_ready, 1)

            def norm_after(s, src, dst, before):
                for g in range(G):
                    before(g)
                    statistics(s, g, src)
                    if g > 0:
                        normalise(s, g - 1, src, dst)
                normalise(s, G - 1, src, dst)

            norm_after(A, x0, xn, lambda g: dve.wait_ge(ld_x[g], 16))
            dve.wait_ge(ld_mask, 16)
            nc.vector.tensor_scalar(mbias[:, :], mrow[:, :], 0.0, MASKED, ALU.is_equal, ALU.mult).then_inc(mbias_ready, 1)
            for g in range(G):
                dve.wait_ge(score_filled, g + 1)
                mark(nc.vector.tensor_reduce(mx[:, grp(g), 0], ps[:, g, 0:TG * KEYS].rearrange("p (t k) -> p t k", k=KEYS),
                                             axis=AX_X, op=ALU.max))
                settle()
                nc.vector.tensor_scalar(negmax[:, grp(g)], mx[:, grp(g), 0], -SCALE_A, None,
                                        ALU.mult).then_inc(negmax_ready, 1)
            dve.wait_ge(gates_ready, 1)

            def residual_a(g):
                dve.wait_ge(prob_a, g + 1)
                mark(nc.vector.reciprocal(rsum[:, grp(g), 0], ssum[:, grp(g), 0]))
                settle()
                mark(nc.vector.tensor_scalar(fac[:, grp(g)], rsum[:, grp(g), 0], gates[:, 0:1], KEEP_A, ALU.mult, ALU.mult))
                settle()
                dve.wait_ge(pv_filled, g + 1)
                for t in tiles(g):
                    i = t % TG // 2
                    ins = nc.vector.scalar_tensor_tensor(x1[:, t, :], ps[:, 4 + g % 2 if t % 2 else g, i * P:(i + 1) * P],
                                                         fac[:, t:t + 1], x0[:, t, :], ALU.mult, ALU.add)
                ins.then_inc(x_ready, 1)
                dve.wait_ge(x_ready, A * G + g + 1)

            norm_after(B, x1, xn, residual_a)

            def residual_b(g):
                dve.wait_ge(ffn_filled, g + 1)
                dve.wait_ge(xb2_ready, g + 1)
                nc.vector.scalar_tensor_tensor(x2[:, grp(g), :], ps[:, g, :].rearrange("p (t n) -> p t n", n=D),
                                               gates[:, 2:3], xb2[:, grp(g), :], ALU.mult, ALU.add).then_inc(x_ready, 1)
                dve.wait_ge(x_ready, B * G + g + 1)

            norm_after(C, x2, xn, residual_b)
            for g in range(G):
                dve.wait_ge(score_filled, G + g + 1)
                s4 = ps[:, g, 0:TG * KEYS].rearrange("p (t j h) -> p t h j", h=H0, j=KEYS // H0)
                mark(nc.vector.tensor_reduce(mx[:, grp(g), :], s4, axis=AX_X, op=ALU.max))
                settle()
                for t in tiles(g):
                    ins = nc.vector.tensor_tensor(
                        prob[:, t, :].rearrange("p (j h) -> p j h", h=H0),
                        ps[:, g, t % TG * KEYS:(t % TG + 1) * KEYS].rearrange("p (j h) -> p j h", h=H0),
                        spread(mx[:, t, :], KEYS // H0), ALU.subtract)
                ins.then_inc(shifted, 1)
            for g in range(G):
                dve.wait_ge(exped, g + 1)
                mark(nc.vector.tensor_reduce(ssum[:, grp(g), :], prob[:, grp(g), :].rearrange("p t (j h) -> p t h j", h=H0),
                                             axis=AX_X, op=ALU.add))
                settle()
                mark(nc.vector.reciprocal(rsum[:, grp(g), :], ssum[:, grp(g), :]))
                settle()
                for t in tiles(g):
                    v = prob[:, t, :].rearrange("p (j h) -> p j h", h=H0)
                    ins = nc.vector.tensor_tensor(v, v, spread(rsum[:, t, :], KEYS // H0), ALU.mult)
                ins.then_inc(prob_c, 1)

            def residual_c(g):
                dve.wait_ge(pv_filled, G + g + 1)
                for half in range(2):
                    def of(buf):
                        return buf[:, grp(g), :].rearrange("p (i h) n -> p h i n", h=2)[:, half]
                    ins = nc.vector.scalar_tensor_tensor(
                        of(x3), ps[:, 4 + g % 2 if half else g, 0:2 * P].rearrange("p (i n) -> p i n", i=2),
                        gates[:, 1:2], of(x2), ALU.mult, ALU.add)
                ins.then_inc(x_ready, 1)
                dve.wait_ge(x_ready, C * G + g + 1)

            norm_after(SA, x3, xn, residual_c)
            dve.wait_ge(ld_bc, 16 * 6)
            for g in range(G):
                dve.wait_ge(vd_filled, g + 1)
                nc.vector.tensor_tensor(vd[:, grp(g), :], ps[:, 4 + g, :].rearrange("p (i n) -> p i n", n=D),
                                        spread(vbb[:, :], TG), ALU.add).then_inc(vd_ready, 1)

            def shift_heads(g):
                dve.wait_ge(sd_filled, g + 1)
                s = ps[:, 0:H1, 0:P].rearrange("p h (i m) -> p h i m", m=L)
                mark(nc.vector.tensor_reduce(mxd[:, :].rearrange("p (h i) -> p h i", h=H1), s, axis=AX_X, op=ALU.max))
                settle()
                if g >= 2:
                    dve.wait_ge(pdT_ready, g - 1)
                nc.vector.tensor_tensor(pd[:, g % 2, :, :].rearrange("p h (i m) -> p h i m", m=L), s,
                                        along(mxd[:, :].rearrange("p (h i) -> p h i", h=H1), L),
                                        ALU.subtract).then_inc(sd_shifted, 1)

            def weigh_heads(g):
                dve.wait_ge(sd_exped, g + 1)
                v = pd[:, g % 2, :, :].rearrange("p h (i m) -> p (h i) m", m=L)
                mark(nc.vector.tensor_reduce(sumd[:, g, :], v, axis=AX_X, op=ALU.add))
                settle()
                mark(nc.vector.reciprocal(rsd[:, g, :], sumd[:, g, :]))
                settle()
                mark(nc.vector.tensor_tensor(v, v, along(rsd[:, g, :], L), ALU.mult))
                settle()
                if g >= 2:
                    dve.wait_ge(od_filled, g - 1)
                nc.vector.transpose(pdT[:, g % 2, :, :].rearrange("p h n -> p (h n)"),
                                    pd[:, g % 2, :, :].rearrange("p h n -> p (h n)")).then_inc(pdT_ready, 1)

            shift_heads(0)
            for g in range(1, G):
                weigh_heads(g - 1)
                shift_heads(g)
            weigh_heads(G - 1)
            dve.wait_ge(prep_filled, J_C8 + 1)
            nc.vector.tensor_tensor(c8[:, :], ps[0:E, 0, 0:P], mb2s[:, :], ALU.add).then_inc(c8_ready, 1)

            def sum_sa(g):
                dve.wait_ge(op_filled, g + 1)
                dve.wait_ge(xr_ready, g + 1)
                mark(nc.vector.tensor_tensor(xr[:, grp(g), :], ps[:, g, :].rearrange("p (t n) -> p t n", n=D),
                                             xr[:, grp(g), :], ALU.add))
                settle()

            norm_after(LN1, xr, hat, sum_sa)
            dve.wait_ge(lg_filled, 1)
            l8 = ps[:, 4, 0:T * E].rearrange("p (t e) -> p t e", e=E)
            mark(nc.vector.tensor_reduce(lmax[:, :], l8, axis=AX_X, op=ALU.max))
            settle()
            nc.vector.tensor_tensor(lsh[:, :, :], l8, along(lmax[:, :], E), ALU.subtract).then_inc(lsh_ready, 1)
            dve.wait_ge(moe_const, 6)
            dve.wait_ge(lsh_ready, 1)
            mark(nc.vector.tensor_scalar(oh[:, :, :], lsh[:, :, :], 0.0, None, ALU.is_equal))
            settle()
            mark(nc.vector.tensor_tensor(ranked[:, :, :], oh[:, :, :], spread(rank8[:, :], T), ALU.mult))
            settle()
            mark(nc.vector.tensor_reduce(best[:, :], ranked[:, :, :], axis=AX_X, op=ALU.max))
            settle()
            nc.vector.tensor_tensor(chosen[:, :, :], ranked[:, :, :], along(best[:, :], E),
                                    ALU.is_equal).then_inc(chosen_ready, 1)
            dve.wait_ge(lexp_ready, 1)
            mark(nc.vector.tensor_reduce(lsum[:, :], lexp[:, :, :], axis=AX_X, op=ALU.add))
            settle()
            mark(nc.vector.reciprocal(gate[:, :], lsum[:, :]))
            dve.wait_ge(count_filled, 1)
            dve.wait_ge(chosen_ready, 1)
            nc.vector.scalar_tensor_tensor(kept[:, :, :].rearrange("p t e -> p (t e)"), ps[:, 5, 0:T * E], float(CAP) + 0.5,
                                           chosen[:, :, :].rearrange("p t e -> p (t e)"), ALU.is_le,
                                           ALU.mult).then_inc(kept_ready, 1)
            for g in range(G):
                dve.wait_ge(keptTb_ready, g + 1)
                nc.vector.tensor_copy(keptT[:, g * GT:(g + 1) * GT], ps[0:E, g, :]).then_inc(keptT_ready, 1)

            def select_tokens(i):
                g, e = divmod(i, E)
                dve.wait_ge(wide_filled, i + 1)
                if i >= 4:
                    dve.wait_ge(xm_used, i - 3)
                nc.vector.tensor_tensor(xm[:, i % 4, :], y1T[:, g * GT:(g + 1) * GT], ps[:, 4 + i % 4, :],
                                        ALU.mult).then_inc(xm_ready, 1)

            def finish_sum(g):
                dve.wait_ge(xm_used, (g + 1) * E)
                if g == 0:
                    dve.wait_ge(y1_ready, G)
                    settle()
                for t in tiles(g):
                    ins = nc.vector.scalar_tensor_tensor(xr[:, t, :], ps[:, g, t % TG * P:(t % TG + 1) * P],
                                                         gate[:, t:t + 1], y1[:, t, :], ALU.mult, ALU.add)
                mark(ins)
                settle()
                statistics(LN2, g, xr)

            def finish(g):
                dve.wait_ge(rstd_ready, LN2 * G + g + 1)
                for t in tiles(g):
                    ins = nc.vector.tensor_scalar(hat[:, t, :], xr[:, t, :], mv[:, t, 0:1], rstd[:, t:t + 1],
                                                  ALU.subtract, ALU.mult)
                mark(ins)
                settle()
                mark(nc.vector.tensor_tensor(hat[:, grp(g), :], hat[:, grp(g), :], spread(l2gb[:, :], TG), ALU.mult))
                settle()
                if g == 0:
                    dve.wait_ge(xf_ready, G)
                nc.vector.tensor_tensor(res[:, grp(g), :], hat[:, grp(g), :], xf[:, grp(g), :],
                                        ALU.add).then_inc(res_ready, 1)

            for g in range(G):
                for e in range(E):
                    select_tokens(g * E + e)
                    if g > 0 and e == 3:
                        finish_sum(g - 1)
                    if g > 0 and e == 5:
                        finish(g - 1)
            finish_sum(G - 1)
            finish(G - 1)


_ORDER = ["x", "ctx_1024", "mask_Bx1xS2_ik1", "g_xattn", "g_ffn",
          "L0_ffn_U1", "L0_ffn_V1", "L0_ffn_b1", "L0_ffn_U2", "L0_ffn_V2", "L0_ffn_b2",
          "L1_xattn_Wq", "L1_xattn_bq", "L1_xattn_Wk", "L1_xattn_bk", "L1_xattn_Wv", "L1_xattn_bv",
          "L1_xattn_Wo", "L1_xattn_bo",
          "L1_ffn_in_proj_w", "L1_ffn_in_proj_b", "L1_ffn_out_proj_w", "L1_ffn_out_proj_b",
          "L1_ffn_ln1_g", "L1_ffn_ln1_b", "L1_ffn_ln2_g", "L1_ffn_ln2_b",
          "L1_ffn_wg", "L1_ffn_w1", "L1_ffn_b1", "L1_ffn_w2", "L1_ffn_b2"]


def kernel(**inputs):
    import numpy as np
    import concourse.bacc as bacc
    from concourse.bass_utils import run_bass_kernel_spmd

    nc = bacc.Bacc("TRN2", target_bir_lowering=False, num_devices=1)
    arrays, args = {}, []
    for name in _ORDER:
        a = np.ascontiguousarray(inputs[name])
        arrays[f"in_{name}"] = a
        args.append(nc.dram_tensor(f"in_{name}", a.shape, mybir.dt.from_np(a.dtype), kind="ExternalInput").ap())
    args.append(nc.dram_tensor("out", (NB, NS, D), F32, kind="ExternalOutput").ap())
    program(nc, *args)
    r = run_bass_kernel_spmd(nc, [arrays], core_ids=[0])
    return r.results[0]["out"]
```

```python
from contextlib import ExitStack

import concourse.bass as bass
from concourse import mybir

F32 = mybir.dt.float32
BF16 = mybir.dt.bfloat16
I32 = mybir.dt.int32
ALU = mybir.AluOpType
ACT = mybir.ActivationFunctionType
AX_X = mybir.AxisListType.X

P = 128
D = 128
NB, NS = 32, 64
T = NB * NS // P
G = 4
TG = T // G
GT = TG * P
KEYS = 64
R = 32
FC = 4
H0 = 16
HD0 = D // H0
H1, HD1 = 4, 32
L, N = 32, 64
E = 8
CAP = NB * NS // E
EPS = 1e-5
SCALE_A = 1.0 / 16.0 ** 0.5
KEEP_A = 1.0 / (1.0 - 0.1 / (128 * 256))
SCALE_C = float(HD0) ** -0.5
SCALE_D = float(HD1) ** -0.5
MASKED = -1e30

A, B, C, SA, LN1, LN2 = range(6)

BQ, BK, BV, IPB, L1G, L1B, FB1, MB1 = 0, 1, 2, 3, 6, 7, 8, 12
NROWS = MB1 + E * FC

(J_CTX0, J_CTX1, J_W, J_CTX2, J_COL, J_KT0, J_VT0, J_CTX3, J_U2, J_U1, J_KT1, J_VT1, J_F1, J_F2,
 J_KT2, J_VT2, J_KT3, J_VT3, J_IP) = range(19)
J_CTX = (J_CTX0, J_CTX1, J_CTX2, J_CTX3)
J_KT = (J_KT0, J_KT1, J_KT2, J_KT3)
J_VT = (J_VT0, J_VT1, J_VT2, J_VT3)
J_W1 = J_IP + 1
J_WC = J_W1 + E
W1_ORDER = [4, 5, 6, 7, 0, 1, 2, 3]


def job_bank(j):
    if j >= J_WC:
        return 6 + j - J_WC
    return (4, 5, 7)[j % 3] if j < J_IP else 4 + j % 2


def job_before(j):
    return max(i + 1 for i in range(-1, j) if i < 0 or job_bank(i) == job_bank(j))


def program(nc, x, ctxt, mask, g_xattn, g_ffn, U1, V1, b1, U2, V2, b2,
            Wq, bq, Wk, bk, Wv, bv, Wo, bo,
            ipw, ipb, opw, opb, ln1g, ln1b, ln2g, ln2b, wg, w1, mb1, w2, mb2, out):
    with ExitStack() as ctx:
        def sb(name, shape, dt=F32):
            return ctx.enter_context(nc.sbuf_tensor(name, shape, dt))

        def sem(name):
            return ctx.enter_context(nc.semaphore(name))

        def row(v):
            return v.rearrange("(o n) -> o n", o=1)

        def spread(ap, k):
            return ap.unsqueeze(1).to_broadcast([P, k, ap.shape[1]])

        def along(ap, k):
            return ap.unsqueeze(len(ap.shape)).to_broadcast([*ap.shape, k])

        ps = ctx.enter_context(nc.psum_tensor("ps", [P, 8, 512], F32))

        x0, x1, x2, x3 = (sb(f"x{i}", [P, T, D]) for i in range(4))
        xb2 = x0
        xn = sb("xn", [P, T, D])
        xr = x2
        y1 = x0
        xf = x1
        res = xn
        xT = sb("xT", [P, T * P])
        stats = sb("stats", [P, T, 6])
        mv = sb("mv", [P, T, 2])
        veps = sb("veps", [P, T])
        rstd = sb("rstd", [P, T])
        mrstd = sb("mrstd", [P, T])
        nmr = sb("nmr", [P, T])
        minus_half = sb("minus_half", [P, TG])

        ctxv = sb("ctxv", [P, T, D])
        xnl = ctxv[:, :, :].rearrange("p t d -> p (t d)").rearrange("p (n l) -> p n l", l=L)
        hat = ctxv
        ctxT = sb("ctxT", [P, T * P])
        kmT = sb("kmT", [P, T * P])
        vmT = sb("vmT", [P, T * P])
        vo = sb("vo", [P, T, D])
        head_mask = sb("head_mask", [P, H0])
        bo16 = sb("bo16", [P, D])

        w_rows = sb("w_rows", [P, 4, D])
        wT = sb("wT", [P, 4, D])
        rows = sb("rows", [NROWS, D])
        col = sb("col", [P, NROWS])
        gates_in = sb("gates_in", [P, 4])
        gates = sb("gates", [P, 4])
        u1 = sb("u1", [P, R])
        v1 = sb("v1", [R, FC * P])
        u2 = sb("u2", [P, FC, R])
        v2 = sb("v2", [R, D])
        b2g = sb("b2g", [P, D])
        ip_rows = sb("ip_rows", [P, 4, D])
        ipT = sb("ipT", [P, 4, D])
        vbb = sb("vbb", [P, D])
        obb = sb("obb", [P, D])
        l1gb, l1bb, l2gb, l2bb = (sb(n, [P, D]) for n in ("l1gb", "l1bb", "l2gb", "l2bb"))
        wgs = sb("wgs", [P, E])
        w1s = sb("w1s", [P, E, FC * P])
        w2s = sb("w2s", [P, E, FC, D])
        w1T = sb("w1T", [P, E, FC, P])
        f1 = w1T[:, 0, :, :].rearrange("p c n -> p (c n)")
        f2 = w1T[:, 1, :, :]
        u2T = w1T[0:R, 2, :, :].rearrange("p c n -> p (c n)")
        u1T = w1T[0:R, 3, 0, :]
        wc = sb("wc", [P, E, D])
        b1z = sb("b1z", [P, FC, E * (E + 1)])
        mb2s = sb("mb2s", [E, D])
        c8 = sb("c8", [E, D])

        mx = sb("mx", [P, T, H0])
        negmax = sb("negmax", [P, T])
        ssum = sb("ssum", [P, T, H0])
        rsum = sb("rsum", [P, T, H0])
        fac = sb("fac", [P, T])
        prob = sb("prob", [P, T, KEYS])
        probT = sb("probT", [P, G, 2, P])
        hT = sb("hT", [P, FC, T * P])
        mrow = hT[0:1, 0, :].bitcast(I32)
        mbias = hT[0:1, 1, 0:NB * KEYS // 2].bitcast(BF16)
        qcT = ctxT
        qdT = hT[:, 0, :].rearrange("p (n l) -> p n l", l=L)
        kdT = hT[:, 1, :].rearrange("p (n l) -> p n l", l=L)
        vd = hT[:, 2, :].rearrange("p (t n) -> p t n", n=D)
        oT = hT[:, 3, :].rearrange("p (l n) -> p l n", n=N)
        pd = ctxT[:, 0:1024].rearrange("p (s h n) -> p s h n", s=2, h=H1)
        pdT = ctxT[:, 1024:2048].rearrange("p (s h n) -> p s h n", s=2, h=H1)
        mxd = sb("mxd", [P, H1 * TG])
        sumd = sb("sumd", [P, G, H1 * TG])
        rsd = sb("rsd", [P, G, H1 * TG])
        y1T = ctxT
        lsh, lexp, oh, ranked = (prob[:, 2 * i:2 * i + 2, :].rearrange("p a (b e) -> p (a b) e", e=E)
                                 for i in range(4))
        lmax = sb("lmax", [P, T])
        lsum = sb("lsum", [P, T])
        gate = sb("gate", [P, T])
        rank8 = sb("rank8", [P, E])
        best = sb("best", [P, T])
        chosen = sb("chosen", [P, T, E], BF16)
        kept = sb("kept", [P, T, E], BF16)
        keptT = kmT[0:E, :]
        keptTb = hT[0:E, 0, 0:T * P // 2].bitcast(BF16)
        xm = vmT[:, :].rearrange("p (i n) -> p i n", i=4)
        ident = sb("ident", [P, P])
        identb = sb("identb", [P, P], BF16)
        tri = sb("tri", [P, P], BF16)
        ones = sb("ones", [P, P], BF16)
        zeros = sb("zeros", [1, GT], BF16)
        pick = sb("pick", [E, E, P], BF16)

        ld_x = [sem(f"ld_x{g}") for g in range(G)]
        ld_ctx = [sem(f"ld_ctx{g}") for g in range(G)]
        ld_mask, ld_w, ld_rows, ld_gate, ld_bo = (sem(n) for n in ("ld_mask", "ld_w", "ld_rows", "ld_gate", "ld_bo"))
        ld_ffn, ld_b2, ld_ip, ld_bc, ld_moe = (sem(n) for n in ("ld_ffn", "ld_b2", "ld_ip", "ld_bc", "ld_moe"))
        ld_w1, ld_w2 = sem("ld_w1"), sem("ld_w2")
        stored = sem("stored")
        pool_own = sem("pool_own")
        ident_ready, moe_const = sem("ident_ready"), sem("moe_const")
        prep_filled, prep_taken, k_masked, v_masked, vo_ready, c8_ready, c8_filled = (
            sem(n) for n in ("prep_filled", "prep_taken", "k_masked", "v_masked", "vo_ready", "c8_ready", "c8_filled"))
        gates_ready, bo_ready = sem("gates_ready"), sem("bo_ready")
        mbias_ready = sem("mbias_ready")
        dve_own = sem("dve_own")
        stats_ready, rstd_ready, norm_ready = (
            [sem(f"{n}{s}") for s in range(6)] for n in ("stats_ready", "rstd_ready", "norm_ready"))
        xT_filled, xT_ready = ([sem(f"{n}{s}") for s in range(4)] for n in ("xT_filled", "xT_ready"))
        vo_filled = sem("vo_filled")
        score_filled, negmax_ready, prob_a, prob_c, shifted, exped = (
            sem(n) for n in ("score_filled", "negmax_ready", "prob_a", "prob_c", "shifted", "exped"))
        probT_filled, probT_ready, pv_filled, x1_ready, x3_ready = (
            sem(n) for n in ("probT_filled", "probT_ready", "pv_filled", "x1_ready", "x3_ready"))
        h_filled, h_ready, ffn_filled, xb2_ready = (
            sem(n) for n in ("h_filled", "h_ready", "ffn_filled", "xb2_ready"))
        qc_filled, qc_ready = sem("qc_filled"), sem("qc_ready")
        qd_filled, qd_ready, kd_filled, kd_ready, vd_filled, vd_ready = (
            sem(n) for n in ("qd_filled", "qd_ready", "kd_filled", "kd_ready", "vd_filled", "vd_ready"))
        sd_filled, sd_shifted, sd_exped, pdT_ready, od_filled, od_ready, op_filled, xr_ready = (
            sem(n) for n in ("sd_filled", "sd_shifted", "sd_exped", "pdT_ready", "od_filled", "od_ready",
                             "op_filled", "xr_ready"))
        hatT_filled, y1T_ready, y1_ready, lg_filled, lsh_ready, lexp_ready, chosen_ready, count_filled = (
            sem(n) for n in ("hatT_filled", "y1T_ready", "y1_ready", "lg_filled", "lsh_ready", "lexp_ready",
                             "chosen_ready", "count_filled"))
        b1z_cleared = sem("b1z_cleared")
        kept_ready, keptT_filled, keptTb_ready, keptT_ready = (
            sem(n) for n in ("kept_ready", "keptT_filled", "keptTb_ready", "keptT_ready"))
        wide_filled, xm_ready, xm_used, moe_filled, xf_ready, res_ready = (
            sem(n) for n in ("wide_filled", "xm_ready", "xm_used", "moe_filled", "xf_ready", "res_ready"))

        def tiles(g):
            return range(g * TG, (g + 1) * TG)

        def grp(g):
            return slice(g * TG, (g + 1) * TG)

        def key_cols(batch):
            c = (batch // 8 * TG + batch % 4) * P + batch % 8 // 4 * KEYS
            return slice(c, c + KEYS)

        def slot(t):
            return t // TG * TG + t % 2 * 2 + t % TG // 2

        block = ctx.enter_context(nc.Block())

        @block.sync
        def _(sp):
            xv = x.rearrange("(t b) s d -> (b s) t d", b=2)
            ov = out.rearrange("(t b) s d -> (b s) t d", b=2)
            cv = ctxt.rearrange("(g h j) s d -> g h s j d", h=2, j=TG)
            for g in range(G):
                sp.dma_start(x0[:, grp(g), :], xv[:, grp(g), :]).then_inc(ld_x[g], 16)
                for h in range(2):
                    sp.dma_start(ctxv[h * KEYS:(h + 1) * KEYS, grp(g), :], cv[g, h, :, :, :]).then_inc(ld_ctx[g], 16)
                if g == 0:
                    sp.dma_start(mrow[:, :], mask.rearrange("b o s -> o (b s)")).then_inc(ld_mask, 16)
            for i, w in enumerate((Wk, Wv, Wq, Wo)):
                sp.dma_start(w_rows[:, i, :], w).then_inc(ld_w, 16)
            for i, v in ((BQ, bq), (BK, bk), (BV, bv), (L1G, ln1g), (L1B, ln1b)):
                sp.dma_start(rows[i:i + 1, :], row(v)).then_inc(ld_rows, 16)
            sp.dma_start(rows[IPB:IPB + 3, :], ipb.rearrange("(i n) -> i n", n=D)).then_inc(ld_rows, 16)
            sp.dma_start(rows[FB1:FB1 + FC, :], b1.rearrange("(i n) -> i n", n=P)).then_inc(ld_rows, 16)
            sp.dma_start(rows[MB1:MB1 + E * FC, :], mb1.rearrange("e (c n) -> (e c) n", n=P)).then_inc(ld_rows, 16)
            sp.dma_start(gates_in[:, 0:2], row(g_xattn).to_broadcast([P, 2])).then_inc(ld_gate, 16)
            sp.dma_start(gates_in[:, 2:4], row(g_ffn).to_broadcast([P, 2])).then_inc(ld_gate, 16)
            sp.dma_start(u1[:, :], U1).then_inc(ld_ffn, 16)
            sp.dma_start(v1[:, :], V1).then_inc(ld_ffn, 16)
            sp.dma_start(u2[:, :, :], U2.rearrange("(c f) r -> f c r", f=P)).then_inc(ld_ffn, 16)
            sp.dma_start(v2[:, :], V2).then_inc(ld_ffn, 16)
            sp.dma_start(b2g[:, :], row(b2).to_broadcast([P, D])).then_inc(ld_b2, 16)
            sp.dma_start(bo16[:, :], row(bo).to_broadcast([P, D])).then_inc(ld_bo, 16)
            sp.dma_start(ip_rows[:, 0:3, :], ipw.rearrange("(i e) d -> e i d", i=3)).then_inc(ld_ip, 16)
            sp.dma_start(ip_rows[:, 3, :], opw).then_inc(ld_ip, 16)
            sp.dma_start(w1s[:, :, :], w1.rearrange("e d f -> d e f")).then_inc(ld_w1, 16)
            sp.dma_start(w2s[:, :, :, :], w2.rearrange("e (c f) d -> f e c d", f=P)).then_inc(ld_w2, 16)
            for dst, v in ((vbb, ipb[2 * D:3 * D]), (obb, opb), (l1gb, ln1g), (l1bb, ln1b), (l2gb, ln2g), (l2bb, ln2b)):
                sp.dma_start(dst[:, :], row(v).to_broadcast([P, D])).then_inc(ld_bc, 16)
            sp.dma_start(wgs[:, :], wg).then_inc(ld_moe, 16)
            sp.dma_start(mb2s[:, :], mb2).then_inc(ld_moe, 16)
            for g in range(G):
                sp.wait_ge(res_ready, g + 1)
                sp.dma_start(ov[:, grp(g), :], res[:, grp(g), :]).then_inc(stored, 16)
            sp.wait_ge(stored, 16 * G)

        (S_XA, S_SCORE_A, S_PT_A, S_PV_A, S_XB, S_HIDDEN, S_OUT_B, S_XC, S_Q, S_SCORE_C, S_PT_C, S_PV_C, S_XD,
         S_QK) = range(14)
        STEPS = G + S_QK

        def has(g):
            return 0 <= g < G

        @block.gpsimd
        def _(pool):
            own = [0]

            def after(ins):
                own[0] += 1
                ins.then_inc(pool_own, 1)
                pool.wait_ge(pool_own, own[0])

            nc.gpsimd.memset(minus_half[:, :], -0.5)
            after(nc.gpsimd.memset(ident[:, :], 0.0))
            nc.gpsimd.affine_select(out=ident[:, :], in_=ident[:, :], compare_op=ALU.not_equal, fill=1.0,
                                    base=0, pattern=[[-1, P]], channel_multiplier=1).then_inc(ident_ready, 1)
            nc.gpsimd.memset(ones[:, :], 1.0).then_inc(ident_ready, 1)

            def rsqrt(s, g):
                pool.wait_ge(stats_ready[s], g + 1)
                nc.gpsimd.tensor_tensor(rstd[:, grp(g)], veps[:, grp(g)], minus_half[:, :],
                                        ALU.pow).then_inc(rstd_ready[s], 1)

            def rsqrt_shift(s, g):
                pool.wait_ge(stats_ready[s], g + 1)
                after(nc.gpsimd.tensor_tensor(rstd[:, grp(g)], veps[:, grp(g)], minus_half[:, :], ALU.pow))
                after(nc.gpsimd.tensor_tensor(mrstd[:, grp(g)], mv[:, grp(g), 0], rstd[:, grp(g)], ALU.mult))
                nc.gpsimd.tensor_scalar(nmr[:, grp(g)], mrstd[:, grp(g)], -1.0, None, ALU.mult).then_inc(rstd_ready[s], 1)

            def mask_heads(buf, jobs, g):
                pool.wait_ge(prep_taken, jobs[g] + 1)
                v = buf[:, g * GT:(g + 1) * GT].rearrange("p (r h) -> p r h", h=H0)
                nc.gpsimd.tensor_tensor(v, v, spread(head_mask[:, :], GT // H0), ALU.mult).then_inc(
                    v_masked if jobs is J_VT else k_masked, 1)

            def add_b2(g):
                pool.wait_ge(x1_ready, g + 1)
                nc.gpsimd.tensor_tensor(xb2[:, grp(g), :], x1[:, grp(g), :], spread(b2g[:, :], TG),
                                        ALU.add).then_inc(xb2_ready, 1)

            def final_base(g):
                pool.wait_ge(x3_ready, g + 1)
                nc.gpsimd.tensor_tensor(xf[:, grp(g), :], x3[:, grp(g), :], spread(l2bb[:, :], TG),
                                        ALU.add).then_inc(xf_ready, 1)

            def self_base(g):
                pool.wait_ge(norm_ready[SA], g + 1)
                nc.gpsimd.tensor_tensor(xr[:, grp(g), :], xn[:, grp(g), :], spread(obb[:, :], TG),
                                        ALU.add).then_inc(xr_ready, 1)

            for g in range(G):
                rsqrt(A, g)
            nc.gpsimd.memset(b1z[:, :, :], 0.0).then_inc(b1z_cleared, 1)
            after(nc.gpsimd.memset(head_mask[:, :], 1.0))
            after(nc.gpsimd.affine_select(out=head_mask[:, :], in_=head_mask[:, :], compare_op=ALU.is_ge, fill=0.0,
                                          base=0, pattern=[[-HD0, H0]], channel_multiplier=1))
            after(nc.gpsimd.affine_select(out=head_mask[:, :], in_=head_mask[:, :], compare_op=ALU.is_ge, fill=0.0,
                                          base=HD0 - 1, pattern=[[HD0, H0]], channel_multiplier=-1))
            pool.wait_ge(ld_bo, 16)
            nc.gpsimd.tensor_scalar(bo16[:, :], bo16[:, :], 1.0 / H0, None, ALU.mult).then_inc(bo_ready, 1)
            for s in range(STEPS):
                if has(s - S_PV_C):
                    rsqrt(SA, s - S_PV_C)
                if has(s - S_OUT_B):
                    rsqrt(C, s - S_OUT_B)
                if has(s - S_PV_A):
                    rsqrt(B, s - S_PV_A)
                if has(s - S_PV_A):
                    mask_heads(vmT, J_VT, s - S_PV_A)
                if s == S_PV_A:
                    pool.wait_ge(gates_ready, 1)
                    pool.wait_ge(ld_b2, 16)
                    after(nc.gpsimd.tensor_scalar(b2g[:, :], b2g[:, :], gates[:, 2:3], None, ALU.mult))
                if has(s - S_XB):
                    add_b2(s - S_XB)
                if has(s - S_HIDDEN):
                    mask_heads(kmT, J_KT, s - S_HIDDEN)
                if s == S_XC + 2:
                    pool.wait_ge(ld_bc, 16 * 6)
                    nc.gpsimd.tensor_scalar(l2gb[:, :], l2gb[:, :], gates[:, 3:4], None, ALU.mult).then_inc(moe_const, 1)
                    after(nc.gpsimd.tensor_scalar(l2bb[:, :], l2bb[:, :], gates[:, 3:4], None, ALU.mult))
                if has(s - S_PV_C):
                    final_base(s - S_PV_C)
                if has(s - S_XD):
                    self_base(s - S_XD)
            nc.gpsimd.memset(zeros[:, :], 0.0).then_inc(moe_const, 1)
            nc.gpsimd.tensor_copy(identb[:, :], ident[:, :]).then_inc(moe_const, 1)
            nc.gpsimd.affine_select(out=tri[:, :], in_=ones[:, :], compare_op=ALU.is_ge, fill=0.0, base=0,
                                    pattern=[[1, P]], channel_multiplier=-1).then_inc(moe_const, 1)
            after(nc.gpsimd.memset(pick[:, :, :], 0.0))
            nc.gpsimd.affine_select(out=pick[:, :, :], in_=pick[:, :, :], compare_op=ALU.not_equal, fill=1.0,
                                    base=0, pattern=[[-1, E], [0, P]], channel_multiplier=1).then_inc(moe_const, 1)
            nc.gpsimd.iota(rank8[:, :], pattern=[[-1, E]], base=E, channel_multiplier=0,
                           allow_small_or_imprecise_dtypes=True).then_inc(moe_const, 1)
            for g in range(G):
                rsqrt(LN1, g)
            for g in range(G):
                pool.wait_ge(norm_ready[LN1], g + 1)
                after(nc.gpsimd.tensor_tensor(y1[:, grp(g), :], hat[:, grp(g), :], spread(l1gb[:, :], TG), ALU.mult))
                nc.gpsimd.tensor_tensor(y1[:, grp(g), :], y1[:, grp(g), :], spread(l1bb[:, :], TG),
                                        ALU.add).then_inc(y1_ready, 1)
            pool.wait_ge(moe_const, 6)
            for g in range(G):
                pool.wait_ge(keptTb_ready, g + 1)
                nc.gpsimd.tensor_copy(keptT[:, g * GT:(g + 1) * GT], keptTb[:, g * GT:(g + 1) * GT]).then_inc(keptT_ready, 1)
            for g in range(G):
                if g == G - 1:
                    rsqrt(LN2, g)
                else:
                    rsqrt_shift(LN2, g)
                    pool.wait_ge(norm_ready[LN2], g + 1)
                    after(nc.gpsimd.tensor_tensor(hat[:, grp(g), :], hat[:, grp(g), :], spread(l2gb[:, :], TG), ALU.mult))
                    nc.gpsimd.tensor_tensor(res[:, grp(g), :], hat[:, grp(g), :], xf[:, grp(g), :],
                                            ALU.add).then_inc(res_ready, 1)

        @block.scalar
        def _(act):
            def take(j, dst, src, **kw):
                act.wait_ge(prep_filled, j + 1)
                fn = ACT.Identity if kw else ACT.Copy
                nc.scalar.activation(dst, src, fn, **kw).then_inc(prep_taken, 1)

            def job(j):
                return ps[:, job_bank(j), :]

            def take_w1(i):
                take(J_W1 + i, w1T[:, W1_ORDER[i], :, :], job(J_W1 + i).rearrange("p (c n) -> p c n", c=FC))

            def take_wc(i):
                e = 4 * (1 - i)
                take(J_WC + i, wc[:, e:e + 4, :], job(J_WC + i).rearrange("p (e n) -> p e n", e=4))

            def take_kt(g):
                take(J_KT[g], kmT[:, g * GT:(g + 1) * GT], job(J_KT[g]), bias=col[:, BK:BK + 1], scale=1.0)

            def take_vt(g):
                take(J_VT[g], vmT[:, g * GT:(g + 1) * GT], job(J_VT[g]), bias=col[:, BV:BV + 1], scale=1.0)

            def normalise(s, g, src, dst):
                act.wait_ge(rstd_ready[s], g + 1)
                for t in tiles(g):
                    ins = nc.scalar.activation(dst[:, t, :], src[:, t, :], ACT.Identity,
                                               bias=nmr[:, t:t + 1], scale=rstd[:, t:t + 1])
                ins.then_inc(norm_ready[s], 1)

            def take_xT(s, g):
                act.wait_ge(xT_filled[s], g + 1)
                nc.scalar.activation(xT[:, g * GT:(g + 1) * GT], ps[:, g, :], ACT.Copy).then_inc(xT_ready[s], 1)

            def take_xT_by_n(g):
                act.wait_ge(xT_filled[SA], g + 1)
                nc.scalar.activation(xnl[:, :, 8 * g:8 * g + 8].rearrange("p n l -> p l n"),
                                     ps[:, g, :].rearrange("p (l n) -> p l n", n=N), ACT.Copy).then_inc(xT_ready[SA], 1)

            def take_probT(k, g):
                act.wait_ge(probT_filled, k * G + g + 1)
                nc.scalar.activation(probT[:, g, :, :], ps[:, g, 0:2 * P].rearrange("p (i q) -> p i q", i=2),
                                     ACT.Copy).then_inc(probT_ready, 1)

            def gelu(g, c):
                act.wait_ge(h_filled, g * FC + c + 1)
                nc.scalar.activation(hT[:, c, g * GT:(g + 1) * GT], ps[:, 4 + c % 2, :], ACT.Gelu_apprx_tanh,
                                     bias=col[:, FB1 + c:FB1 + c + 1], scale=1.0).then_inc(h_ready, 1)

            def exp_a(g):
                act.wait_ge(negmax_ready, g + 1)
                for i in range(TG):
                    q = g * TG + i
                    ins = nc.scalar.activation(prob[:, q, :], ps[:, g, i * KEYS:(i + 1) * KEYS], ACT.Exp,
                                               bias=negmax[:, q:q + 1], scale=SCALE_A, accum_out=ssum[:, q, 0:1])
                ins.then_inc(prob_a, 1)

            def exp_c(g):
                act.wait_ge(shifted, g + 1)
                v = prob[:, grp(g), :]
                nc.scalar.activation(v, v, ACT.Exp, scale=SCALE_C).then_inc(exped, 1)

            def take_proj(filled, done, g, bank, dst, which):
                act.wait_ge(filled, g + 1)
                nc.scalar.activation(dst[:, :, 8 * g:8 * g + 8], ps[:, bank, :].rearrange("p (n l) -> p n l", n=N),
                                     ACT.Identity, bias=col[:, IPB + which:IPB + which + 1], scale=1.0).then_inc(done, 1)

            def take_heads(g):
                act.wait_ge(od_filled, g + 1)
                for k in range(4):
                    ins = nc.scalar.activation(
                        oT[:, :, 16 * g:16 * g + 16].rearrange("p l (q k) -> p k q l", k=4)[:, k],
                        ps[:, 4 + k, 0:P].rearrange("p (q l) -> p q l", q=TG), ACT.Copy)
                ins.then_inc(od_ready, 1)

            def take_hatT(g):
                act.wait_ge(hatT_filled, g + 1)
                nc.scalar.activation(y1T[:, g * GT:(g + 1) * GT], ps[:, g, :], ACT.Identity,
                                     bias=col[:, L1B:L1B + 1], scale=col[:, L1G:L1G + 1]).then_inc(y1T_ready, 1)

            for s in range(STEPS):
                if has(s - S_QK):
                    take_proj(qd_filled, qd_ready, s - S_QK, s - S_QK, qdT, 0)
                    take_proj(kd_filled, kd_ready, s - S_QK, 7, kdT, 1)
                if has(s - S_XD):
                    take_xT_by_n(s - S_XD)
                if has(s - S_PT_C):
                    take_probT(1, s - S_PT_C)
                if has(s - S_Q):
                    g = s - S_Q
                    act.wait_ge(qc_filled, g + 1)
                    nc.scalar.activation(qcT[:, g * GT:(g + 1) * GT], ps[:, g, :], ACT.Identity,
                                         bias=col[:, BQ:BQ + 1], scale=1.0).then_inc(qc_ready, 1)
                if has(s - S_SCORE_C):
                    exp_c(s - S_SCORE_C)
                if has(s - S_XC):
                    take_xT(C, s - S_XC)
                if has(s - S_HIDDEN):
                    for c in range(FC):
                        gelu(s - S_HIDDEN, c)
                if has(s - S_XB):
                    take_xT(B, s - S_XB)
                if has(s - S_PT_A):
                    take_probT(0, s - S_PT_A)
                if has(s):
                    take(J_CTX[s], ctxT[:, s * GT:(s + 1) * GT], job(J_CTX[s]))
                    take_xT(A, s)
                if has(s - S_SCORE_A):
                    exp_a(s - S_SCORE_A)
                if s == 1:
                    take(J_W, wT[:, :, :], job(J_W).rearrange("p (i n) -> p i n", i=4))
                if s == 2:
                    act.wait_ge(prep_filled, J_COL + 1)
                    act.wait_ge(b1z_cleared, 1)
                    nc.scalar.activation(b1z[:, :, :].rearrange("p c (e k) -> p e c k", k=E + 1)[:, :, :, 0],
                                         job(J_COL)[:, MB1:MB1 + E * FC].rearrange("p (e c) -> p e c", c=FC), ACT.Copy)
                    take(J_COL, col[:, :], job(J_COL)[:, 0:NROWS])
                    act.wait_ge(ld_gate, 32)
                    nc.scalar.activation(gates[:, :], gates_in[:, :], ACT.Tanh).then_inc(gates_ready, 1)
                    act.wait_ge(prep_taken, J_COL + 1)
                    take_kt(0)
                    take_vt(0)
                if s == 3:
                    take(J_U2, u2T, job(J_U2)[0:R, :])
                    take(J_U1, u1T, job(J_U1)[0:R, 0:P])
                    take_kt(1)
                    take_vt(1)
                if s == 4:
                    take(J_F1, f1, job(J_F1))
                    take(J_F2, f2, job(J_F2).rearrange("p (c n) -> p c n", c=FC))
                    for g in (2, 3):
                        take_kt(g)
                        take_vt(g)
                if s == S_HIDDEN + G:
                    take(J_IP, ipT[:, :, :], job(J_IP).rearrange("p (i n) -> p i n", i=4))
                if S_OUT_B + G <= s < S_OUT_B + G + 4:
                    take_w1(2 * (s - S_OUT_B - G))
                    take_w1(2 * (s - S_OUT_B - G) + 1)
            for g in range(G):
                act.wait_ge(sd_shifted, g + 1)
                v = pd[:, g % 2, :, :]
                nc.scalar.activation(v, v, ACT.Exp, scale=SCALE_D).then_inc(sd_exped, 1)
                if g > 0:
                    take_heads(g - 1)
            take_heads(G - 1)
            for g in range(G):
                take_hatT(g)
                if g < 2:
                    take_wc(g)
            act.wait_ge(lsh_ready, 1)
            nc.scalar.activation(lexp[:, :, :], lsh[:, :, :], ACT.Exp).then_inc(lexp_ready, 1)
            for g in range(G):
                act.wait_ge(keptT_filled, g + 1)
                nc.scalar.activation(keptTb[:, g * GT:(g + 1) * GT], ps[0:E, g, :], ACT.Copy).then_inc(keptTb_ready, 1)
            for g in range(G - 1):
                normalise(LN2, g, xr, hat)

        @block.tensor
        def _(pe):
            def mm(o, lhsT, rhs, start=True, stop=True):
                return nc.tensor.matmul(o, lhsT, rhs, start=start, stop=stop)

            def job(j):
                if job_before(j):
                    pe.wait_ge(prep_taken, job_before(j))
                return ps[:, job_bank(j), :]

            def transpose4(dst, src):
                for i in range(4):
                    ins = nc.tensor.transpose(dst[:, i * P:(i + 1) * P], src(i), ident[:, :])
                return ins

            def x_transposes(s, g):
                pe.wait_ge(norm_ready[s], g + 1)
                transpose4(ps[:, g, :], lambda i: xn[:, g * TG + i, :]).then_inc(xT_filled[s], 1)

            def prob_transposes(k, g):
                pe.wait_ge(prob_a if k == 0 else prob_c, g + 1)
                for i in range(2):
                    q = g * TG + 2 * i
                    ins = nc.tensor.transpose(ps[:, g, i * P:(i + 1) * P],
                                              prob[:, q:q + 2, :].rearrange("p t k -> p (t k)"), ident[:, :])
                ins.then_inc(probT_filled, 1)

            def prob_values(k, g, values):
                pe.wait_ge(probT_ready, k * G + g + 1)
                for t in tiles(g):
                    i, half = t % 2, t % TG // 2
                    for b in range(2):
                        j = g * TG + (2 * (t % TG) + b) % TG
                        ins = mm(ps[64 * b:64 * b + 64, 6 if half else g, i * P:(i + 1) * P],
                                 probT[64 * half:64 * half + 64, g, i, 64 * b:64 * b + 64],
                                 values[64 * half:64 * half + 64, j, :])
                ins.then_inc(pv_filled, 1)

            def w1_job(i):
                transpose4(job(J_W1 + i), lambda c: w1s[:, W1_ORDER[i], c * P:(c + 1) * P]).then_inc(prep_filled, 1)

            def wc_job(j):
                o = job(J_WC + j)
                pe.wait_ge(prep_taken, J_W1 + 4 * (j + 1))
                for i in range(4):
                    e = 4 * (1 - j) + i
                    for c in range(FC):
                        ins = mm(o[:, i * P:(i + 1) * P], w1T[:, e, c, :], w2s[:, e, c, :],
                                 start=(c == 0), stop=(c == FC - 1))
                ins.then_inc(prep_filled, 1)

            def kt_job(g):
                mm(job(J_KT[g]), wT[:, 0, :], ctxT[:, g * GT:(g + 1) * GT]).then_inc(prep_filled, 1)

            def vt_job(g):
                mm(job(J_VT[g]), wT[:, 1, :], ctxT[:, g * GT:(g + 1) * GT]).then_inc(prep_filled, 1)

            def scores_a(g):
                pe.wait_ge(mbias_ready, g + 1)
                pe.wait_ge(xT_ready[A], g + 1)
                for b in range(2):
                    mm(ps[64 * b:64 * b + 64, g, 0:TG * KEYS], ones[0:1, 0:64],
                       mbias[0:1, (2 * g + b) * TG * KEYS:(2 * g + b + 1) * TG * KEYS], stop=False)
                for t in tiles(g):
                    for b in range(2):
                        c = slot(t) % TG * KEYS
                        ins = mm(ps[64 * b:64 * b + 64, g, c:c + KEYS], xT[:, t * P + 64 * b:t * P + 64 * b + 64],
                                 ctxT[:, key_cols(2 * t + b)], start=False, stop=(t % TG == TG - 1))
                ins.then_inc(score_filled, 1)

            def scores_c(g):
                pe.wait_ge(qc_ready, g + 1)
                pe.wait_ge(k_masked, g + 1)
                for t in tiles(g):
                    for b in range(2):
                        c = slot(t) % TG * KEYS
                        ins = mm(ps[64 * b:64 * b + 64, g, c:c + KEYS],
                                 qcT[:, t * P + 64 * b:t * P + 64 * b + 64], kmT[:, key_cols(2 * t + b)])
                ins.then_inc(score_filled, 1)

            def values_out(g):
                pe.wait_ge(v_masked, g + 1)
                if g == 0:
                    pe.wait_ge(prep_taken, J_IP)
                else:
                    pe.wait_ge(vo_ready, g)
                for i in range(TG):
                    c = (g * TG + i) * P
                    ins = mm(ps[:, 7, i * P:(i + 1) * P], vmT[:, c:c + P], wT[:, 3, :])
                ins.then_inc(vo_filled, 1)

            def hidden(g, c):
                if g == 0 and c < 2:
                    pe.wait_ge(prep_taken, J_IP)
                else:
                    pe.wait_ge(h_ready, g * FC + c - 1)
                mm(ps[:, 4 + c % 2, :], f1[:, c * P:(c + 1) * P], xT[:, g * GT:(g + 1) * GT]).then_inc(h_filled, 1)

            def ffn_out(g):
                pe.wait_ge(h_ready, (g + 1) * FC)
                for i in range(TG):
                    t = g * TG + i
                    for c in range(FC):
                        ins = mm(ps[:, g, i * P:(i + 1) * P], hT[:, c, t * P:(t + 1) * P], f2[:, c, :],
                                 start=(c == 0), stop=(c == FC - 1))
                ins.then_inc(ffn_filled, 1)

            pe.wait_ge(ident_ready, 2)
            for s in range(STEPS):
                if has(s - S_QK):
                    g = s - S_QK
                    pe.wait_ge(xT_ready[SA], g + 1)
                    mm(ps[:, g, :], ipT[:, 0, :], xnl[:, :, 8 * g:8 * g + 8]).then_inc(qd_filled, 1)
                    if g == 0:
                        pe.wait_ge(vo_ready, G)
                    else:
                        pe.wait_ge(kd_ready, g)
                    mm(ps[:, 7, :], ipT[:, 1, :], xnl[:, :, 8 * g:8 * g + 8]).then_inc(kd_filled, 1)
                if has(s - S_PV_C):
                    g = s - S_PV_C
                    if g == 0:
                        pe.wait_ge(vo_ready, G)
                        pe.wait_ge(x1_ready, G)
                    else:
                        pe.wait_ge(x3_ready, g)
                    prob_values(1, g, vo)
                if has(s - S_PT_C):
                    prob_transposes(1, s - S_PT_C)
                if has(s - S_SCORE_C):
                    scores_c(s - S_SCORE_C)
                if has(s - S_Q):
                    g = s - S_Q
                    pe.wait_ge(xT_ready[C], g + 1)
                    mm(ps[:, g, :], wT[:, 2, :], xT[:, g * GT:(g + 1) * GT]).then_inc(qc_filled, 1)
                if has(s - S_XC):
                    x_transposes(C, s - S_XC)
                if has(s - S_OUT_B):
                    ffn_out(s - S_OUT_B)
                if has(s - S_HIDDEN):
                    g = s - S_HIDDEN
                    pe.wait_ge(xT_ready[B], g + 1)
                    for c in range(FC):
                        hidden(g, c)
                    values_out(g)
                if has(s - S_XB):
                    x_transposes(B, s - S_XB)
                if has(s - S_PV_A):
                    g = s - S_PV_A
                    if g > 0:
                        pe.wait_ge(x1_ready, g)
                    prob_values(0, g, ctxv)
                if has(s - S_PT_A):
                    prob_transposes(0, s - S_PT_A)
                if has(s - S_SCORE_A):
                    scores_a(s - S_SCORE_A)
                if has(s):
                    pe.wait_ge(ld_ctx[s], 32)
                    transpose4(job(J_CTX[s]), lambda i: ctxv[:, s * TG + i, :]).then_inc(prep_filled, 1)
                    x_transposes(A, s)
                if s == 1:
                    pe.wait_ge(ld_w, 16 * 4)
                    transpose4(job(J_W), lambda i: w_rows[:, i, :]).then_inc(prep_filled, 1)
                if s == 2:
                    pe.wait_ge(ld_rows, 16 * 8)
                    nc.tensor.transpose(job(J_COL)[:, 0:NROWS], rows[:, :], ident[0:NROWS, 0:NROWS]).then_inc(prep_filled, 1)
                    pe.wait_ge(prep_taken, J_W + 1)
                    kt_job(0)
                    vt_job(0)
                if s == 3:
                    pe.wait_ge(ld_ffn, 16 * 4)
                    o = job(J_U2)
                    for c in range(FC):
                        ins = nc.tensor.transpose(o[0:R, c * P:(c + 1) * P], u2[:, c, :], ident[:, :])
                    ins.then_inc(prep_filled, 1)
                    nc.tensor.transpose(job(J_U1)[0:R, 0:P], u1[:, :], ident[:, :]).then_inc(prep_filled, 1)
                    kt_job(1)
                    vt_job(1)
                if s == 4:
                    o = job(J_F1)
                    pe.wait_ge(prep_taken, J_U1 + 1)
                    mm(o, u1T, v1[:, :]).then_inc(prep_filled, 1)
                    o = job(J_F2)
                    for c in range(FC):
                        ins = mm(o[:, c * P:(c + 1) * P], u2T[:, c * P:(c + 1) * P], v2[:, :])
                    ins.then_inc(prep_filled, 1)
                    pe.wait_ge(prep_taken, J_CTX3 + 1)
                    for g in (2, 3):
                        kt_job(g)
                        vt_job(g)
                if s == S_HIDDEN + G:
                    pe.wait_ge(h_ready, G * FC)
                    pe.wait_ge(ld_ip, 16 * 2)
                    transpose4(job(J_IP), lambda i: ip_rows[:, i, :]).then_inc(prep_filled, 1)
                    pe.wait_ge(ld_w1, 16)
                if S_OUT_B + G <= s < S_OUT_B + G + 4:
                    w1_job(2 * (s - S_OUT_B - G))
                    w1_job(2 * (s - S_OUT_B - G) + 1)
                if has(s - S_XD):
                    x_transposes(SA, s - S_XD)
            pe.wait_ge(x3_ready, G)
            pe.wait_ge(kd_ready, G)
            pe.wait_ge(prep_taken, J_WC)
            for g in range(G):
                for i in range(TG):
                    q = g * TG + i
                    ins = mm(ps[:, 4 + g, i * P:(i + 1) * P], xnl[:, 4 * q:4 * q + 4, :].rearrange("p n l -> p (n l)"),
                             ipT[:, 2, :])
                ins.then_inc(vd_filled, 1)
            pe.wait_ge(kd_ready, G)

            def head_scores(g):
                if g >= 1:
                    pe.wait_ge(sd_shifted, g)
                for i in range(TG):
                    for k in range(4):
                        n = 4 * (g * TG + i) + k
                        for h in range(H1):
                            hs = slice(HD1 * h, HD1 * h + HD1)
                            ins = mm(ps[L * k:L * k + L, h, i * L:(i + 1) * L], qdT[hs, n, :], kdT[hs, n, :])
                ins.then_inc(sd_filled, 1)

            def head_values(g):
                pe.wait_ge(pdT_ready, g + 1)
                if g == 0:
                    pe.wait_ge(vd_ready, G)
                else:
                    pe.wait_ge(od_ready, g)
                for i in range(TG):
                    for h in range(H1):
                        for k in range(4):
                            ks = slice(L * k, L * k + L)
                            ins = mm(ps[HD1 * h:HD1 * h + HD1, 4 + k, i * L:(i + 1) * L],
                                     vd[ks, g * TG + i, HD1 * h:HD1 * h + HD1],
                                     pdT[ks, g % 2, h, i * L:(i + 1) * L])
                ins.then_inc(od_filled, 1)

            head_scores(0)
            for g in range(1, G):
                head_scores(g)
                head_values(g - 1)
            pe.wait_ge(sd_shifted, G)
            head_values(G - 1)
            pe.wait_ge(od_ready, G)
            flat = oT[:, :, :].rearrange("p l n -> p (l n)")
            for g in range(G):
                for i in range(TG):
                    t = g * TG + i
                    ins = mm(ps[:, g, i * P:(i + 1) * P], flat[:, t * P:(t + 1) * P], ipT[:, 3, :])
                ins.then_inc(op_filled, 1)
            pe.wait_ge(ld_moe, 16 * 2)
            pe.wait_ge(ld_w2, 16)

            def logits(g):
                pe.wait_ge(y1T_ready, g + 1)
                for t in tiles(g):
                    ins = mm(ps[:, 4, t * E:(t + 1) * E], y1T[:, t * P:(t + 1) * P], wgs[:, :])
                return ins

            def c8_terms(first, last):
                for i in range(first, last):
                    e, c = divmod(i, FC)
                    ins = mm(ps[0:E, 5, 0:P], b1z[:, c, e * E:(e + 1) * E], w2s[:, e, c, :],
                             start=(i == 0), stop=(i == E * FC - 1))
                if last == E * FC:
                    ins.then_inc(c8_filled, 1)

            pe.wait_ge(prep_taken, J_COL + 1)
            for g in range(G):
                if g < 2:
                    wc_job(g)
                pe.wait_ge(norm_ready[LN1], g + 1)
                transpose4(ps[:, g, :], lambda i: hat[:, g * TG + i, :]).then_inc(hatT_filled, 1)
                if g > 0:
                    logits(g - 1)
            c8_terms(0, 4)
            ins = logits(G - 1)
            ins.then_inc(lg_filled, 1)
            c8_terms(4, 12)
            pe.wait_ge(moe_const, 6)
            pe.wait_ge(chosen_ready, 1)
            mm(ps[:, 4, T * E:2 * T * E], tri[:, :], chosen[:, :, :].rearrange("p t e -> p (t e)"), stop=False)
            for t in range(T - 1):
                ins = mm(ps[:, 4, (T + t + 1) * E:2 * T * E], ones[:, :], spread(chosen[:, t, :], T - 1 - t),
                         start=False, stop=(t == T - 2))
            ins.then_inc(count_filled, 1)
            c8_terms(12, 16)
            pe.wait_ge(kept_ready, 1)
            for g in range(G):
                for i in range(TG):
                    ins = mm(ps[0:E, g, i * P:(i + 1) * P], kept[:, g * TG + i, :], identb[:, :])
                ins.then_inc(keptT_filled, 1)

            def widen(i):
                g, e = divmod(i, E)
                pe.wait_ge(keptTb_ready, g + 1)
                if i == 1:
                    pe.wait_ge(c8_ready, 1)
                if i >= 4:
                    pe.wait_ge(xm_ready, i - 3)
                mm(ps[:, 4 + i % 4, :], pick[:, e, :], keptTb[:, g * GT:(g + 1) * GT]).then_inc(wide_filled, 1)

            c8_terms(16, E * FC)
            for i in range(3):
                widen(i)
            for i in range(G * E):
                g, e = divmod(i, E)
                if i + 3 < G * E:
                    widen(i + 3)
                if e == 0:
                    mm(ps[:, g, :], zeros[0:1, 0:P], zeros[0:1, :], stop=False)
                if e == E - 1:
                    pe.wait_ge(keptT_ready, g + 1)
                    for t in range(TG):
                        mm(ps[:, g, t * P:(t + 1) * P], keptT[:, g * GT + t * P:g * GT + (t + 1) * P], c8[:, :],
                           start=False, stop=False)
                pe.wait_ge(xm_ready, i + 1)
                for t in range(TG):
                    ins = mm(ps[:, g, t * P:(t + 1) * P], xm[:, i % 4, t * P:(t + 1) * P], wc[:, e, :],
                             start=False, stop=(e == E - 1 and t == TG - 1))
                ins.then_inc(xm_used, 1)

        @block.vector
        def _(dve):
            own = [0]

            def mark(ins):
                own[0] += 1
                ins.then_inc(dve_own, 1)

            def settle():
                dve.wait_ge(dve_own, own[0])

            def statistics(s, g, src):
                for t in tiles(g):
                    ins = nc.vector.bn_stats(stats[:, t, :], src[:, t, :])
                mark(ins)
                settle()
                for t in tiles(g):
                    ins = nc.vector.bn_aggr(mv[:, t, :], stats[:, t, :])
                mark(ins)
                settle()
                nc.vector.tensor_scalar(veps[:, grp(g)], mv[:, grp(g), 1], EPS, None, ALU.add).then_inc(stats_ready[s], 1)

            def normalise(s, g, src, dst):
                dve.wait_ge(rstd_ready[s], g + 1)
                for t in tiles(g):
                    ins = nc.vector.tensor_scalar(dst[:, t, :], src[:, t, :], mv[:, t, 0:1], rstd[:, t:t + 1],
                                                  ALU.subtract, ALU.mult)
                ins.then_inc(norm_ready[s], 1)

            def by_slot(buf, g, half):
                return buf[:, g * TG + 2 * half:g * TG + 2 * half + 2, :]

            def mask_bias(g):
                for b in range(2):
                    m = mrow[:, 2 * g * TG * KEYS:2 * (g + 1) * TG * KEYS].rearrange(
                        "o (i j b k) -> o b j i k", i=2, j=2, b=2)
                    c = (2 * g + b) * TG * KEYS
                    ins = nc.vector.tensor_scalar(
                        mbias[:, c:c + TG * KEYS].rearrange("o (j i k) -> o j i k", j=2, i=2), m[:, b], 0.0, MASKED,
                        ALU.is_equal, ALU.mult)
                ins.then_inc(mbias_ready, 1)

            def row_maxima(g):
                dve.wait_ge(score_filled, g + 1)
                mark(nc.vector.tensor_reduce(mx[:, grp(g), 0], ps[:, g, 0:TG * KEYS].rearrange("p (t k) -> p t k", k=KEYS),
                                             axis=AX_X, op=ALU.max))
                settle()
                nc.vector.tensor_scalar(negmax[:, grp(g)], mx[:, grp(g), 0], -SCALE_A, None,
                                        ALU.mult).then_inc(negmax_ready, 1)

            def row_factors(g):
                if g == 0:
                    dve.wait_ge(gates_ready, 1)
                dve.wait_ge(prob_a, g + 1)
                mark(nc.vector.reciprocal(rsum[:, grp(g), 0], ssum[:, grp(g), 0]))
                settle()
                mark(nc.vector.tensor_scalar(fac[:, grp(g)], rsum[:, grp(g), 0], gates[:, 0:1], KEEP_A, ALU.mult, ALU.mult))

            def residual_a(g):
                dve.wait_ge(pv_filled, g + 1)
                settle()
                for t in tiles(g):
                    i, half = t % 2, t % TG // 2
                    q = slot(t)
                    ins = nc.vector.scalar_tensor_tensor(x1[:, t, :], ps[:, 6 if half else g, i * P:(i + 1) * P],
                                                         fac[:, q:q + 1], x0[:, t, :], ALU.mult, ALU.add)
                ins.then_inc(x1_ready, 1)
                dve.wait_ge(x1_ready, g + 1)
                statistics(B, g, x1)

            def take_vo(g):
                dve.wait_ge(vo_filled, g + 1)
                dve.wait_ge(bo_ready, 1)
                nc.vector.tensor_tensor(vo[:, grp(g), :], ps[:, 7, :].rearrange("p (t n) -> p t n", n=D),
                                        spread(bo16[:, :], TG), ALU.add).then_inc(vo_ready, 1)

            def residual_b(g):
                dve.wait_ge(ffn_filled, g + 1)
                dve.wait_ge(xb2_ready, g + 1)
                mark(nc.vector.scalar_tensor_tensor(x2[:, grp(g), :], ps[:, g, :].rearrange("p (t n) -> p t n", n=D),
                                                    gates[:, 2:3], xb2[:, grp(g), :], ALU.mult, ALU.add))
                settle()
                statistics(C, g, x2)

            def shift_scores(g):
                dve.wait_ge(score_filled, G + g + 1)
                s = ps[:, g, 0:TG * KEYS]
                mark(nc.vector.tensor_reduce(mx[:, grp(g), :], s.rearrange("p (t j h) -> p t h j", h=H0, j=KEYS // H0),
                                             axis=AX_X, op=ALU.max))
                settle()
                nc.vector.tensor_tensor(prob[:, grp(g), :].rearrange("p t (j h) -> p t j h", h=H0),
                                        s.rearrange("p (t j h) -> p t j h", h=H0, j=KEYS // H0),
                                        over_keys(mx[:, grp(g), :]), ALU.subtract).then_inc(shifted, 1)

            def over_keys(v):
                return v.unsqueeze(2).to_broadcast([P, TG, KEYS // H0, H0])

            def weigh_scores(g):
                dve.wait_ge(exped, g + 1)
                mark(nc.vector.tensor_reduce(ssum[:, grp(g), :], prob[:, grp(g), :].rearrange("p t (j h) -> p t h j", h=H0),
                                             axis=AX_X, op=ALU.add))
                settle()
                mark(nc.vector.reciprocal(rsum[:, grp(g), :], ssum[:, grp(g), :]))
                settle()
                v = prob[:, grp(g), :].rearrange("p t (j h) -> p t j h", h=H0)
                nc.vector.tensor_tensor(v, v, over_keys(rsum[:, grp(g), :]), ALU.mult).then_inc(prob_c, 1)

            def residual_c(g):
                dve.wait_ge(pv_filled, G + g + 1)
                for half in range(2):
                    ins = nc.vector.scalar_tensor_tensor(
                        by_slot(x3, g, half), ps[:, 6 if half else g, 0:2 * P].rearrange("p (i n) -> p i n", i=2),
                        gates[:, 1:2], by_slot(x2, g, half), ALU.mult, ALU.add)
                ins.then_inc(x3_ready, 1)
                dve.wait_ge(x3_ready, g + 1)
                statistics(SA, g, x3)

            dve.wait_ge(ld_x[0], 16)
            statistics(A, 0, x0)
            dve.wait_ge(ld_mask, 16)
            mask_bias(0)
            normalise(A, 0, x0, xn)
            for s in range(STEPS):
                if has(s - S_PV_C):
                    residual_c(s - S_PV_C)
                if has(s - S_SCORE_C):
                    shift_scores(s - S_SCORE_C)
                if has(s - S_PV_C):
                    normalise(SA, s - S_PV_C, x3, xn)
                if has(s - S_SCORE_C):
                    weigh_scores(s - S_SCORE_C)
                if has(s - S_OUT_B):
                    residual_b(s - S_OUT_B)
                    take_vo(s - S_OUT_B)
                    normalise(C, s - S_OUT_B, x2, xn)
                if has(s - S_PV_A):
                    row_factors(s - S_PV_A)
                    residual_a(s - S_PV_A)
                if has(s + 1):
                    dve.wait_ge(ld_x[s + 1], 16)
                    statistics(A, s + 1, x0)
                    mask_bias(s + 1)
                if has(s - S_SCORE_A):
                    row_maxima(s - S_SCORE_A)
                if has(s - S_PV_A):
                    normalise(B, s - S_PV_A, x1, xn)
                if has(s + 1):
                    normalise(A, s + 1, x0, xn)
            dve.wait_ge(ld_bc, 16 * 6)
            for g in range(G):
                dve.wait_ge(vd_filled, g + 1)
                nc.vector.tensor_tensor(vd[:, grp(g), :], ps[:, 4 + g, :].rearrange("p (i n) -> p i n", n=D),
                                        spread(vbb[:, :], TG), ALU.add).then_inc(vd_ready, 1)

            def shift_heads(g):
                dve.wait_ge(sd_filled, g + 1)
                s = ps[:, 0:H1, 0:P].rearrange("p h (i m) -> p h i m", m=L)
                mark(nc.vector.tensor_reduce(mxd[:, :].rearrange("p (h i) -> p h i", h=H1), s, axis=AX_X, op=ALU.max))
                settle()
                if g >= 2:
                    dve.wait_ge(pdT_ready, g - 1)
                nc.vector.tensor_tensor(pd[:, g % 2, :, :].rearrange("p h (i m) -> p h i m", m=L), s,
                                        along(mxd[:, :].rearrange("p (h i) -> p h i", h=H1), L),
                                        ALU.subtract).then_inc(sd_shifted, 1)

            def weigh_heads(g):
                dve.wait_ge(sd_exped, g + 1)
                v = pd[:, g % 2, :, :].rearrange("p h (i m) -> p (h i) m", m=L)
                mark(nc.vector.tensor_reduce(sumd[:, g, :], v, axis=AX_X, op=ALU.add))
                settle()
                mark(nc.vector.reciprocal(rsd[:, g, :], sumd[:, g, :]))
                settle()
                mark(nc.vector.tensor_tensor(v, v, along(rsd[:, g, :], L), ALU.mult))
                settle()
                if g >= 2:
                    dve.wait_ge(od_filled, g - 1)
                nc.vector.transpose(pdT[:, g % 2, :, :].rearrange("p h n -> p (h n)"),
                                    pd[:, g % 2, :, :].rearrange("p h n -> p (h n)")).then_inc(pdT_ready, 1)

            shift_heads(0)
            for g in range(1, G):
                weigh_heads(g - 1)
                shift_heads(g)
            weigh_heads(G - 1)
            for g in range(G):
                dve.wait_ge(op_filled, g + 1)
                dve.wait_ge(xr_ready, g + 1)
                mark(nc.vector.tensor_tensor(xr[:, grp(g), :], ps[:, g, :].rearrange("p (t n) -> p t n", n=D),
                                             xr[:, grp(g), :], ALU.add))
                settle()
                statistics(LN1, g, xr)
                if g > 0:
                    normalise(LN1, g - 1, xr, hat)
            normalise(LN1, G - 1, xr, hat)
            dve.wait_ge(lg_filled, 1)
            l8 = ps[:, 4, 0:T * E].rearrange("p (t e) -> p t e", e=E)
            mark(nc.vector.tensor_reduce(lmax[:, :], l8, axis=AX_X, op=ALU.max))
            settle()
            nc.vector.tensor_tensor(lsh[:, :, :], l8, along(lmax[:, :], E), ALU.subtract).then_inc(lsh_ready, 1)
            dve.wait_ge(moe_const, 6)
            dve.wait_ge(lsh_ready, 1)
            mark(nc.vector.scalar_tensor_tensor(ranked[:, :, :], lsh[:, :, :], 0.0, spread(rank8[:, :], T),
                                                ALU.is_equal, ALU.mult))
            settle()
            mark(nc.vector.tensor_reduce(best[:, :], ranked[:, :, :], axis=AX_X, op=ALU.max))
            settle()
            nc.vector.tensor_tensor(chosen[:, :, :], ranked[:, :, :], along(best[:, :], E),
                                    ALU.is_equal).then_inc(chosen_ready, 1)
            dve.wait_ge(lexp_ready, 1)
            mark(nc.vector.tensor_reduce(lsum[:, :], lexp[:, :, :], axis=AX_X, op=ALU.add))
            settle()
            mark(nc.vector.reciprocal(gate[:, :], lsum[:, :]))
            dve.wait_ge(count_filled, 1)
            dve.wait_ge(chosen_ready, 1)
            nc.vector.scalar_tensor_tensor(kept[:, :, :].rearrange("p t e -> p (t e)"), ps[:, 4, T * E:2 * T * E], float(CAP) + 0.5,
                                           chosen[:, :, :].rearrange("p t e -> p (t e)"), ALU.is_le,
                                           ALU.mult).then_inc(kept_ready, 1)
            dve.wait_ge(c8_filled, 1)
            dve.wait_ge(ld_moe, 16 * 2)
            nc.vector.tensor_tensor(c8[:, :], ps[0:E, 5, 0:P], mb2s[:, :], ALU.add).then_inc(c8_ready, 1)

            def select_tokens(i):
                g, e = divmod(i, E)
                dve.wait_ge(wide_filled, i + 1)
                if i >= 4:
                    dve.wait_ge(xm_used, i - 3)
                nc.vector.tensor_tensor(xm[:, i % 4, :], y1T[:, g * GT:(g + 1) * GT], ps[:, 4 + i % 4, :],
                                        ALU.mult).then_inc(xm_ready, 1)

            def finish_sum(g):
                dve.wait_ge(xm_used, (g + 1) * E)
                if g == 0:
                    dve.wait_ge(y1_ready, G)
                    settle()
                for t in tiles(g):
                    ins = nc.vector.scalar_tensor_tensor(xr[:, t, :], ps[:, g, t % TG * P:(t % TG + 1) * P],
                                                         gate[:, t:t + 1], y1[:, t, :], ALU.mult, ALU.add)
                mark(ins)
                settle()
                statistics(LN2, g, xr)

            for g in range(G):
                for e in range(E):
                    select_tokens(g * E + e)
                    if g > 0 and e == 3:
                        finish_sum(g - 1)
            g = G - 1
            finish_sum(g)
            dve.wait_ge(moe_const, 1)
            for t in tiles(g):
                ins = nc.vector.scalar_tensor_tensor(hat[:, t, :], xr[:, t, :], mv[:, t, 0:1], l2gb[:, :],
                                                     ALU.subtract, ALU.mult)
            mark(ins)
            settle()
            dve.wait_ge(rstd_ready[LN2], g + 1)
            dve.wait_ge(xf_ready, G)
            for t in tiles(g):
                ins = nc.vector.scalar_tensor_tensor(res[:, t, :], hat[:, t, :], rstd[:, t:t + 1], xf[:, t, :],
                                                     ALU.mult, ALU.add)
            ins.then_inc(res_ready, 1)


_ORDER = ["x", "ctx_1024", "mask_Bx1xS2_ik1", "g_xattn", "g_ffn",
          "L0_ffn_U1", "L0_ffn_V1", "L0_ffn_b1", "L0_ffn_U2", "L0_ffn_V2", "L0_ffn_b2",
          "L1_xattn_Wq", "L1_xattn_bq", "L1_xattn_Wk", "L1_xattn_bk", "L1_xattn_Wv", "L1_xattn_bv",
          "L1_xattn_Wo", "L1_xattn_bo",
          "L1_ffn_in_proj_w", "L1_ffn_in_proj_b", "L1_ffn_out_proj_w", "L1_ffn_out_proj_b",
          "L1_ffn_ln1_g", "L1_ffn_ln1_b", "L1_ffn_ln2_g", "L1_ffn_ln2_b",
          "L1_ffn_wg", "L1_ffn_w1", "L1_ffn_b1", "L1_ffn_w2", "L1_ffn_b2"]


def kernel(**inputs):
    import numpy as np
    import concourse.bacc as bacc
    from concourse.bass_utils import run_bass_kernel_spmd

    nc = bacc.Bacc("TRN2", target_bir_lowering=False, num_devices=1)
    arrays, args = {}, []
    for name in _ORDER:
        a = np.ascontiguousarray(inputs[name])
        arrays[f"in_{name}"] = a
        args.append(nc.dram_tensor(f"in_{name}", a.shape, mybir.dt.from_np(a.dtype), kind="ExternalInput").ap())
    args.append(nc.dram_tensor("out", (NB, NS, D), F32, kind="ExternalOutput").ap())
    program(nc, *args)
    r = run_bass_kernel_spmd(nc, [arrays], core_ids=[0])
    return r.results[0]["out"]
```

```python
from contextlib import ExitStack

import concourse.bass as bass
from concourse import mybir

F32 = mybir.dt.float32
BF16 = mybir.dt.bfloat16
I32 = mybir.dt.int32
I16 = mybir.dt.int16
ALU = mybir.AluOpType
ACT = mybir.ActivationFunctionType
AX_X = mybir.AxisListType.X

P = 128
D = 128
NB, NS = 32, 64
T = NB * NS // P
G = 4
TG = T // G
GT = TG * P
KEYS = 64
R = 32
FC = 4
H0 = 16
HD0 = D // H0
H1, HD1 = 4, 32
L, N = 32, 64
E = 8
CAP = NB * NS // E
EPS = 1e-5
SCALE_A = 1.0 / 16.0 ** 0.5
KEEP_A = 1.0 / (1.0 - 0.1 / (128 * 256))
SCALE_C = float(HD0) ** -0.5
SCALE_D = float(HD1) ** -0.5
MASKED = -1e30

A, B, C, SA, LN1, LN2 = range(6)

BQ, BK, BV, IPB, L1G, L1B, FB1, MB1 = 0, 1, 2, 3, 6, 7, 8, 12
NROWS = MB1 + E * FC

(J_CTX0, J_CTX1, J_W, J_CTX2, J_COL, J_KT0, J_VT0, J_CTX3, J_U2, J_U1, J_KT1, J_VT1, J_F1, J_F2,
 J_KT2, J_VT2, J_KT3, J_VT3, J_IP) = range(19)
J_CTX = (J_CTX0, J_CTX1, J_CTX2, J_CTX3)
J_KT = (J_KT0, J_KT1, J_KT2, J_KT3)
J_VT = (J_VT0, J_VT1, J_VT2, J_VT3)
J_W1 = J_IP + 1
J_WC = J_W1 + E
J_BACK = J_WC + 4
W1_ORDER = [4, 5, 6, 7, 0, 1, 2, 3]

RING = (6, 7, 0, 1, 2, 3)


def selected_by(g, e, half=1):
    return 2 * (g * (E - 1) + e - 1) + half + 1


def job_bank(j):
    if j >= J_WC + 3:
        return (7, 4, 6)[j - J_WC - 3]
    return (4, 5, 7)[j % 3] if j < J_IP else 4 + j % 2


def job_before(j):
    return max(i + 1 for i in range(-1, j) if i < 0 or job_bank(i) == job_bank(j))


def program(nc, x, ctxt, mask, g_xattn, g_ffn, U1, V1, b1, U2, V2, b2,
            Wq, bq, Wk, bk, Wv, bv, Wo, bo,
            ipw, ipb, opw, opb, ln1g, ln1b, ln2g, ln2b, wg, w1, mb1, w2, mb2, out):
    with ExitStack() as ctx:
        def sb(name, shape, dt=F32):
            return ctx.enter_context(nc.sbuf_tensor(name, shape, dt))

        def sem(name):
            return ctx.enter_context(nc.semaphore(name))

        def row(v):
            return v.rearrange("(o n) -> o n", o=1)

        def spread(ap, k):
            return ap.unsqueeze(1).to_broadcast([P, k, ap.shape[1]])

        def along(ap, k):
            return ap.unsqueeze(len(ap.shape)).to_broadcast([*ap.shape, k])

        ps = ctx.enter_context(nc.psum_tensor("ps", [P, 8, 512], F32))

        x0, x1, x2, x3 = (sb(f"x{i}", [P, T, D]) for i in range(4))
        xb2 = x0
        xn = sb("xn", [P, T, D])
        xr = x2
        y1 = x0
        xf = x1
        res = xn
        xT = sb("xT", [P, T * P])
        stats = sb("stats", [P, T, 6])
        mv = sb("mv", [P, T, 2])
        veps = sb("veps", [P, T])
        rstd = sb("rstd", [P, T])
        mrstd = sb("mrstd", [P, T])
        nmr = sb("nmr", [P, T])
        minus_half = sb("minus_half", [P, TG])

        ctxv = sb("ctxv", [P, T, D])
        xnl = ctxv[:, :, :].rearrange("p t d -> p (t d)").rearrange("p (n l) -> p n l", l=L)
        hat = ctxv
        ctxT = sb("ctxT", [P, T * P])
        kmT = sb("kmT", [P, T * P])
        vmT = sb("vmT", [P, T * P])
        vo = sb("vo", [P, T, D])
        head_mask = sb("head_mask", [P, H0])
        bo16 = sb("bo16", [P, D])

        w_rows = sb("w_rows", [P, 4, D])
        wT = sb("wT", [P, 4, D])
        rows = sb("rows", [NROWS, D])
        col = sb("col", [P, NROWS])
        gates_in = sb("gates_in", [P, 4])
        gates = sb("gates", [P, 4])
        u1 = sb("u1", [P, R])
        v1 = sb("v1", [R, FC * P])
        u2 = sb("u2", [P, FC, R])
        v2 = sb("v2", [R, D])
        b2g = sb("b2g", [P, D])
        ip_rows = sb("ip_rows", [P, 4, D])
        ipT = sb("ipT", [P, 4, D])
        vbb = sb("vbb", [P, D])
        obb = sb("obb", [P, D])
        l1gb, l1bb, l2gb, l2bb = (sb(n, [P, D]) for n in ("l1gb", "l1bb", "l2gb", "l2bb"))
        wgs = sb("wgs", [P, E])
        w1s = sb("w1s", [P, E, FC * P])
        w2s = sb("w2s", [P, E, FC, D])
        w1T = sb("w1T", [P, E, FC, P + 1])
        f1 = w1T[:, 0, :, :].rearrange("p c n -> p (c n)")[:, 0:FC * P]
        f2 = w1T[:, 1, :, 0:P]
        u2T = w1T[0:R, 2, :, :].rearrange("p c n -> p (c n)")[:, 0:FC * P]
        u1T = w1T[0:R, 3, 0, 0:P]
        wc = sb("wc", [P, E, D])
        wcT = vmT[:, 0:E * (P + 1)].rearrange("p (e n) -> p e n", e=E)
        mb2s = sb("mb2s", [E, D])
        c8 = sb("c8", [E, D])

        mx = sb("mx", [P, T, H0])
        negmax = sb("negmax", [P, T])
        ssum = sb("ssum", [P, T, H0])
        rsum = sb("rsum", [P, T, H0])
        fac = sb("fac", [P, T])
        prob = sb("prob", [P, T, KEYS])
        probT = sb("probT", [P, G, 2, P])
        hT = sb("hT", [P, FC, T * P])
        mrow = hT[0:1, 0, :].bitcast(I32)
        mbias = hT[0:1, 1, 0:NB * KEYS // 2].bitcast(BF16)
        qcT = ctxT
        qdT = hT[:, 0, :].rearrange("p (n l) -> p n l", l=L)
        kdT = hT[:, 1, :].rearrange("p (n l) -> p n l", l=L)
        vd = hT[:, 2, :].rearrange("p (t n) -> p t n", n=D)
        oT = hT[:, 3, :].rearrange("p (l n) -> p l n", n=N)
        pd = ctxT[:, 0:1024].rearrange("p (s h n) -> p s h n", s=2, h=H1)
        pdT = ctxT[:, 1024:2048].rearrange("p (s h n) -> p s h n", s=2, h=H1)
        mxd = sb("mxd", [P, H1 * TG])
        sumd = sb("sumd", [P, G, H1 * TG])
        rsd = sb("rsd", [P, G, H1 * TG])
        y1T = ctxT
        lsh, lexp, ranked = (prob[:, 2 * i:2 * i + 2, :].rearrange("p a (b e) -> p (a b) e", e=E)
                             for i in range(3))
        lmax = sb("lmax", [P, T])
        lsum = sb("lsum", [P, T])
        gate = sb("gate", [P, T])
        rank8 = sb("rank8", [P, E])
        best = sb("best", [P, T])
        chosen = sb("chosen", [P, T, E], BF16)
        kept = sb("kept", [P, T, E], BF16)
        kept0 = sb("kept0", [P, T])
        keptT = kmT[0:E, :]
        acc = vmT[:, :].rearrange("p (t n) -> p t n", n=D)
        gb = hT[:, 1, :].rearrange("p (t n) -> p t n", n=D)
        ident = sb("ident", [P, P])
        identb = sb("identb", [P, P], BF16)
        tri = sb("tri", [P, P], BF16)
        ones = sb("ones", [P, P], BF16)

        ld_x = [sem(f"ld_x{g}") for g in range(G)]
        ld_ctx = [sem(f"ld_ctx{g}") for g in range(G)]
        ld_mask, ld_w, ld_rows, ld_gate, ld_bo = (sem(n) for n in ("ld_mask", "ld_w", "ld_rows", "ld_gate", "ld_bo"))
        ld_ffn, ld_b2, ld_ip, ld_bc, ld_moe = (sem(n) for n in ("ld_ffn", "ld_b2", "ld_ip", "ld_bc", "ld_moe"))
        ld_w1, ld_w2 = sem("ld_w1"), sem("ld_w2")
        stored = sem("stored")
        pool_own = sem("pool_own")
        ident_ready, moe_const = sem("ident_ready"), sem("moe_const")
        prep_filled, prep_taken, k_masked, v_masked, vo_ready, c8_ready, c8_filled = (
            sem(n) for n in ("prep_filled", "prep_taken", "k_masked", "v_masked", "vo_ready", "c8_ready", "c8_filled"))
        gates_ready, bo_ready = sem("gates_ready"), sem("bo_ready")
        mbias_ready = sem("mbias_ready")
        dve_own = sem("dve_own")
        stats_ready, rstd_ready, norm_ready = (
            [sem(f"{n}{s}") for s in range(6)] for n in ("stats_ready", "rstd_ready", "norm_ready"))
        xT_filled, xT_ready = ([sem(f"{n}{s}") for s in range(4)] for n in ("xT_filled", "xT_ready"))
        vo_filled = sem("vo_filled")
        score_filled, negmax_ready, prob_a, prob_c, shifted, exped = (
            sem(n) for n in ("score_filled", "negmax_ready", "prob_a", "prob_c", "shifted", "exped"))
        probT_filled, probT_ready, pv_filled, x1_ready, x3_ready = (
            sem(n) for n in ("probT_filled", "probT_ready", "pv_filled", "x1_ready", "x3_ready"))
        h_filled, h_ready, ffn_filled, xb2_ready = (
            sem(n) for n in ("h_filled", "h_ready", "ffn_filled", "xb2_ready"))
        qc_filled, qc_ready = sem("qc_filled"), sem("qc_ready")
        qd_filled, qd_ready, kd_filled, kd_ready, vd_filled, vd_ready = (
            sem(n) for n in ("qd_filled", "qd_ready", "kd_filled", "kd_ready", "vd_filled", "vd_ready"))
        sd_filled, sd_shifted, sd_exped, pdT_ready, od_filled, od_ready, op_filled, xr_ready = (
            sem(n) for n in ("sd_filled", "sd_shifted", "sd_exped", "pdT_ready", "od_filled", "od_ready",
                             "op_filled", "xr_ready"))
        hatT_filled, y1T_ready, y1_ready, lg_filled, lsh_ready, lexp_ready, chosen_ready, count_filled = (
            sem(n) for n in ("hatT_filled", "y1T_ready", "y1_ready", "lg_filled", "lsh_ready", "lexp_ready",
                             "chosen_ready", "count_filled"))
        b1_ready = sem("b1_ready")
        last_res_ready = sem("last_res_ready")
        odd_hat_ready = sem("odd_hat_ready")
        kept_ready, keptT_filled, keptT_ready, gate_ready, kept0_ready = (
            sem(n) for n in ("kept_ready", "keptT_filled", "keptT_ready", "gate_ready", "kept0_ready"))
        expert_filled, opened, selected, bias_filled, gb_ready, y1b_ready, xf_ready, res_ready = (
            sem(n) for n in ("expert_filled", "opened", "selected", "bias_filled", "gb_ready", "y1b_ready", "xf_ready",
                             "res_ready"))

        def tiles(g):
            return range(g * TG, (g + 1) * TG)

        def grp(g):
            return slice(g * TG, (g + 1) * TG)

        def key_cols(batch):
            c = (batch // 8 * TG + batch % 4) * P + batch % 8 // 4 * KEYS
            return slice(c, c + KEYS)

        def slot(t):
            return t // TG * TG + t % 2 * 2 + t % TG // 2

        block = ctx.enter_context(nc.Block())

        @block.sync
        def _(sp):
            xv = x.rearrange("(t b) s d -> (b s) t d", b=2)
            ov = out.rearrange("(t b) s d -> (b s) t d", b=2)
            cv = ctxt.rearrange("(g h j) s d -> g h s j d", h=2, j=TG)
            for g in range(G):
                sp.dma_start(x0[:, grp(g), :], xv[:, grp(g), :]).then_inc(ld_x[g], 16)
                for h in range(2):
                    sp.dma_start(ctxv[h * KEYS:(h + 1) * KEYS, grp(g), :], cv[g, h, :, :, :]).then_inc(ld_ctx[g], 16)
                if g == 0:
                    sp.dma_start(mrow[:, :], mask.rearrange("b o s -> o (b s)")).then_inc(ld_mask, 16)
            for i, w in enumerate((Wk, Wv, Wq, Wo)):
                sp.dma_start(w_rows[:, i, :], w).then_inc(ld_w, 16)
            for i, v in ((BQ, bq), (BK, bk), (BV, bv), (L1G, ln1g), (L1B, ln1b)):
                sp.dma_start(rows[i:i + 1, :], row(v)).then_inc(ld_rows, 16)
            sp.dma_start(rows[IPB:IPB + 3, :], ipb.rearrange("(i n) -> i n", n=D)).then_inc(ld_rows, 16)
            sp.dma_start(rows[FB1:FB1 + FC, :], b1.rearrange("(i n) -> i n", n=P)).then_inc(ld_rows, 16)
            sp.dma_start(rows[MB1:MB1 + E * FC, :], mb1.rearrange("e (c n) -> (e c) n", n=P)).then_inc(ld_rows, 16)
            sp.dma_start(gates_in[:, 0:2], row(g_xattn).to_broadcast([P, 2])).then_inc(ld_gate, 16)
            sp.dma_start(gates_in[:, 2:4], row(g_ffn).to_broadcast([P, 2])).then_inc(ld_gate, 16)
            sp.dma_start(u1[:, :], U1).then_inc(ld_ffn, 16)
            sp.dma_start(v1[:, :], V1).then_inc(ld_ffn, 16)
            sp.dma_start(u2[:, :, :], U2.rearrange("(c f) r -> f c r", f=P)).then_inc(ld_ffn, 16)
            sp.dma_start(v2[:, :], V2).then_inc(ld_ffn, 16)
            sp.dma_start(b2g[:, :], row(b2).to_broadcast([P, D])).then_inc(ld_b2, 16)
            sp.dma_start(bo16[:, :], row(bo).to_broadcast([P, D])).then_inc(ld_bo, 16)
            sp.dma_start(ip_rows[:, 0:3, :], ipw.rearrange("(i e) d -> e i d", i=3)).then_inc(ld_ip, 16)
            sp.dma_start(ip_rows[:, 3, :], opw).then_inc(ld_ip, 16)
            sp.dma_start(w1s[:, :, :], w1.rearrange("e d f -> d e f")).then_inc(ld_w1, 16)
            sp.dma_start(w2s[:, :, :, :], w2.rearrange("e (c f) d -> f e c d", f=P)).then_inc(ld_w2, 16)
            for dst, v in ((vbb, ipb[2 * D:3 * D]), (obb, opb), (l1gb, ln1g), (l1bb, ln1b), (l2gb, ln2g), (l2bb, ln2b)):
                sp.dma_start(dst[:, :], row(v).to_broadcast([P, D])).then_inc(ld_bc, 16)
            sp.dma_start(wgs[:, :], wg).then_inc(ld_moe, 16)
            sp.dma_start(mb2s[:, :], mb2).then_inc(ld_moe, 16)
            for g in range(G):
                if g < G - 1:
                    sp.wait_ge(res_ready, g + 1)
                else:
                    sp.wait_ge(last_res_ready, 1)
                sp.dma_start(ov[:, grp(g), :], res[:, grp(g), :]).then_inc(stored, 16)
            sp.wait_ge(stored, 16 * G)

        (S_XA, S_SCORE_A, S_PT_A, S_PV_A, S_XB, S_HIDDEN, S_OUT_B, S_XC, S_Q, S_SCORE_C, S_PT_C, S_PV_C, S_XD,
         S_QK) = range(14)
        STEPS = G + S_QK

        def has(g):
            return 0 <= g < G

        @block.gpsimd
        def _(pool):
            own = [0]

            def after(ins):
                own[0] += 1
                ins.then_inc(pool_own, 1)
                pool.wait_ge(pool_own, own[0])

            nc.gpsimd.memset(minus_half[:, :], -0.5)
            after(nc.gpsimd.memset(ident[:, :], 0.0))
            nc.gpsimd.affine_select(out=ident[:, :], in_=ident[:, :], compare_op=ALU.not_equal, fill=1.0,
                                    base=0, pattern=[[-1, P]], channel_multiplier=1).then_inc(ident_ready, 1)
            nc.gpsimd.memset(ones[:, :], 1.0).then_inc(ident_ready, 1)

            def rsqrt(s, g):
                pool.wait_ge(stats_ready[s], g + 1)
                nc.gpsimd.tensor_tensor(rstd[:, grp(g)], veps[:, grp(g)], minus_half[:, :],
                                        ALU.pow).then_inc(rstd_ready[s], 1)

            def rsqrt_shift(s, g):
                pool.wait_ge(stats_ready[s], g + 1)
                after(nc.gpsimd.tensor_tensor(rstd[:, grp(g)], veps[:, grp(g)], minus_half[:, :], ALU.pow))
                after(nc.gpsimd.tensor_tensor(mrstd[:, grp(g)], mv[:, grp(g), 0], rstd[:, grp(g)], ALU.mult))
                nc.gpsimd.tensor_scalar(nmr[:, grp(g)], mrstd[:, grp(g)], -1.0, None, ALU.mult).then_inc(rstd_ready[s], 1)

            def mask_heads(buf, jobs, g):
                pool.wait_ge(prep_taken, jobs[g] + 1)
                v = buf[:, g * GT:(g + 1) * GT].rearrange("p (r h) -> p r h", h=H0)
                nc.gpsimd.tensor_tensor(v, v, spread(head_mask[:, :], GT // H0), ALU.mult).then_inc(
                    v_masked if jobs is J_VT else k_masked, 1)

            def add_b2(g):
                pool.wait_ge(x1_ready, g + 1)
                nc.gpsimd.tensor_tensor(xb2[:, grp(g), :], x1[:, grp(g), :], spread(b2g[:, :], TG),
                                        ALU.add).then_inc(xb2_ready, 1)

            def final_base(g):
                pool.wait_ge(x3_ready, g + 1)
                nc.gpsimd.tensor_tensor(xf[:, grp(g), :], x3[:, grp(g), :], spread(l2bb[:, :], TG),
                                        ALU.add).then_inc(xf_ready, 1)

            def self_base(g):
                pool.wait_ge(norm_ready[SA], g + 1)
                nc.gpsimd.tensor_tensor(xr[:, grp(g), :], xn[:, grp(g), :], spread(obb[:, :], TG),
                                        ALU.add).then_inc(xr_ready, 1)

            for g in range(G):
                rsqrt(A, g)
            after(nc.gpsimd.memset(head_mask[:, :], 1.0))
            after(nc.gpsimd.affine_select(out=head_mask[:, :], in_=head_mask[:, :], compare_op=ALU.is_ge, fill=0.0,
                                          base=0, pattern=[[-HD0, H0]], channel_multiplier=1))
            after(nc.gpsimd.affine_select(out=head_mask[:, :], in_=head_mask[:, :], compare_op=ALU.is_ge, fill=0.0,
                                          base=HD0 - 1, pattern=[[HD0, H0]], channel_multiplier=-1))
            pool.wait_ge(ld_bo, 16)
            nc.gpsimd.tensor_scalar(bo16[:, :], bo16[:, :], 1.0 / H0, None, ALU.mult).then_inc(bo_ready, 1)
            for s in range(STEPS):
                if has(s - S_PV_C):
                    rsqrt(SA, s - S_PV_C)
                if has(s - S_OUT_B):
                    rsqrt(C, s - S_OUT_B)
                if has(s - S_PV_A):
                    rsqrt(B, s - S_PV_A)
                if has(s - S_PV_A):
                    mask_heads(vmT, J_VT, s - S_PV_A)
                if s == S_PV_A:
                    pool.wait_ge(gates_ready, 1)
                    pool.wait_ge(ld_b2, 16)
                    after(nc.gpsimd.tensor_scalar(b2g[:, :], b2g[:, :], gates[:, 2:3], None, ALU.mult))
                if has(s - S_XB):
                    add_b2(s - S_XB)
                if has(s - S_HIDDEN):
                    mask_heads(kmT, J_KT, s - S_HIDDEN)
                if s == S_XC + 3:
                    pool.wait_ge(ffn_filled, G)
                    nc.gpsimd.tensor_copy(w1T[:, :, :, P], col[:, MB1:MB1 + E * FC].rearrange(
                        "p (e c) -> p e c", c=FC)).then_inc(b1_ready, 1)
                if s == S_XC + 2:
                    pool.wait_ge(ld_bc, 16 * 6)
                    nc.gpsimd.tensor_scalar(l2gb[:, :], l2gb[:, :], gates[:, 3:4], None, ALU.mult).then_inc(moe_const, 1)
                    after(nc.gpsimd.tensor_scalar(l2bb[:, :], l2bb[:, :], gates[:, 3:4], None, ALU.mult))
                if has(s - S_PV_C):
                    final_base(s - S_PV_C)
                if has(s - S_XD):
                    self_base(s - S_XD)
            nc.gpsimd.tensor_copy(identb[:, :], ident[:, :]).then_inc(moe_const, 1)
            nc.gpsimd.affine_select(out=tri[:, :], in_=ones[:, :], compare_op=ALU.is_ge, fill=0.0, base=0,
                                    pattern=[[1, P]], channel_multiplier=-1).then_inc(moe_const, 1)
            nc.gpsimd.iota(rank8[:, :], pattern=[[-1, E]], base=E, channel_multiplier=0,
                           allow_small_or_imprecise_dtypes=True).then_inc(moe_const, 1)
            for g in range(G):
                (rsqrt if g % 2 else rsqrt_shift)(LN1, g)
            for g in range(G):
                pool.wait_ge(odd_hat_ready if g % 2 else norm_ready[LN1], g // 2 + 1)
                after(nc.gpsimd.tensor_tensor(y1[:, grp(g), :], hat[:, grp(g), :], spread(l1gb[:, :], TG), ALU.mult))
                nc.gpsimd.tensor_tensor(y1[:, grp(g), :], y1[:, grp(g), :], spread(l1bb[:, :], TG),
                                        ALU.add).then_inc(y1_ready, 1)
            pool.wait_ge(moe_const, 4)
            for g in range(G):
                pool.wait_ge(gb_ready, g + 1)
                pool.wait_ge(y1_ready, g + 1)
                nc.gpsimd.tensor_tensor(y1[:, grp(g), :], y1[:, grp(g), :], gb[:, grp(g), :], ALU.add).then_inc(y1b_ready, 1)
            rsqrt_shift(LN2, 0)
            for g in range(G - 1):
                if g + 1 < G - 1:
                    rsqrt_shift(LN2, g + 1)
                pool.wait_ge(norm_ready[LN2], g + 1)
                after(nc.gpsimd.tensor_tensor(hat[:, grp(g), :], hat[:, grp(g), :], spread(l2gb[:, :], TG), ALU.mult))
                nc.gpsimd.tensor_tensor(res[:, grp(g), :], hat[:, grp(g), :], xf[:, grp(g), :],
                                        ALU.add).then_inc(res_ready, 1)
            rsqrt(LN2, G - 1)

        @block.scalar
        def _(act):
            def take(j, dst, src, **kw):
                act.wait_ge(prep_filled, j + 1)
                fn = ACT.Identity if kw else ACT.Copy
                nc.scalar.activation(dst, src, fn, **kw).then_inc(prep_taken, 1)

            def job(j):
                return ps[:, job_bank(j), :]

            def take_w1(i):
                take(J_W1 + i, w1T[:, W1_ORDER[i], :, 0:P], job(J_W1 + i).rearrange("p (c n) -> p c n", c=FC))

            def take_wc(i):
                e = W1_ORDER[2 * i]
                take(J_WC + i, wcT[:, e:e + 2, :], job(J_WC + i)[:, 0:2 * (P + 1)].rearrange("p (e n) -> p e n", e=2))

            def take_back(i):
                e = W1_ORDER[4 * i]
                take(J_BACK + i, wc[:, e:e + 4, :], job(J_BACK + i).rearrange("p (e n) -> p e n", e=4))

            def take_kt(g):
                take(J_KT[g], kmT[:, g * GT:(g + 1) * GT], job(J_KT[g]), bias=col[:, BK:BK + 1], scale=1.0)

            def take_vt(g):
                take(J_VT[g], vmT[:, g * GT:(g + 1) * GT], job(J_VT[g]), bias=col[:, BV:BV + 1], scale=1.0)

            def normalise(s, g, src, dst):
                act.wait_ge(rstd_ready[s], g + 1)
                for t in tiles(g):
                    ins = nc.scalar.activation(dst[:, t, :], src[:, t, :], ACT.Identity,
                                               bias=nmr[:, t:t + 1], scale=rstd[:, t:t + 1])
                ins.then_inc(norm_ready[s], 1)

            def take_xT(s, g):
                act.wait_ge(xT_filled[s], g + 1)
                nc.scalar.activation(xT[:, g * GT:(g + 1) * GT], ps[:, g, :], ACT.Copy).then_inc(xT_ready[s], 1)

            def take_xT_by_n(g):
                act.wait_ge(xT_filled[SA], g + 1)
                nc.scalar.activation(xnl[:, :, 8 * g:8 * g + 8].rearrange("p n l -> p l n"),
                                     ps[:, g, :].rearrange("p (l n) -> p l n", n=N), ACT.Copy).then_inc(xT_ready[SA], 1)

            def take_probT(k, g):
                act.wait_ge(probT_filled, k * G + g + 1)
                nc.scalar.activation(probT[:, g, :, :], ps[:, g, 0:2 * P].rearrange("p (i q) -> p i q", i=2),
                                     ACT.Copy).then_inc(probT_ready, 1)

            def gelu(g, c):
                act.wait_ge(h_filled, g * FC + c + 1)
                nc.scalar.activation(hT[:, c, g * GT:(g + 1) * GT], ps[:, 4 + c % 2, :], ACT.Gelu_apprx_tanh,
                                     bias=col[:, FB1 + c:FB1 + c + 1], scale=1.0).then_inc(h_ready, 1)

            def exp_a(g):
                act.wait_ge(negmax_ready, g + 1)
                for i in range(TG):
                    q = g * TG + i
                    ins = nc.scalar.activation(prob[:, q, :], ps[:, g, i * KEYS:(i + 1) * KEYS], ACT.Exp,
                                               bias=negmax[:, q:q + 1], scale=SCALE_A, accum_out=ssum[:, q, 0:1])
                ins.then_inc(prob_a, 1)

            def exp_c(g):
                act.wait_ge(shifted, g + 1)
                v = prob[:, grp(g), :]
                nc.scalar.activation(v, v, ACT.Exp, scale=SCALE_C).then_inc(exped, 1)

            def take_proj(filled, done, g, bank, dst, which):
                act.wait_ge(filled, g + 1)
                nc.scalar.activation(dst[:, :, 8 * g:8 * g + 8], ps[:, bank, :].rearrange("p (n l) -> p n l", n=N),
                                     ACT.Identity, bias=col[:, IPB + which:IPB + which + 1], scale=1.0).then_inc(done, 1)

            def take_heads(g):
                act.wait_ge(od_filled, g + 1)
                for k in range(4):
                    ins = nc.scalar.activation(
                        oT[:, :, 16 * g:16 * g + 16].rearrange("p l (q k) -> p k q l", k=4)[:, k],
                        ps[:, 4 + k, 0:P].rearrange("p (q l) -> p q l", q=TG), ACT.Copy)
                ins.then_inc(od_ready, 1)

            def take_hatT(g):
                act.wait_ge(hatT_filled, g + 1)
                nc.scalar.activation(y1T[:, g * GT:(g + 1) * GT], ps[:, g, :], ACT.Identity,
                                     bias=col[:, L1B:L1B + 1], scale=col[:, L1G:L1G + 1]).then_inc(y1T_ready, 1)

            for s in range(STEPS):
                if s == S_XC + G - 1:
                    take_w1(0)
                    take_w1(1)
                if s == S_XD:
                    take_w1(6)
                    take_w1(7)
                if has(s - S_SCORE_C):
                    exp_c(s - S_SCORE_C)
                if has(s - S_QK):
                    take_proj(qd_filled, qd_ready, s - S_QK, s - S_QK, qdT, 0)
                    take_proj(kd_filled, kd_ready, s - S_QK, 7, kdT, 1)
                if has(s - S_PT_C):
                    take_probT(1, s - S_PT_C)
                if has(s - S_Q):
                    g = s - S_Q
                    act.wait_ge(qc_filled, g + 1)
                    nc.scalar.activation(qcT[:, g * GT:(g + 1) * GT], ps[:, g, :], ACT.Identity,
                                         bias=col[:, BQ:BQ + 1], scale=1.0).then_inc(qc_ready, 1)
                if s == S_XC + G - 1:
                    take_w1(2)
                    take_w1(3)
                if has(s - S_XC):
                    take_xT(C, s - S_XC)
                if has(s - S_HIDDEN):
                    for c in range(FC):
                        gelu(s - S_HIDDEN, c)
                if has(s - S_PT_A):
                    take_probT(0, s - S_PT_A)
                if has(s - S_XB):
                    take_xT(B, s - S_XB)
                if has(s):
                    take(J_CTX[s], ctxT[:, s * GT:(s + 1) * GT], job(J_CTX[s]))
                    take_xT(A, s)
                if s < 3 and has(s - S_SCORE_A):
                    exp_a(s - S_SCORE_A)
                if s == 1:
                    take(J_W, wT[:, :, :], job(J_W).rearrange("p (i n) -> p i n", i=4))
                if s == 2:
                    take(J_COL, col[:, :], job(J_COL)[:, 0:NROWS])
                    act.wait_ge(ld_gate, 32)
                    nc.scalar.activation(gates[:, :], gates_in[:, :], ACT.Tanh).then_inc(gates_ready, 1)
                    act.wait_ge(prep_taken, J_COL + 1)
                    take_kt(0)
                    take_vt(0)
                if s == 3:
                    take(J_U2, u2T, job(J_U2)[0:R, :])
                    take(J_U1, u1T, job(J_U1)[0:R, 0:P])
                    take_kt(1)
                    take_vt(1)
                if s == 4:
                    take(J_F1, f1, job(J_F1))
                    take(J_F2, f2, job(J_F2).rearrange("p (c n) -> p c n", c=FC))
                    for g in (2, 3):
                        take_kt(g)
                        take_vt(g)
                if s >= 3 and has(s - S_SCORE_A):
                    exp_a(s - S_SCORE_A)
                if s == S_HIDDEN + G:
                    take(J_IP, ipT[:, :, :], job(J_IP).rearrange("p (i n) -> p i n", i=4))
                if s == S_XD - 1:
                    take_w1(4)
                    take_w1(5)
                if has(s - S_XD):
                    take_xT_by_n(s - S_XD)
                if 0 <= s - S_XD < 3:
                    take_wc(s - S_XD)
            for g in range(G):
                act.wait_ge(sd_shifted, g + 1)
                v = pd[:, g % 2, :, :]
                nc.scalar.activation(v, v, ACT.Exp, scale=SCALE_D).then_inc(sd_exped, 1)
                if g > 0:
                    take_heads(g - 1)
            take_heads(G - 1)
            normalise(LN1, 0, xr, hat)
            take_wc(3)
            take_back(0)
            take_hatT(0)
            take_back(1)
            normalise(LN1, 2, xr, hat)
            for g in range(1, G):
                take_hatT(g)
            act.wait_ge(lsh_ready, 1)
            nc.scalar.activation(lexp[:, :, :], lsh[:, :, :], ACT.Exp).then_inc(lexp_ready, 1)

            def open_sum(g):
                act.wait_ge(expert_filled, g * E + 1)
                act.wait_ge(kept0_ready, 1)
                for t in tiles(g):
                    ins = nc.scalar.activation(acc[:, t, :], ps[:, RING[g * E % len(RING)],
                                                                t % TG * P:(t % TG + 1) * P], ACT.Copy,
                                               scale=kept0[:, t:t + 1])
                ins.then_inc(opened, 1)

            for g in range(G):
                if g < 2:
                    open_sum(g)
                act.wait_ge(keptT_filled, g + 1)
                nc.scalar.activation(keptT[:, g * GT:(g + 1) * GT], ps[0:E, 5, :], ACT.Copy).then_inc(keptT_ready, 1)
                if g == G - 1:
                    open_sum(2)
                act.wait_ge(bias_filled, g + 1)
                act.wait_ge(gate_ready, 1)
                for t in tiles(g):
                    ins = nc.scalar.activation(gb[:, t, :], ps[:, 4, t % TG * P:(t % TG + 1) * P], ACT.Copy,
                                               scale=gate[:, t:t + 1])
                ins.then_inc(gb_ready, 1)
            normalise(LN2, 0, xr, hat)
            normalise(LN2, 1, xr, hat)
            open_sum(3)
            normalise(LN2, 2, xr, hat)

        @block.tensor
        def _(pe):
            def mm(o, lhsT, rhs, start=True, stop=True):
                return nc.tensor.matmul(o, lhsT, rhs, start=start, stop=stop)

            def job(j):
                if job_before(j):
                    pe.wait_ge(prep_taken, job_before(j))
                return ps[:, job_bank(j), :]

            def transpose4(dst, src):
                for i in range(4):
                    ins = nc.tensor.transpose(dst[:, i * P:(i + 1) * P], src(i), ident[:, :])
                return ins

            def x_transposes(s, g):
                pe.wait_ge(norm_ready[s], g + 1)
                transpose4(ps[:, g, :], lambda i: xn[:, g * TG + i, :]).then_inc(xT_filled[s], 1)

            def prob_transposes(k, g):
                pe.wait_ge(prob_a if k == 0 else prob_c, g + 1)
                for i in range(2):
                    q = g * TG + 2 * i
                    ins = nc.tensor.transpose(ps[:, g, i * P:(i + 1) * P],
                                              prob[:, q:q + 2, :].rearrange("p t k -> p (t k)"), ident[:, :])
                ins.then_inc(probT_filled, 1)

            def prob_values(k, g, values):
                pe.wait_ge(probT_ready, k * G + g + 1)
                for t in tiles(g):
                    i, half = t % 2, t % TG // 2
                    for b in range(2):
                        j = g * TG + (2 * (t % TG) + b) % TG
                        ins = mm(ps[64 * b:64 * b + 64, 6 if half else g, i * P:(i + 1) * P],
                                 probT[64 * half:64 * half + 64, g, i, 64 * b:64 * b + 64],
                                 values[64 * half:64 * half + 64, j, :])
                ins.then_inc(pv_filled, 1)

            def w1_job(i):
                transpose4(job(J_W1 + i), lambda c: w1s[:, W1_ORDER[i], c * P:(c + 1) * P]).then_inc(prep_filled, 1)

            def wc_job(j):
                o = job(J_WC + j)
                pe.wait_ge(ld_w2, 16)
                pe.wait_ge(prep_taken, J_W1 + 2 * (j + 1))
                pe.wait_ge(b1_ready, 1)
                for i in range(2):
                    e = W1_ORDER[2 * j + i]
                    for c in range(FC):
                        ins = mm(o[:, i * (P + 1):(i + 1) * (P + 1)], w2s[:, e, c, :], w1T[:, e, c, :],
                                 start=(c == 0), stop=(c == FC - 1))
                ins.then_inc(prep_filled, 1)

            def back_job(j):
                o = job(J_BACK + j)
                pe.wait_ge(prep_taken, J_WC + 2 * (j + 1))
                transpose4(o, lambda i: wcT[:, W1_ORDER[4 * j + i], 0:P]).then_inc(prep_filled, 1)

            def kt_job(g):
                mm(job(J_KT[g]), wT[:, 0, :], ctxT[:, g * GT:(g + 1) * GT]).then_inc(prep_filled, 1)

            def vt_job(g):
                mm(job(J_VT[g]), wT[:, 1, :], ctxT[:, g * GT:(g + 1) * GT]).then_inc(prep_filled, 1)

            def scores_a(g):
                pe.wait_ge(mbias_ready, g + 1)
                pe.wait_ge(xT_ready[A], g + 1)
                for b in range(2):
                    mm(ps[64 * b:64 * b + 64, g, 0:TG * KEYS], ones[0:1, 0:64],
                       mbias[0:1, (2 * g + b) * TG * KEYS:(2 * g + b + 1) * TG * KEYS], stop=False)
                for t in tiles(g):
                    for b in range(2):
                        c = slot(t) % TG * KEYS
                        ins = mm(ps[64 * b:64 * b + 64, g, c:c + KEYS], xT[:, t * P + 64 * b:t * P + 64 * b + 64],
                                 ctxT[:, key_cols(2 * t + b)], start=False, stop=(t % TG == TG - 1))
                ins.then_inc(score_filled, 1)

            def scores_c(g):
                pe.wait_ge(qc_ready, g + 1)
                pe.wait_ge(k_masked, g + 1)
                for t in tiles(g):
                    for b in range(2):
                        c = slot(t) % TG * KEYS
                        ins = mm(ps[64 * b:64 * b + 64, g, c:c + KEYS],
                                 qcT[:, t * P + 64 * b:t * P + 64 * b + 64], kmT[:, key_cols(2 * t + b)])
                ins.then_inc(score_filled, 1)

            def values_out(g):
                pe.wait_ge(v_masked, g + 1)
                if g == 0:
                    pe.wait_ge(prep_taken, J_IP)
                else:
                    pe.wait_ge(vo_ready, g)
                for i in range(TG):
                    c = (g * TG + i) * P
                    ins = mm(ps[:, 7, i * P:(i + 1) * P], vmT[:, c:c + P], wT[:, 3, :])
                ins.then_inc(vo_filled, 1)

            def hidden(g, c):
                if g == 0 and c < 2:
                    pe.wait_ge(prep_taken, max(j + 1 for j in range(J_IP) if job_bank(j) == 4 + c))
                else:
                    pe.wait_ge(h_ready, g * FC + c - 1)
                mm(ps[:, 4 + c % 2, :], f1[:, c * P:(c + 1) * P], xT[:, g * GT:(g + 1) * GT]).then_inc(h_filled, 1)

            def ffn_out(g):
                pe.wait_ge(h_ready, (g + 1) * FC)
                for i in range(TG):
                    t = g * TG + i
                    for c in range(FC):
                        ins = mm(ps[:, g, i * P:(i + 1) * P], hT[:, c, t * P:(t + 1) * P], f2[:, c, :],
                                 start=(c == 0), stop=(c == FC - 1))
                ins.then_inc(ffn_filled, 1)

            pe.wait_ge(ident_ready, 2)
            for s in range(STEPS):
                if has(s - S_SCORE_C):
                    scores_c(s - S_SCORE_C)
                if has(s - S_PV_C):
                    g = s - S_PV_C
                    if g == 0:
                        pe.wait_ge(vo_ready, G)
                        pe.wait_ge(x1_ready, G)
                    else:
                        pe.wait_ge(x3_ready, g)
                    prob_values(1, g, vo)
                if has(s - S_QK):
                    g = s - S_QK
                    pe.wait_ge(xT_ready[SA], g + 1)
                    mm(ps[:, g, :], ipT[:, 0, :], xnl[:, :, 8 * g:8 * g + 8]).then_inc(qd_filled, 1)
                    if g == 0:
                        pe.wait_ge(vo_ready, G)
                    else:
                        pe.wait_ge(kd_ready, g)
                    mm(ps[:, 7, :], ipT[:, 1, :], xnl[:, :, 8 * g:8 * g + 8]).then_inc(kd_filled, 1)
                if has(s - S_PT_C):
                    prob_transposes(1, s - S_PT_C)
                if has(s - S_Q):
                    g = s - S_Q
                    pe.wait_ge(xT_ready[C], g + 1)
                    mm(ps[:, g, :], wT[:, 2, :], xT[:, g * GT:(g + 1) * GT]).then_inc(qc_filled, 1)
                if s == S_XC + G - 1:
                    for i in range(4):
                        w1_job(i)
                if has(s - S_OUT_B):
                    ffn_out(s - S_OUT_B)
                if has(s - S_XC):
                    x_transposes(C, s - S_XC)
                if has(s - S_HIDDEN):
                    g = s - S_HIDDEN
                    pe.wait_ge(xT_ready[B], g + 1)
                    hidden(g, 0)
                    hidden(g, 1)
                    values_out(g)
                    hidden(g, 2)
                    hidden(g, 3)
                if has(s - S_PV_A):
                    g = s - S_PV_A
                    if g > 0:
                        pe.wait_ge(x1_ready, g)
                    prob_values(0, g, ctxv)
                if has(s - S_PT_A):
                    prob_transposes(0, s - S_PT_A)
                if has(s - S_SCORE_A):
                    scores_a(s - S_SCORE_A)
                if has(s - S_XB):
                    x_transposes(B, s - S_XB)
                if has(s):
                    pe.wait_ge(ld_ctx[s], 32)
                    transpose4(job(J_CTX[s]), lambda i: ctxv[:, s * TG + i, :]).then_inc(prep_filled, 1)
                    x_transposes(A, s)
                if s == 1:
                    pe.wait_ge(ld_w, 16 * 4)
                    transpose4(job(J_W), lambda i: w_rows[:, i, :]).then_inc(prep_filled, 1)
                if s == 2:
                    pe.wait_ge(ld_rows, 16 * 8)
                    nc.tensor.transpose(job(J_COL)[:, 0:NROWS], rows[:, :], ident[0:NROWS, 0:NROWS]).then_inc(prep_filled, 1)
                    pe.wait_ge(prep_taken, J_W + 1)
                    kt_job(0)
                    vt_job(0)
                if s == 3:
                    pe.wait_ge(ld_ffn, 16 * 4)
                    o = job(J_U2)
                    for c in range(FC):
                        ins = nc.tensor.transpose(o[0:R, c * P:(c + 1) * P], u2[:, c, :], ident[:, :])
                    ins.then_inc(prep_filled, 1)
                    nc.tensor.transpose(job(J_U1)[0:R, 0:P], u1[:, :], ident[:, :]).then_inc(prep_filled, 1)
                    kt_job(1)
                    vt_job(1)
                if s == 4:
                    o = job(J_F1)
                    pe.wait_ge(prep_taken, J_U1 + 1)
                    mm(o, u1T, v1[:, :]).then_inc(prep_filled, 1)
                    o = job(J_F2)
                    for c in range(FC):
                        ins = mm(o[:, c * P:(c + 1) * P], u2T[:, c * P:(c + 1) * P], v2[:, :])
                    ins.then_inc(prep_filled, 1)
                    pe.wait_ge(prep_taken, J_CTX3 + 1)
                    for g in (2, 3):
                        kt_job(g)
                        vt_job(g)
                if s == S_HIDDEN + G:
                    pe.wait_ge(h_ready, G * FC)
                    pe.wait_ge(ld_ip, 16 * 2)
                    transpose4(job(J_IP), lambda i: ip_rows[:, i, :]).then_inc(prep_filled, 1)
                    pe.wait_ge(ld_w1, 16)
                if s in (S_XD - 1, S_XD):
                    w1_job(2 * (s - S_XD + 3))
                    w1_job(2 * (s - S_XD + 3) + 1)
                if has(s - S_XD):
                    x_transposes(SA, s - S_XD)
                if 0 <= s - S_XD < 3:
                    wc_job(s - S_XD)
            pe.wait_ge(x3_ready, G)
            pe.wait_ge(prep_taken, J_WC + 3)

            def self_values(g):
                for i in range(TG):
                    q = g * TG + i
                    ins = mm(ps[:, 4 + g, i * P:(i + 1) * P], xnl[:, 4 * q:4 * q + 4, :].rearrange("p n l -> p (n l)"),
                             ipT[:, 2, :])
                ins.then_inc(vd_filled, 1)

            for g in range(G - 1):
                self_values(g)
            pe.wait_ge(kd_ready, G)

            def head_scores(g):
                if g >= 1:
                    pe.wait_ge(sd_shifted, g)
                for i in range(TG):
                    for k in range(4):
                        n = 4 * (g * TG + i) + k
                        for h in range(H1):
                            hs = slice(HD1 * h, HD1 * h + HD1)
                            ins = mm(ps[L * k:L * k + L, h, i * L:(i + 1) * L], qdT[hs, n, :], kdT[hs, n, :])
                ins.then_inc(sd_filled, 1)

            def head_values(g):
                pe.wait_ge(pdT_ready, g + 1)
                if g == 0:
                    pe.wait_ge(vd_ready, G)
                else:
                    pe.wait_ge(od_ready, g)
                for i in range(TG):
                    for h in range(H1):
                        for k in range(4):
                            ks = slice(L * k, L * k + L)
                            ins = mm(ps[HD1 * h:HD1 * h + HD1, 4 + k, i * L:(i + 1) * L],
                                     vd[ks, g * TG + i, HD1 * h:HD1 * h + HD1],
                                     pdT[ks, g % 2, h, i * L:(i + 1) * L])
                ins.then_inc(od_filled, 1)

            head_scores(0)
            self_values(G - 1)
            for g in range(1, G):
                head_scores(g)
                head_values(g - 1)
            pe.wait_ge(sd_shifted, G)
            head_values(G - 1)
            flat = oT[:, :, :].rearrange("p l n -> p (l n)")
            pe.wait_ge(od_ready, G)
            for g in range(G):
                for i in range(TG):
                    t = g * TG + i
                    ins = mm(ps[:, g, i * P:(i + 1) * P], flat[:, t * P:(t + 1) * P], ipT[:, 3, :])
                ins.then_inc(op_filled, 1)
            pe.wait_ge(ld_moe, 16 * 2)
            pe.wait_ge(ld_w2, 16)

            def expert(i):
                g, e = divmod(i, E)
                pe.wait_ge(y1T_ready, G if i == 5 else g + 1)
                before = i - len(RING)
                if before >= 0 and before % E == 0:
                    pe.wait_ge(opened, before // E + 1)
                elif before >= 0:
                    pe.wait_ge(selected, selected_by(*divmod(before, E)))
                for t in range(TG):
                    c = g * GT + t * P
                    ins = mm(ps[:, RING[i % len(RING)], t * P:(t + 1) * P], y1T[:, c:c + P], wc[:, e, :])
                ins.then_inc(expert_filled, 1)

            def logits(g):
                pe.wait_ge(y1T_ready, g + 1)
                for t in tiles(g):
                    ins = mm(ps[:, 4, t * E:(t + 1) * E], y1T[:, t * P:(t + 1) * P], wgs[:, :])
                return ins

            def hat_transposes(g):
                pe.wait_ge(odd_hat_ready if g % 2 else norm_ready[LN1], g // 2 + 1)
                transpose4(ps[:, g, :], lambda i: hat[:, g * TG + i, :]).then_inc(hatT_filled, 1)

            wc_job(3)
            back_job(0)
            hat_transposes(0)
            back_job(1)
            nc.tensor.transpose(ps[0:E, 5, 0:P], wcT[:, :, P], ident[:, :]).then_inc(c8_filled, 1)
            hat_transposes(1)
            logits(0)
            pe.wait_ge(prep_taken, J_BACK + 2)
            expert(0)
            hat_transposes(2)
            logits(1)
            expert(1)
            hat_transposes(3)
            logits(2)
            logits(3).then_inc(lg_filled, 1)
            expert(2)
            expert(3)
            expert(4)
            pe.wait_ge(moe_const, 4)
            pe.wait_ge(chosen_ready, 1)
            mm(ps[:, 4, T * E:2 * T * E], tri[:, :], chosen[:, :, :].rearrange("p t e -> p (t e)"), stop=False)
            for t in range(T - 1):
                ins = mm(ps[:, 4, (T + t + 1) * E:2 * T * E], ones[:, :], spread(chosen[:, t, :], T - 1 - t),
                         start=False, stop=(t == T - 2))
            ins.then_inc(count_filled, 1)
            for i in range(5, G * E):
                expert(i)
                g, part = divmod(i - 5, 3)
                if has(g) and part == 0:
                    pe.wait_ge(kept_ready, 1)
                    if g == 0:
                        pe.wait_ge(c8_ready, 1)
                    else:
                        pe.wait_ge(keptT_ready, g)
                    for t in range(TG):
                        ins = mm(ps[0:E, 5, t * P:(t + 1) * P], kept[:, g * TG + t, :], identb[:, :])
                    ins.then_inc(keptT_filled, 1)
                if has(g) and part == 2:
                    pe.wait_ge(keptT_ready, g + 1)
                    if g > 0:
                        pe.wait_ge(gb_ready, g)
                    for t in range(TG):
                        c = g * GT + t * P
                        ins = mm(ps[:, 4, t * P:(t + 1) * P], keptT[:, c:c + P], c8[:, :])
                    ins.then_inc(bias_filled, 1)

        @block.vector
        def _(dve):
            own = [0]

            def mark(ins):
                own[0] += 1
                ins.then_inc(dve_own, 1)

            def settle():
                dve.wait_ge(dve_own, own[0])

            def statistics(s, g, src):
                for t in tiles(g):
                    ins = nc.vector.bn_stats(stats[:, t, :], src[:, t, :])
                mark(ins)
                settle()
                for t in tiles(g):
                    ins = nc.vector.bn_aggr(mv[:, t, :], stats[:, t, :])
                mark(ins)
                settle()
                nc.vector.tensor_scalar(veps[:, grp(g)], mv[:, grp(g), 1], EPS, None, ALU.add).then_inc(stats_ready[s], 1)

            def normalise(s, g, src, dst, ready=None):
                dve.wait_ge(rstd_ready[s], g + 1)
                for t in tiles(g):
                    ins = nc.vector.tensor_scalar(dst[:, t, :], src[:, t, :], mv[:, t, 0:1], rstd[:, t:t + 1],
                                                  ALU.subtract, ALU.mult)
                ins.then_inc(ready or norm_ready[s], 1)

            def by_slot(buf, g, half):
                return buf[:, g * TG + 2 * half:g * TG + 2 * half + 2, :]

            def mask_bias(g):
                for b in range(2):
                    m = mrow[:, 2 * g * TG * KEYS:2 * (g + 1) * TG * KEYS].rearrange(
                        "o (i j b k) -> o b j i k", i=2, j=2, b=2)
                    c = (2 * g + b) * TG * KEYS
                    ins = nc.vector.tensor_scalar(
                        mbias[:, c:c + TG * KEYS].rearrange("o (j i k) -> o j i k", j=2, i=2), m[:, b], 0.0, MASKED,
                        ALU.is_equal, ALU.mult)
                ins.then_inc(mbias_ready, 1)

            def row_maxima(g):
                dve.wait_ge(score_filled, g + 1)
                mark(nc.vector.tensor_reduce(mx[:, grp(g), 0], ps[:, g, 0:TG * KEYS].rearrange("p (t k) -> p t k", k=KEYS),
                                             axis=AX_X, op=ALU.max))
                settle()
                nc.vector.tensor_scalar(negmax[:, grp(g)], mx[:, grp(g), 0], -SCALE_A, None,
                                        ALU.mult).then_inc(negmax_ready, 1)

            def row_factors(g):
                if g == 0:
                    dve.wait_ge(gates_ready, 1)
                dve.wait_ge(prob_a, g + 1)
                mark(nc.vector.reciprocal(rsum[:, grp(g), 0], ssum[:, grp(g), 0]))
                settle()
                mark(nc.vector.tensor_scalar(fac[:, grp(g)], rsum[:, grp(g), 0], gates[:, 0:1], KEEP_A, ALU.mult, ALU.mult))

            def residual_a(g):
                dve.wait_ge(pv_filled, g + 1)
                settle()
                for t in tiles(g):
                    i, half = t % 2, t % TG // 2
                    q = slot(t)
                    ins = nc.vector.scalar_tensor_tensor(x1[:, t, :], ps[:, 6 if half else g, i * P:(i + 1) * P],
                                                         fac[:, q:q + 1], x0[:, t, :], ALU.mult, ALU.add)
                ins.then_inc(x1_ready, 1)
                dve.wait_ge(x1_ready, g + 1)
                statistics(B, g, x1)

            def take_vo(g):
                dve.wait_ge(vo_filled, g + 1)
                dve.wait_ge(bo_ready, 1)
                nc.vector.tensor_tensor(vo[:, grp(g), :], ps[:, 7, :].rearrange("p (t n) -> p t n", n=D),
                                        spread(bo16[:, :], TG), ALU.add).then_inc(vo_ready, 1)

            def residual_b(g):
                dve.wait_ge(ffn_filled, g + 1)
                dve.wait_ge(xb2_ready, g + 1)
                mark(nc.vector.scalar_tensor_tensor(x2[:, grp(g), :], ps[:, g, :].rearrange("p (t n) -> p t n", n=D),
                                                    gates[:, 2:3], xb2[:, grp(g), :], ALU.mult, ALU.add))
                settle()
                statistics(C, g, x2)

            def shift_scores(g):
                dve.wait_ge(score_filled, G + g + 1)
                s = ps[:, g, 0:TG * KEYS]
                mark(nc.vector.tensor_reduce(mx[:, grp(g), :], s.rearrange("p (t j h) -> p t h j", h=H0, j=KEYS // H0),
                                             axis=AX_X, op=ALU.max))
                settle()
                nc.vector.tensor_tensor(prob[:, grp(g), :].rearrange("p t (j h) -> p t j h", h=H0),
                                        s.rearrange("p (t j h) -> p t j h", h=H0, j=KEYS // H0),
                                        over_keys(mx[:, grp(g), :]), ALU.subtract).then_inc(shifted, 1)

            def over_keys(v):
                return v.unsqueeze(2).to_broadcast([P, TG, KEYS // H0, H0])

            def weigh_scores(g):
                dve.wait_ge(exped, g + 1)
                mark(nc.vector.tensor_reduce(ssum[:, grp(g), :], prob[:, grp(g), :].rearrange("p t (j h) -> p t h j", h=H0),
                                             axis=AX_X, op=ALU.add))
                settle()
                mark(nc.vector.reciprocal(rsum[:, grp(g), :], ssum[:, grp(g), :]))
                settle()
                v = prob[:, grp(g), :].rearrange("p t (j h) -> p t j h", h=H0)
                nc.vector.tensor_tensor(v, v, over_keys(rsum[:, grp(g), :]), ALU.mult).then_inc(prob_c, 1)

            def residual_c(g):
                dve.wait_ge(pv_filled, G + g + 1)
                for half in range(2):
                    ins = nc.vector.scalar_tensor_tensor(
                        by_slot(x3, g, half), ps[:, 6 if half else g, 0:2 * P].rearrange("p (i n) -> p i n", i=2),
                        gates[:, 1:2], by_slot(x2, g, half), ALU.mult, ALU.add)
                ins.then_inc(x3_ready, 1)
                dve.wait_ge(x3_ready, g + 1)
                statistics(SA, g, x3)

            dve.wait_ge(ld_x[0], 16)
            statistics(A, 0, x0)
            dve.wait_ge(ld_mask, 16)
            mask_bias(0)
            normalise(A, 0, x0, xn)
            for s in range(STEPS):
                if has(s - S_SCORE_C):
                    shift_scores(s - S_SCORE_C)
                if s - S_XC == G - 1:
                    normalise(C, G - 1, x2, xn)
                if has(s - S_PV_C):
                    residual_c(s - S_PV_C)
                if has(s - S_SCORE_C):
                    weigh_scores(s - S_SCORE_C)
                if has(s - S_PV_C):
                    normalise(SA, s - S_PV_C, x3, xn)
                if has(s - S_OUT_B):
                    residual_b(s - S_OUT_B)
                    if s - S_OUT_B < G - 1:
                        normalise(C, s - S_OUT_B, x2, xn)
                if has(s - S_HIDDEN):
                    take_vo(s - S_HIDDEN)
                if has(s - S_PV_A):
                    row_factors(s - S_PV_A)
                    residual_a(s - S_PV_A)
                if has(s + 1):
                    dve.wait_ge(ld_x[s + 1], 16)
                    statistics(A, s + 1, x0)
                    mask_bias(s + 1)
                if has(s - S_SCORE_A):
                    row_maxima(s - S_SCORE_A)
                if has(s - S_PV_A):
                    normalise(B, s - S_PV_A, x1, xn)
                if has(s + 1):
                    normalise(A, s + 1, x0, xn)
            dve.wait_ge(ld_bc, 16 * 6)

            def take_values(g):
                dve.wait_ge(vd_filled, g + 1)
                nc.vector.tensor_tensor(vd[:, grp(g), :], ps[:, 4 + g, :].rearrange("p (i n) -> p i n", n=D),
                                        spread(vbb[:, :], TG), ALU.add).then_inc(vd_ready, 1)

            def shift_heads(g):
                dve.wait_ge(sd_filled, g + 1)
                s = ps[:, 0:H1, 0:P].rearrange("p h (i m) -> p h i m", m=L)
                mark(nc.vector.tensor_reduce(mxd[:, :].rearrange("p (h i) -> p h i", h=H1), s, axis=AX_X, op=ALU.max))
                settle()
                if g >= 2:
                    dve.wait_ge(pdT_ready, g - 1)
                nc.vector.tensor_tensor(pd[:, g % 2, :, :].rearrange("p h (i m) -> p h i m", m=L), s,
                                        along(mxd[:, :].rearrange("p (h i) -> p h i", h=H1), L),
                                        ALU.subtract).then_inc(sd_shifted, 1)

            def weigh_heads(g):
                dve.wait_ge(sd_exped, g + 1)
                v = pd[:, g % 2, :, :].rearrange("p h (i m) -> p (h i) m", m=L)
                mark(nc.vector.tensor_reduce(sumd[:, g, :], v, axis=AX_X, op=ALU.add))
                settle()
                mark(nc.vector.reciprocal(rsd[:, g, :], sumd[:, g, :]))
                settle()
                mark(nc.vector.tensor_tensor(v, v, along(rsd[:, g, :], L), ALU.mult))
                settle()
                if g >= 2:
                    dve.wait_ge(od_filled, g - 1)
                nc.vector.transpose(pdT[:, g % 2, :, :].rearrange("p h n -> p (h n)"),
                                    pd[:, g % 2, :, :].rearrange("p h n -> p (h n)")).then_inc(pdT_ready, 1)

            for g in range(G - 1):
                take_values(g)
            shift_heads(0)
            take_values(G - 1)
            for g in range(1, G):
                weigh_heads(g - 1)
                shift_heads(g)
            weigh_heads(G - 1)
            for g in range(G):
                dve.wait_ge(op_filled, g + 1)
                dve.wait_ge(xr_ready, g + 1)
                mark(nc.vector.tensor_tensor(xr[:, grp(g), :], ps[:, g, :].rearrange("p (t n) -> p t n", n=D),
                                             xr[:, grp(g), :], ALU.add))
                settle()
                statistics(LN1, g, xr)
                if g == 2:
                    normalise(LN1, 1, xr, hat, odd_hat_ready)
            normalise(LN1, 3, xr, hat, odd_hat_ready)
            dve.wait_ge(c8_filled, 1)
            dve.wait_ge(ld_moe, 16 * 2)
            nc.vector.tensor_tensor(c8[:, :], ps[0:E, 5, 0:P], mb2s[:, :], ALU.add).then_inc(c8_ready, 1)
            dve.wait_ge(lg_filled, 1)
            l8 = ps[:, 4, 0:T * E].rearrange("p (t e) -> p t e", e=E)
            mark(nc.vector.tensor_reduce(lmax[:, :], l8, axis=AX_X, op=ALU.max))
            settle()
            nc.vector.tensor_tensor(lsh[:, :, :], l8, along(lmax[:, :], E), ALU.subtract).then_inc(lsh_ready, 1)
            dve.wait_ge(moe_const, 4)
            dve.wait_ge(lsh_ready, 1)
            mark(nc.vector.scalar_tensor_tensor(ranked[:, :, :], lsh[:, :, :], 0.0, spread(rank8[:, :], T),
                                                ALU.is_equal, ALU.mult))
            settle()
            mark(nc.vector.tensor_reduce(best[:, :], ranked[:, :, :], axis=AX_X, op=ALU.max))
            settle()
            nc.vector.tensor_tensor(chosen[:, :, :], ranked[:, :, :], along(best[:, :], E),
                                    ALU.is_equal).then_inc(chosen_ready, 1)
            dve.wait_ge(lexp_ready, 1)
            mark(nc.vector.tensor_reduce(lsum[:, :], lexp[:, :, :], axis=AX_X, op=ALU.add))
            settle()
            nc.vector.reciprocal(gate[:, :], lsum[:, :]).then_inc(gate_ready, 1)
            dve.wait_ge(count_filled, 1)
            dve.wait_ge(chosen_ready, 1)
            nc.vector.scalar_tensor_tensor(kept[:, :, :].rearrange("p t e -> p (t e)"), ps[:, 4, T * E:2 * T * E], float(CAP) + 0.5,
                                           chosen[:, :, :].rearrange("p t e -> p (t e)"), ALU.is_le,
                                           ALU.mult).then_inc(kept_ready, 1)
            dve.wait_ge(kept_ready, 1)
            nc.vector.tensor_copy(kept0[:, :], kept[:, :, 0]).then_inc(kept0_ready, 1)

            def select(i):
                g, e = divmod(i, E)
                dve.wait_ge(expert_filled, i + 1)
                if e == 1:
                    dve.wait_ge(opened, g + 1)
                for half in range(2):
                    if e > 1:
                        dve.wait_ge(selected, selected_by(g, e - 1, half))
                    t = g * TG + 2 * half
                    nc.vector.copy_predicated(acc[:, t:t + 2, :], along(kept[:, t:t + 2, e].bitcast(I16), D),
                                              ps[:, RING[i % len(RING)], half * 2 * P:(half + 1) * 2 * P].rearrange(
                                                  "p (t n) -> p t n", n=D)).then_inc(selected, 1)

            def finish_sum(g):
                dve.wait_ge(selected, selected_by(g, E - 1))
                dve.wait_ge(gate_ready, 1)
                dve.wait_ge(y1b_ready, g + 1)
                for t in tiles(g):
                    ins = nc.vector.scalar_tensor_tensor(xr[:, t, :], acc[:, t, :], gate[:, t:t + 1], y1[:, t, :], ALU.mult, ALU.add)
                mark(ins)
                settle()
                statistics(LN2, g, xr)

            dve.wait_ge(kept_ready, 1)
            for i in range(G * E):
                if i % E > 0:
                    select(i)
                elif i > 0:
                    finish_sum(i // E - 1)
            g = G - 1
            finish_sum(g)
            dve.wait_ge(moe_const, 1)
            for t in tiles(g):
                ins = nc.vector.scalar_tensor_tensor(hat[:, t, :], xr[:, t, :], mv[:, t, 0:1], l2gb[:, :],
                                                     ALU.subtract, ALU.mult)
            mark(ins)
            settle()
            dve.wait_ge(rstd_ready[LN2], g + 1)
            dve.wait_ge(xf_ready, G)
            for t in tiles(g):
                ins = nc.vector.scalar_tensor_tensor(res[:, t, :], hat[:, t, :], rstd[:, t:t + 1], xf[:, t, :],
                                                     ALU.mult, ALU.add)
            ins.then_inc(last_res_ready, 1)


_ORDER = ["x", "ctx_1024", "mask_Bx1xS2_ik1", "g_xattn", "g_ffn",
          "L0_ffn_U1", "L0_ffn_V1", "L0_ffn_b1", "L0_ffn_U2", "L0_ffn_V2", "L0_ffn_b2",
          "L1_xattn_Wq", "L1_xattn_bq", "L1_xattn_Wk", "L1_xattn_bk", "L1_xattn_Wv", "L1_xattn_bv",
          "L1_xattn_Wo", "L1_xattn_bo",
          "L1_ffn_in_proj_w", "L1_ffn_in_proj_b", "L1_ffn_out_proj_w", "L1_ffn_out_proj_b",
          "L1_ffn_ln1_g", "L1_ffn_ln1_b", "L1_ffn_ln2_g", "L1_ffn_ln2_b",
          "L1_ffn_wg", "L1_ffn_w1", "L1_ffn_b1", "L1_ffn_w2", "L1_ffn_b2"]


def kernel(**inputs):
    import numpy as np
    import concourse.bacc as bacc
    from concourse.bass_utils import run_bass_kernel_spmd

    nc = bacc.Bacc("TRN2", target_bir_lowering=False, num_devices=1)
    arrays, args = {}, []
    for name in _ORDER:
        a = np.ascontiguousarray(inputs[name])
        arrays[f"in_{name}"] = a
        args.append(nc.dram_tensor(f"in_{name}", a.shape, mybir.dt.from_np(a.dtype), kind="ExternalInput").ap())
    args.append(nc.dram_tensor("out", (NB, NS, D), F32, kind="ExternalOutput").ap())
    program(nc, *args)
    r = run_bass_kernel_spmd(nc, [arrays], core_ids=[0])
    return r.results[0]["out"]
```
